# Optimizing a Trainium2 kernel written in Bass

```python
import numpy as np
import jax
import jax.numpy as jnp

def _softmax(x, axis=-1):
    return jax.nn.softmax(x, axis=axis)

def _gelu(x):
    return jax.nn.gelu(x, approximate=True)

def _silu(x):
    return jax.nn.silu(x)

def _sigmoid(x):
    return jax.nn.sigmoid(x)

def _layernorm(x, axis=-1, eps=1e-05):
    m = jnp.mean(x, axis=axis, keepdims=True)
    v = jnp.var(x, axis=axis, keepdims=True)
    return (x - m) / jnp.sqrt(v + eps)

def _scatter_add(tgt, idx, src, axis=0):
    return tgt.at[idx].add(src)

def _segment_sum(src, seg, n):
    return jax.ops.segment_sum(src, seg, n)
kernel_name = 'mk_prb_d1_jaxref_r8_7fbf65'

def setup_inputs(seed: int=0):
    np.random.seed(seed)
    _w = jnp.asarray

    def _L0_attn_setup():
        import jax, jax.numpy as jnp
        import numpy as np
        H = 128
        NH = 16
        L = 4
        B = 4
        N = 256
        EPS_LN = 1e-12

        def gelu(x):
            return jax.nn.gelu(x, approximate=False)

        def layernorm(x, g, b):
            m = jnp.mean(x, axis=-1, keepdims=True)
            v = jnp.mean((x - m) ** 2, axis=-1, keepdims=True)
            return (x - m) / jnp.sqrt(v + EPS_LN) * g + b

        def conv1d_grouped(x, w, b, groups):
            y = jax.lax.conv_general_dilated(x, w, window_strides=(1,), padding=[(2, 2)], dimension_numbers=('NCH', 'OIH', 'NCH'), feature_group_count=groups)
            return y + b[None, :, None]

        def rope(x):
            b, n, c = x.shape
            half = c // 2
            inv = 1.0 / 10000.0 ** (jnp.arange(0, c, 2, dtype=jnp.float32) / c)
            freqs = jnp.arange(n, dtype=jnp.float32)[:, None] * inv[None, :]
            freqs = jnp.repeat(freqs, 2, axis=-1)
            cos, sin = (jnp.cos(freqs), jnp.sin(freqs))
            xp = x.reshape(b, n, half, 2)
            xr = jnp.stack([-xp[..., 1], xp[..., 0]], axis=-1).reshape(b, n, c)
            return x * cos + xr * sin

        def linear_attention(x, Wq, bq, Wk, bk, Wv, bv, g, bb):
            b, n, c = x.shape
            hd = c // NH
            q = gelu(x @ Wq + bq) + 0.21
            k = gelu(x @ Wk + bk) + 0.21
            v = x @ Wv + bv
            q_r = rope(q)
            k_r = rope(k)
            to_h = lambda t: t.reshape(b, n, NH, hd).transpose(0, 2, 1, 3)
            q, k, v, q_r, k_r = map(to_h, (q, k, v, q_r, k_r))
            kmean = jnp.mean(k, axis=2, keepdims=True)
            z = 1.0 / (jnp.einsum('bhnd,bhmd->bhnm', q, kmean) + 1e-06)
            kv = jnp.einsum('bhnd,bhne->bhde', k_r, v) / n
            out = jnp.einsum('bhnd,bhde->bhne', q_r, kv) * z
            out = out.transpose(0, 2, 1, 3).reshape(b, n, c)
            return layernorm(out + x, g, bb)
        key = jax.random.key(seed)
        ks = jax.random.split(key, 10)
        s = 0.02
        r = lambda k, sh: jax.random.normal(k, sh, dtype=jnp.float32) * s
        d = {}
        d['x'] = jax.random.normal(ks[0], (B, N, H), dtype=jnp.float32)
        d['conv1_w'] = r(ks[1], (4 * H, 1, 5))
        d['conv1_b'] = jnp.zeros((4 * H,), jnp.float32)
        d['conv2_w'] = r(ks[2], (H, 4, 5))
        d['conv2_b'] = jnp.zeros((H,), jnp.float32)
        d['ln0_g'] = jnp.ones((H,), jnp.float32)
        d['ln0_b'] = jnp.zeros((H,), jnp.float32)
        d['Wq'] = r(ks[3], (L, H, H))
        d['bq'] = jnp.zeros((L, H), jnp.float32)
        d['Wk'] = r(ks[4], (L, H, H))
        d['bk'] = jnp.zeros((L, H), jnp.float32)
        d['Wv'] = r(ks[5], (L, H, H))
        d['bv'] = jnp.zeros((L, H), jnp.float32)
        d['lnA_g'] = jnp.ones((L, H), jnp.float32)
        d['lnA_b'] = jnp.zeros((L, H), jnp.float32)
        d['W1'] = r(ks[6], (H, 4 * H))
        d['b1'] = jnp.zeros((4 * H,), jnp.float32)
        d['W2'] = r(ks[7], (4 * H, H))
        d['b2'] = jnp.zeros((H,), jnp.float32)
        d['ln2_g'] = jnp.ones((H,), jnp.float32)
        d['ln2_b'] = jnp.zeros((H,), jnp.float32)
        return d
    _L0_attn_in = _L0_attn_setup()

    def _L0_ffn_setup():
        import jax, jax.numpy as jnp
        import numpy as np
        from jax import lax
        HIDDEN = 128
        INTER = 64
        E = 64
        K = 6
        G = 8
        TG = 4
        NSH = 2
        ISH = INTER * NSH

        def _moe_forward(hidden_states, gate_w, gate_bias, eg_w, eu_w, ed_w, sg_w, su_w, sd_w):
            B, S, H = hidden_states.shape
            x = hidden_states.reshape(-1, H)
            T = x.shape[0]
            shared = jax.nn.silu(x @ sg_w.T) * (x @ su_w.T) @ sd_w.T
            logits = x @ gate_w.T
            scores = jax.nn.sigmoid(logits) + gate_bias
            group_scores = scores.reshape(T, G, E // G).max(axis=-1)
            _, sel_groups = lax.top_k(group_scores, TG)
            group_mask = jnp.zeros((T, G), scores.dtype).at[jnp.arange(T)[:, None], sel_groups].set(1.0)
            mask = jnp.repeat(group_mask, E // G, axis=1)
            masked_scores = scores * mask
            topk_w, topk_i = lax.top_k(masked_scores, K)
            topk_w = topk_w / (topk_w.sum(axis=-1, keepdims=True) + 1e-08)
            comb = jnp.zeros((T, E), x.dtype).at[jnp.arange(T)[:, None], topk_i].add(topk_w)
            h = jax.nn.silu(jnp.einsum('th,eih->eti', x, eg_w)) * jnp.einsum('th,eih->eti', x, eu_w)
            routed = jnp.einsum('eti,ehi,te->th', h, ed_w, comb)
            return (shared + routed).reshape(B, S, H)
        key = jax.random.key(seed)
        ks = jax.random.split(key, 9)
        s = 0.02
        return {'hidden_states': jax.random.normal(ks[0], (1, 128, HIDDEN), jnp.float32), 'gate_w': jax.random.normal(ks[1], (E, HIDDEN), jnp.float32) * s, 'gate_bias': jnp.zeros((E,), jnp.float32), 'eg_w': jax.random.normal(ks[2], (E, INTER, HIDDEN), jnp.float32) * s, 'eu_w': jax.random.normal(ks[3], (E, INTER, HIDDEN), jnp.float32) * s, 'ed_w': jax.random.normal(ks[4], (E, HIDDEN, INTER), jnp.float32) * s, 'sg_w': jax.random.normal(ks[5], (ISH, HIDDEN), jnp.float32) * s, 'su_w': jax.random.normal(ks[6], (ISH, HIDDEN), jnp.float32) * s, 'sd_w': jax.random.normal(ks[7], (HIDDEN, ISH), jnp.float32) * s}
    _L0_ffn_in = _L0_ffn_setup()
    _d = {'L0_attn_x': _L0_attn_in['x'], 'L0_attn_conv1_w': _L0_attn_in['conv1_w'], 'L0_attn_conv1_b': _L0_attn_in['conv1_b'], 'L0_attn_conv2_w': _L0_attn_in['conv2_w'], 'L0_attn_conv2_b': _L0_attn_in['conv2_b'], 'L0_attn_ln0_g': _L0_attn_in['ln0_g'], 'L0_attn_ln0_b': _L0_attn_in['ln0_b'], 'L0_attn_Wq': _L0_attn_in['Wq'], 'L0_attn_bq': _L0_attn_in['bq'], 'L0_attn_Wk': _L0_attn_in['Wk'], 'L0_attn_bk': _L0_attn_in['bk'], 'L0_attn_Wv': _L0_attn_in['Wv'], 'L0_attn_bv': _L0_attn_in['bv'], 'L0_attn_lnA_g': _L0_attn_in['lnA_g'], 'L0_attn_lnA_b': _L0_attn_in['lnA_b'], 'L0_attn_W1': _L0_attn_in['W1'], 'L0_attn_b1': _L0_attn_in['b1'], 'L0_attn_W2': _L0_attn_in['W2'], 'L0_attn_b2': _L0_attn_in['b2'], 'L0_attn_ln2_g': _L0_attn_in['ln2_g'], 'L0_attn_ln2_b': _L0_attn_in['ln2_b'], 'L0_ffn_gate_w': _L0_ffn_in['gate_w'], 'L0_ffn_gate_bias': _L0_ffn_in['gate_bias'], 'L0_ffn_eg_w': _L0_ffn_in['eg_w'], 'L0_ffn_eu_w': _L0_ffn_in['eu_w'], 'L0_ffn_ed_w': _L0_ffn_in['ed_w'], 'L0_ffn_sg_w': _L0_ffn_in['sg_w'], 'L0_ffn_su_w': _L0_ffn_in['su_w'], 'L0_ffn_sd_w': _L0_ffn_in['sd_w']}
    _x0 = _d['L0_attn_x']
    _d['L0_attn_x'] = jax.random.normal(jax.random.fold_in(jax.random.key(seed), 1), (4, 1024, 128), dtype=_x0.dtype)
    del _x0
    return _d

def reference(L0_attn_x, L0_attn_conv1_w, L0_attn_conv1_b, L0_attn_conv2_w, L0_attn_conv2_b, L0_attn_ln0_g, L0_attn_ln0_b, L0_attn_Wq, L0_attn_bq, L0_attn_Wk, L0_attn_bk, L0_attn_Wv, L0_attn_bv, L0_attn_lnA_g, L0_attn_lnA_b, L0_attn_W1, L0_attn_b1, L0_attn_W2, L0_attn_b2, L0_attn_ln2_g, L0_attn_ln2_b, L0_ffn_gate_w, L0_ffn_gate_bias, L0_ffn_eg_w, L0_ffn_eu_w, L0_ffn_ed_w, L0_ffn_sg_w, L0_ffn_su_w, L0_ffn_sd_w):

    def _L0_attn_ref(x, conv1_w, conv1_b, conv2_w, conv2_b, ln0_g, ln0_b, Wq, bq, Wk, bk, Wv, bv, lnA_g, lnA_b, W1, b1, W2, b2, ln2_g, ln2_b):
        import jax, jax.numpy as jnp
        import numpy as np
        H = 128
        NH = 16
        L = 4
        B = 4
        N = 256
        EPS_LN = 1e-12

        def gelu(x):
            return jax.nn.gelu(x, approximate=False)

        def layernorm(x, g, b):
            m = jnp.mean(x, axis=-1, keepdims=True)
            v = jnp.mean((x - m) ** 2, axis=-1, keepdims=True)
            return (x - m) / jnp.sqrt(v + EPS_LN) * g + b

        def conv1d_grouped(x, w, b, groups):
            y = jax.lax.conv_general_dilated(x, w, window_strides=(1,), padding=[(2, 2)], dimension_numbers=('NCH', 'OIH', 'NCH'), feature_group_count=groups)
            return y + b[None, :, None]

        def rope(x):
            b, n, c = x.shape
            half = c // 2
            inv = 1.0 / 10000.0 ** (jnp.arange(0, c, 2, dtype=jnp.float32) / c)
            freqs = jnp.arange(n, dtype=jnp.float32)[:, None] * inv[None, :]
            freqs = jnp.repeat(freqs, 2, axis=-1)
            cos, sin = (jnp.cos(freqs), jnp.sin(freqs))
            xp = x.reshape(b, n, half, 2)
            xr = jnp.stack([-xp[..., 1], xp[..., 0]], axis=-1).reshape(b, n, c)
            return x * cos + xr * sin

        def linear_attention(x, Wq, bq, Wk, bk, Wv, bv, g, bb):
            b, n, c = x.shape
            hd = c // NH
            q = gelu(x @ Wq + bq) + 0.21
            k = gelu(x @ Wk + bk) + 0.21
            v = x @ Wv + bv
            q_r = rope(q)
            k_r = rope(k)
            to_h = lambda t: t.reshape(b, n, NH, hd).transpose(0, 2, 1, 3)
            q, k, v, q_r, k_r = map(to_h, (q, k, v, q_r, k_r))
            kmean = jnp.mean(k, axis=2, keepdims=True)
            z = 1.0 / (jnp.einsum('bhnd,bhmd->bhnm', q, kmean) + 1e-06)
            kv = jnp.einsum('bhnd,bhne->bhde', k_r, v) / n
            out = jnp.einsum('bhnd,bhde->bhne', q_r, kv) * z
            out = out.transpose(0, 2, 1, 3).reshape(b, n, c)
            return layernorm(out + x, g, bb)
        b, n, c = x.shape
        h = x.transpose(0, 2, 1)
        h = conv1d_grouped(h, conv1_w, conv1_b, c)
        h = gelu(h)
        h = conv1d_grouped(h, conv2_w, conv2_b, c)
        h = h.transpose(0, 2, 1)
        h = layernorm(h + x, ln0_g, ln0_b)
        for i in range(Wq.shape[0]):
            h = linear_attention(h, Wq[i], bq[i], Wk[i], bk[i], Wv[i], bv[i], lnA_g[i], lnA_b[i])
        f = gelu(h @ W1 + b1) @ W2 + b2
        return layernorm(f + h, ln2_g, ln2_b)

    def _L0_ffn_ref(hidden_states, gate_w, gate_bias, eg_w, eu_w, ed_w, sg_w, su_w, sd_w):
        import jax, jax.numpy as jnp
        import numpy as np
        from jax import lax
        HIDDEN = 128
        INTER = 64
        E = 64
        K = 6
        G = 8
        TG = 4
        NSH = 2
        ISH = INTER * NSH

        def _moe_forward(hidden_states, gate_w, gate_bias, eg_w, eu_w, ed_w, sg_w, su_w, sd_w):
            B, S, H = hidden_states.shape
            x = hidden_states.reshape(-1, H)
            T = x.shape[0]
            shared = jax.nn.silu(x @ sg_w.T) * (x @ su_w.T) @ sd_w.T
            logits = x @ gate_w.T
            scores = jax.nn.sigmoid(logits) + gate_bias
            group_scores = scores.reshape(T, G, E // G).max(axis=-1)
            _, sel_groups = lax.top_k(group_scores, TG)
            group_mask = jnp.zeros((T, G), scores.dtype).at[jnp.arange(T)[:, None], sel_groups].set(1.0)
            mask = jnp.repeat(group_mask, E // G, axis=1)
            masked_scores = scores * mask
            topk_w, topk_i = lax.top_k(masked_scores, K)
            topk_w = topk_w / (topk_w.sum(axis=-1, keepdims=True) + 1e-08)
            comb = jnp.zeros((T, E), x.dtype).at[jnp.arange(T)[:, None], topk_i].add(topk_w)
            h = jax.nn.silu(jnp.einsum('th,eih->eti', x, eg_w)) * jnp.einsum('th,eih->eti', x, eu_w)
            routed = jnp.einsum('eti,ehi,te->th', h, ed_w, comb)
            return (shared + routed).reshape(B, S, H)
        return _moe_forward(hidden_states, gate_w, gate_bias, eg_w, eu_w, ed_w, sg_w, su_w, sd_w)
    x = L0_attn_x
    xn = _layernorm(x, axis=-1)
    x = x + _L0_attn_ref(xn, L0_attn_conv1_w, L0_attn_conv1_b, L0_attn_conv2_w, L0_attn_conv2_b, L0_attn_ln0_g, L0_attn_ln0_b, L0_attn_Wq, L0_attn_bq, L0_attn_Wk, L0_attn_bk, L0_attn_Wv, L0_attn_bv, L0_attn_lnA_g, L0_attn_lnA_b, L0_attn_W1, L0_attn_b1, L0_attn_W2, L0_attn_b2, L0_attn_ln2_g, L0_attn_ln2_b) + _L0_ffn_ref(xn, L0_ffn_gate_w, L0_ffn_gate_bias, L0_ffn_eg_w, L0_ffn_eu_w, L0_ffn_ed_w, L0_ffn_sg_w, L0_ffn_su_w, L0_ffn_sd_w)
    return x

_drawn_inputs = setup_inputs


def setup_inputs(seed=0):
    import zlib

    import numpy as np

    out = dict(_drawn_inputs(seed))
    spreads = {'L0_attn_conv1_b': (0.0, 0.8),
     'L0_attn_conv2_b': (0.0, 0.388),
     'L0_attn_ln0_g': (1.0, 0.2),
     'L0_attn_ln0_b': (0.0, 0.425),
     'L0_attn_bq': (0.0, 2.0),
     'L0_attn_bk': (0.0, 2.0),
     'L0_attn_bv': (0.0, 0.339),
     'L0_attn_lnA_g': (1.0, 0.2),
     'L0_attn_lnA_b': (0.0, 0.1),
     'L0_attn_b1': (0.0, 0.684),
     'L0_attn_b2': (0.0, 0.325),
     'L0_attn_ln2_g': (1.0, 0.2),
     'L0_attn_ln2_b': (0.0, 0.318),
     'L0_ffn_gate_bias': (0.0, 0.8)}
    factors = {'L0_attn_conv1_w': 8.0,
     'L0_attn_conv2_w': 8.0,
     'L0_attn_Wq': 64.0,
     'L0_attn_Wk': 64.0,
     'L0_ffn_gate_w': 8.0,
     'L0_ffn_eg_w': 8.0,
     'L0_ffn_eu_w': 8.0,
     'L0_ffn_ed_w': 8.0,
     'L0_ffn_sg_w': 8.0,
     'L0_ffn_su_w': 8.0,
     'L0_ffn_sd_w': 8.0,
     'L0_attn_Wv': 2.846,
     'L0_attn_W1': 4.028}
    for name, (base, spread) in spreads.items():
        noise = np.random.default_rng([zlib.crc32(name.encode()), seed]).standard_normal(out[name].shape)
        drawn = base * np.exp(spread * noise) if base else spread * noise
        out[name] = jnp.asarray(drawn.astype(out[name].dtype))
    for name, factor in factors.items():
        out[name] = (out[name] * factor).astype(out[name].dtype)
    return out
```

```python
from contextlib import ExitStack

import numpy as np
import concourse.bass as bass
from concourse import mybir

F32 = mybir.dt.float32
BF16 = mybir.dt.bfloat16
I32 = mybir.dt.int32
U32 = mybir.dt.uint32
ALU = mybir.AluOpType
ACT = mybir.ActivationFunctionType
AX = mybir.AxisListType

P = 128
B, N, H = 4, 1024, 128
T = B * N
TILES = T // P
BT = N // P
HALF = 512
CT = HALF // P
E, G, TG, K, I = 64, 8, 4, 6, 64
EG = E // G
SLOT_TILES = T * K // P + E
SLOTS = SLOT_TILES * P
CHUNKS = SLOT_TILES // CT
XCHUNKS = T // HALF
LAYERS, HEADS = 4, 16
HD = H // HEADS
CG, CW, TAPS, MUL = 4, 32, 5, 4
X4W = N + 2
H1W = N + TAPS - 1
SHIFT = 0.21
EPS_X, EPS_LN, EPS_Z, EPS_W = 1e-5, 1e-12, 1e-6, 1e-8
STEPS = LAYERS * B
HALFWAY = STEPS // 2
GPARTS = ((0, 26), (26, 32))


def const_table():
    at, n = {}, 0
    for name, width in (("ident", P), ("iota_e", E), ("tri_g", G * G), ("iota_j", 2), ("dmask", CW), ("dmask3", CW),
                        ("dmask2", CW), ("bdmask", P), ("hmask", HEADS), ("rot", P), ("utri", P)):
        at[name] = (n, width)
        n += width
    return at, n


def block_kernel(nc, a, out):
    consts_at, consts_n = const_table()
    with ExitStack() as ctx:
        def sb(name, shape, dt=F32):
            return ctx.enter_context(nc.sbuf_tensor(name, shape, dt))

        def sem(name):
            return ctx.enter_context(nc.semaphore(name))

        def carve(region, sizes):
            at, views = 0, []
            for size in sizes:
                views.append(region[:, at:at + size])
                at += size
            assert at <= region.shape[1], (at, region.shape)
            return views

        xs = nc.dram_tensor("rows_in", [SLOTS, H], F32).ap()
        ys = nc.dram_tensor("rows_out", [SLOTS, H], F32).ap()
        te_dram = nc.dram_tensor("tile_expert", [P, 2], I32).ap()

        x_tm = sb("x_tm", [P, TILES, H])
        xn_tm = sb("xn_tm", [P, TILES, H])
        xn_fm = sb("xn_fm", [P, T])
        h_fm = sb("h_fm", [P, T])
        cst = sb("cst", [P, consts_n])
        c = {name: cst[:, at:at + width] for name, (at, width) in consts_at.items()}
        ident = c["ident"]
        cols = sb("cols", [P, 4 * LAYERS + 2 + 1 + 1 + 2 * MUL])
        wk = sb("wk", [P, TILES, K])
        addr = sb("addr", [P, TILES * K], I32)
        te_row = sb("te_row", [1, 2 * P], I32)
        ln2g_b = sb("ln2g_b", [P, H])
        ln2b_r = sb("ln2b_r", [1, H])
        ones_r = sb("ones_r", [1, P])
        nw_a = sb("nw_a", [P, BT])
        nw_t = sb("nw_t", [P, BT])
        rstd = sb("rstd", [P, BT])
        stats = sb("stats", [P, BT, 6])
        mv = sb("mv", [P, BT, 2])
        bq_c, bk_c, gA_c, bA_c = (cols[:, k * LAYERS:(k + 1) * LAYERS] for k in range(4))
        k0 = 4 * LAYERS
        ln0g_c, ln0b_c, cb2_c, fb2_c = (cols[:, k0 + k:k0 + k + 1] for k in range(4))
        cb1_c, fb1_c = cols[:, k0 + 4:k0 + 8], cols[:, k0 + 8:k0 + 12]

        arena = sb("arena", [P, 2 * E * H])
        u = sb("u", [P, 14144])
        w = sb("w", [P, CG * H1W])

        x4_r, w1a_r, w1b_r, w2c_r, tmp, zeros = carve(arena, [2 * CG * X4W, CG * P, CG * P, CG * TAPS * CW, 4096, 2048])
        onehot_r, scores, base_r, utri_r, ones_r_, picked_r, gate_sb, gbias, gs, grank, top8_r, idx8_r, idxf_r, slot, \
            slot_i, t1, t2, scan0, scan1, ntile, cnt_i, te_f, te_i, wsum = carve(u, [
                TILES * K * E // 2, TILES * E, (TILES + 1) * E, P // 2, P // 2, TILES * E // 2, E, E, TILES * G,
                TILES * G, TILES * 8, TILES * 8, TILES * K, TILES * K, TILES * K, TILES * K, TILES * K, E, E, E, E,
                2, 2, TILES])
        onehot = onehot_r.bitcast(BF16).rearrange("p (q e) -> p q e", e=E)
        picked = picked_r.bitcast(BF16)
        utri = utri_r.bitcast(BF16)
        ones_bf = ones_r_.bitcast(BF16)
        base = base_r.rearrange("p (t e) -> p t e", e=E)
        top8 = top8_r.rearrange("p (t k) -> p t k", k=8)
        idx8 = idx8_r.bitcast(U32).rearrange("p (t k) -> p t k", k=8)
        idxf = idxf_r.rearrange("p (t k) -> p t k", k=K)
        slot_i, t1, t2, cnt_i, te_i = (v.bitcast(I32) for v in (slot_i, t1, t2, cnt_i, te_i))
        scan = [scan0, scan1]
        st0, st1, xf0, xf1 = carve(w, [HALF] * 4)
        xn_st = [v.rearrange("p (t f) -> p t f", f=H) for v in (st0, st1)]
        xf_st = [xf0, xf1]
        x4 = x4_r.rearrange("p (r g m) -> p r g m", r=2, g=CG)
        w1a, w1b = (v.rearrange("p (g m) -> p g m", g=CG) for v in (w1a_r, w1b_r))
        w2c = w2c_r.rearrange("p (g m) -> p g m", m=CW)
        h1 = w[:, :].rearrange("p (g m) -> p g m", g=CG)
        cwv = sb("cwv", [P, 2 * CG * MUL + CG * TAPS])
        w1v, w1v4, w2v = carve(cwv, [CG * MUL, CG * MUL, CG * TAPS])
        cos_tm, sin_tm, cos_fm, sin_fm = carve(xn_fm, [N] * 4)
        wqkv_r, bv_r, kva, kvb, z = carve(w, [LAYERS * 3 * H, LAYERS * H, P, P, BT * HEADS])
        wqkv = wqkv_r.rearrange("p (l m f) -> p l m f", l=LAYERS, m=3)
        bv_b = bv_r.rearrange("p (l f) -> p l f", l=LAYERS)
        q0_, q1_, qc0, qc1, qs0, qs1, kf, kr, t2r, v0, v1, xo_r, xh_r = carve(
            u, [N] * 9 + [BT * (H + 2)] * 2 + [N] * 2)
        qp, qc, qs = [q0_, q1_], [qc0, qc1], [qs0, qs1]
        vv = [v.rearrange("p (t f) -> p t f", f=H + 2) for v in (v0, v1)]
        xo = xo_r.rearrange("p (t f) -> p t f", f=H)
        xh = xh_r.rearrange("p (t f) -> p t f", f=H)
        kacc = sb("kacc", [P, 2, 2])
        km = sb("km", [P, 1])
        kb = sb("kb", [P, 2, HEADS])
        ksum = sb("ksum", [P, 2])
        wgu_sb = arena[:, 0:E * H].rearrange("p (e v) -> p e v", e=E)
        wed_sb = arena[0:I, E * H:2 * E * H].rearrange("p (e v) -> p e v", e=E)
        xg0, xg1, xT0, xT1, sg0, sg1, hh0, hh1, hT0, hT1, yo0, yo1 = carve(u, [HALF] * 4 + [CT * I] * 4 + [HALF] * 4)
        xg = [v.rearrange("p (t f) -> p t f", f=H) for v in (xg0, xg1)]
        xT = [xT0, xT1]
        sg = [v.rearrange("p (t f) -> p t f", f=I) for v in (sg0, sg1)]
        hh = [v.rearrange("p (t f) -> p t f", f=I) for v in (hh0, hh1)]
        hT = [hT0[0:I, :], hT1[0:I, :]]
        yo = [v.rearrange("p (t f) -> p t f", f=H) for v in (yo0, yo1)]
        yg_a = arena[:, :].rearrange("p (q f) -> p q f", f=H)
        swg, swu, swd, shs0, shs1, shh0, shh1 = carve(u, [P, P, P] + [HALF] * 4)
        shs, shh = [shs0, shs1], [shh0, shh1]
        fw1, fw2, fh_r, fy0, fy1, ft0, ft1 = carve(u, [4 * H, 4 * H, 8 * HALF] + [HALF] * 4)
        fh = fh_r.rearrange("p (b j m) -> p b j m", b=2, j=MUL)
        fy, ft = [fy0, fy1], [v.rearrange("p (t f) -> p t f", f=H) for v in (ft0, ft1)]

        bank = [ctx.enter_context(nc.psum_tensor(f"bank{k}", [P, HALF], F32)) for k in range(8)]

        x_in = [sem(f"x_in{q}") for q in range(4)]
        const_in = sem("const_in")
        param_in = sem("param_in")
        attn_in = sem("attn_in")
        tables_in = sem("tables_in")
        experts_in = sem("experts_in")
        shared_in = sem("shared_in")
        ffn_in = sem("ffn_in")
        fills = sem("fills")
        rows_zero = sem("rows_zero")
        xn_ready = sem("xn_ready")
        xn_kept = sem("xn_kept")
        xt_ps = sem("xt_ps")
        xf_ready = sem("xf_ready")
        xf_kept = sem("xf_kept")
        logits_ps = sem("logits_ps")
        sig_ready = sem("sig_ready")
        pick_ready = sem("pick_ready")
        count_ps = sem("count_ps")
        base_ready = sem("base_ready")
        rank_ps = sem("rank_ps")
        rank_read = sem("rank_read")
        addr_ready = sem("addr_ready")
        te_ready = sem("te_ready")
        te_out = sem("te_out")
        te_in = sem("te_in")
        scattered = sem("scattered")
        convw_ready = sem("convw_ready")
        x4_in = [sem(f"x4_in{r}") for r in range(2)]
        c1_ps = sem("c1_ps")
        c1_done = sem("c1_done")
        c2_ps = sem("c2_ps")
        c2_done = sem("c2_done")
        res_ps = sem("res_ps")
        res_read = sem("res_read")
        xh_ready = sem("xh_ready")
        back_ps = sem("back_ps")
        back_done = sem("back_done")
        h_ready = sem("h_ready")
        qk_ps = sem("qk_ps")
        qk_done = sem("qk_done")
        v_ps = sem("v_ps")
        v_done = sem("v_done")
        kb_ready = sem("kb_ready")
        q_ready = sem("q_ready")
        kt_ps = sem("kt_ps")
        kr_ready = sem("kr_ready")
        kvden_ps = sem("kvden_ps")
        kva_ready = sem("kva_ready")
        den_read = sem("den_read")
        kvb_ps = sem("kvb_ps")
        kvb_ready = sem("kvb_ready")
        out_ps = sem("out_ps")
        out_read = sem("out_read")
        phase = sem("phase")
        shg_ps = sem("shg_ps")
        shs_ready = sem("shs_ready")
        shh_ready = sem("shh_ready")
        shd_ps = sem("shd_ps")
        shd_read = sem("shd_read")
        rows_in = [sem(f"rows_in{b}") for b in range(2)]
        rowsT_ps = sem("rowsT_ps")
        rowsT_ready = sem("rowsT_ready")
        gu_ps = sem("gu_ps")
        silu_ready = sem("silu_ready")
        gated_ready = sem("gated_ready")
        gatedT_ps = sem("gatedT_ps")
        gatedT_ready = sem("gatedT_ready")
        down_ps = sem("down_ps")
        rows_ready = sem("rows_ready")
        rows_out = [sem(f"rows_out{b}") for b in range(2)]
        gathered = sem("gathered")
        part_done = sem("part_done")
        f1_ps = sem("f1_ps")
        fh_ready = sem("fh_ready")
        f2_ps = sem("f2_ps")
        fy_ready = sem("fy_ready")
        fy_ps = sem("fy_ps")
        fy_read = sem("fy_read")
        sum_ready = sem("sum_ready")
        out_sent = sem("out_sent")

        NFILL = SLOTS // (P * 16)
        NX4 = CG * 4
        NCONST = 4
        NPARAM = 3

        x_v = a["x"].rearrange("b (t p) f -> p (b t) f", p=P)
        out_v = out.rearrange("b (t p) f -> p (b t) f", p=P)
        xs_v = xs.rearrange("(c p r) f -> c p (r f)", p=P, r=CT)
        ys_v = ys.rearrange("(c p r) f -> c p (r f)", p=P, r=CT)
        fill_v = xs.rearrange("(z p r) f -> z p (r f)", p=P, r=16)

        def yg(t, k):
            q = t * K + k
            n = 2 * E
            return yg_a[:, q, :] if q < n else xn_tm[:, q - n, :]

        def is_first(i):
            return isinstance(i, int) and i == 0

        def pipeline(eng, count, stages):
            def step(i, b):
                for off, stage in stages:
                    o = b + off
                    if isinstance(i, int) and not 0 <= 2 * i + o < count:
                        continue
                    stage(i + o // 2, o % 2)

            last = count // 2 - 2
            for s in range(-1, 4):
                step(s // 2, s % 2)
            with eng.Fori(2, last + 1) as i:
                step(i, 0)
                step(i, 1)
            for s in range(2 * last + 2, count + 2):
                step(s // 2, s % 2)

        def phase_end(eng, k):
            eng.drain().then_inc(phase, 1)
            eng.wait_ge(phase, 3 * k)

        block = ctx.enter_context(nc.Block())

        @block.sync
        def _(sp):
            n = TILES // 4
            for q in range(4):
                sp.dma_start(x_tm[:, q * n:(q + 1) * n, :], x_v[:, q * n:(q + 1) * n, :]).then_inc(x_in[q], 16)
                if q == 0:
                    sp.dma_start(cst[:, :], a["consts"]).then_inc(const_in, 16)
                    sp.dma_start(gate_sb, a["gate_w"]).then_inc(const_in, 16)
                    sp.dma_start(gbias, a["gate_bias"].rearrange("(a e) -> a e", a=1).broadcast_to([P, E])).then_inc(const_in, 16)
                    sp.dma_start(cwv[:, :], a["conv_w"]).then_inc(const_in, 16)
            sp.dma_start(cols[:, :], a["cols"]).then_inc(param_in, 16)
            sp.dma_start(ln2g_b[:, :], a["ln2_g"].rearrange("(a f) -> a f", a=1).broadcast_to([P, H])).then_inc(param_in, 16)
            sp.dma_start(ln2b_r[:, :], a["ln2_b"].rearrange("(a f) -> a f", a=1)).then_inc(param_in, 16)
            sp.wait_ge(fills, 1)
            for k in range(NFILL):
                sp.dma_start(fill_v[k], zeros).then_inc(rows_zero, 16)
            sp.wait_ge(te_ready, 1)
            sp.dma_start(te_dram[:, :], te_i).then_inc(te_out, 16)
            sp.wait_ge(te_out, 16)
            sp.dma_start(te_row[:, :], te_dram.rearrange("(o p) a -> o (p a)", o=1)).then_inc(te_in, 16)
            sp.wait_ge(c2_ps, 2 * B)
            sp.dma_start(wqkv, a["wqkv"]).then_inc(attn_in, 16)
            sp.dma_start(bv_r, a["bv"].rearrange("(a l) f -> a (l f)", a=1).broadcast_to([P, LAYERS * H])).then_inc(attn_in, 16)
            sp.wait_ge(addr_ready, 1)
            sp.dma_start(swg, a["sg"]).then_inc(shared_in, 16)
            sp.dma_start(swu, a["su"]).then_inc(shared_in, 16)
            sp.dma_start(swd, a["sd"]).then_inc(shared_in, 16)
            sp.wait_ge(rows_zero, 16 * NFILL)
            sp.dma_start(wgu_sb, a["wgu"]).then_inc(experts_in, 16)
            sp.dma_start(wed_sb, a["wed"]).then_inc(experts_in, 16)
            sp.wait_ge(phase, 3)
            sp.dma_start(xn_fm[:, :], a["rope"]).then_inc(tables_in, 16)

            def load_rows(i, b):
                if not is_first(i):
                    sp.wait_ge(rowsT_ps, i * 2 + (b - 1))
                sp.dma_start(xg[b].rearrange("p r f -> p (r f)"), xs_v[bass.ds(i * 2 + b, 1)]).then_inc(rows_in[b], 16)

            def store_rows(i, b):
                sp.wait_ge(rows_ready, i * 2 + (b + 1))
                sp.dma_start(ys_v[bass.ds(i * 2 + b, 1)], yo[b].rearrange("p r f -> p (r f)")).then_inc(rows_out[b], 16)

            sp.wait_ge(scattered, 16 * TILES * K)
            sp.wait_ge(phase, 6)
            load_rows(0, 0)
            load_rows(0, 1)
            load_rows(1, 0)
            with sp.Fori(0, CHUNKS // 2 - 2) as i:
                load_rows(i + 1, 1)
                store_rows(i, 0)
                load_rows(i + 2, 0)
                store_rows(i, 1)
            load_rows(CHUNKS // 2 - 1, 1)
            for q in range(CHUNKS - 4, CHUNKS):
                store_rows(q // 2, q % 2)
            sp.wait_ge(phase, 12)
            sp.dma_start(fw1, a["w1"]).then_inc(ffn_in, 16)
            sp.dma_start(fw2.rearrange("p (j f) -> p j f", f=H), a["w2"].rearrange("(j p) f -> p j f", p=P)).then_inc(ffn_in, 16)
            for k, (lo, hi) in enumerate(GPARTS):
                sp.wait_ge(sum_ready, k + 1)
                sp.dma_start(out_v[:, lo:hi, :], x_tm[:, lo:hi, :]).then_inc(out_sent, 16)
            sp.wait_ge(out_sent, 16 * len(GPARTS))

        @block.gpsimd
        def _(pool):
            pool.memset(zeros, 0.0).then_inc(fills, 1)
            pool.memset(ones_bf, 1.0).then_inc(fills, 1)
            pool.memset(ones_r[:, :], 1.0).then_inc(fills, 1)
            x4_all = x4_r.rearrange("p (q m) -> p q m", m=X4W)
            pool.memset(x4_all[:, :, 0:2], 0.0).then_inc(fills, 1)
            pool.memset(x4_all[:, :, N - 2:X4W], 0.0).then_inc(fills, 1)

            def keep(i, b):
                c1 = i * 2 + (b + 1)
                pool.wait_ge(xn_ready, c1)
                pool.tensor_copy(xn_tm[:, bass.ds(i * 8 + b * CT, CT), :], xn_st[b]).then_inc(xn_kept, 1)
                pool.wait_ge(xf_ready, c1)
                pool.tensor_copy(xn_fm[:, bass.ds((i * 2 + b) * HALF, HALF)], xf_st[b]).then_inc(xf_kept, 1)

            for b in range(2):
                keep(0, b)
            with pool.Fori(1, XCHUNKS // 2) as i:
                for b in range(2):
                    keep(i, b)
            pool.wait_ge(xf_kept, XCHUNKS)
            pool.wait_ge(xn_kept, XCHUNKS)
            pool.wait_ge(logits_ps, XCHUNKS)
            pool.memset(h1[:, :, 0:2], 0.0).then_inc(fills, 1)
            pool.memset(h1[:, :, N + 2:], 0.0).then_inc(fills, 1)

            pool.wait_ge(addr_ready, 1)
            pool.wait_ge(rows_zero, 16 * NFILL)
            for t in range(TILES):
                for k in range(K):
                    q = t * K + k
                    pool.indirect_dma_start(xs[:, :], bass.IndirectOffsetOnAxis(addr[:, q:q + 1].bitcast(U32), 0),
                                            xn_tm[:, t, :], None).then_inc(scattered, 16)
            for b in range(2):
                pool.wait_ge(rows_out[b], 16 * CHUNKS // 2)
            pool.wait_ge(phase, 9)
            for part, (lo, hi) in enumerate(GPARTS):
                if part:
                    pool.wait_ge(part_done, part)
                for t in range(lo, hi):
                    for k in range(K):
                        q = t * K + k
                        pool.indirect_dma_start(yg(t - lo, k), None, ys[:, :],
                                                bass.IndirectOffsetOnAxis(addr[:, q:q + 1].bitcast(U32), 0)).then_inc(gathered, 16)

        @block.vector
        def _(dve):
            def inv_sqrt(n, eps):
                y, var, s, t = rstd[:, 0:n], mv[:, 0:n, 1], nw_a[:, 0:n], nw_t[:, 0:n]
                dve.tensor_scalar(s, var, eps, None, ALU.add)
                dve.drain()
                dve.tensor_scalar(t.bitcast(I32), s.bitcast(I32), 1, None, ALU.logical_shift_right)
                dve.drain()
                dve.tensor_scalar(y.bitcast(I32), t.bitcast(I32), -1.0, float(0x5f3759df), ALU.mult, ALU.add)
                for _ in range(3):
                    dve.drain()
                    dve.scalar_tensor_tensor(t, y, -0.5, y, ALU.mult, ALU.mult)
                    dve.drain()
                    dve.tensor_tensor(t, t, s, ALU.mult)
                    dve.drain()
                    dve.scalar_tensor_tensor(y, t, 1.5, y, ALU.add, ALU.mult)

            def moments(n, tile, eps):
                for t in range(n):
                    dve.bn_stats(stats[:, t, :], tile(t))
                dve.drain()
                for t in range(n):
                    dve.bn_aggr(mv[:, t, :], stats[:, t, :])
                dve.drain()
                inv_sqrt(n, eps)
                dve.drain()

            def norm(i, b):
                def tile(t):
                    return x_tm[:, bass.ds(i * (2 * CT) + (b * CT + t), 1), :].rearrange("p a f -> p (a f)")

                moments(CT, tile, EPS_X)
                if not is_first(i):
                    dve.wait_ge(xt_ps, i * 2 + (b - 1))
                    dve.wait_ge(xn_kept, i * 2 + (b - 1))
                for t in range(CT):
                    ins = dve.tensor_scalar(xn_st[b][:, t, :], tile(t), mv[:, t, 0:1], rstd[:, t:t + 1],
                                            ALU.subtract, ALU.mult)
                ins.then_inc(xn_ready, 1)
                dve.drain()

            dve.wait_ge(x_in[0], 16)
            for b in range(2):
                norm(0, b)
            for q in range(1, 4):
                dve.wait_ge(x_in[q], 16)
            with dve.Fori(1, XCHUNKS // 2) as i:
                for b in range(2):
                    norm(i, b)

            dve.wait_ge(const_in, 16 * NCONST)
            for dst, mask, val in ((w1a, c["dmask"], w1v), (w1b, c["dmask3"], w1v4)):
                dve.tensor_tensor(dst.rearrange("p g (c j) -> p g c j", j=MUL),
                                  mask.unsqueeze(1).unsqueeze(3).broadcast_to([P, CG, CW, MUL]),
                                  val.rearrange("p (g j) -> p g j", j=MUL).unsqueeze(2).broadcast_to([P, CG, CW, MUL]), ALU.mult)
            dve.tensor_tensor(w2c, c["dmask2"].unsqueeze(1).broadcast_to([P, CG * TAPS, CW]),
                              w2v.unsqueeze(2).broadcast_to([P, CG * TAPS, CW]), ALU.mult)
            dve.tensor_copy(utri, c["utri"])
            dve.drain().then_inc(convw_ready, 1)

            dve.wait_ge(sig_ready, XCHUNKS)
            sc3 = scores.rearrange("p (t e) -> p t e", e=E)
            dve.tensor_tensor(sc3, sc3, gbias.unsqueeze(1).broadcast_to([P, TILES, E]), ALU.add)
            dve.drain()
            dve.tensor_reduce(gs, scores.rearrange("p (g e) -> p g e", e=EG), AX.X, ALU.max)
            dve.drain()
            g3 = gs.rearrange("p (t g) -> p t g", g=G)
            other = g3.unsqueeze(2).broadcast_to([P, TILES, G, G])
            own = g3.unsqueeze(3).broadcast_to([P, TILES, G, G])
            beats, ties = (v.rearrange("p (t g h) -> p t g h", g=G, h=G) for v in (tmp[:, 0:2048], tmp[:, 2048:4096]))
            tri = c["tri_g"].rearrange("p (g h) -> p g h", g=G).unsqueeze(1).broadcast_to([P, TILES, G, G])
            dve.tensor_tensor(ties, other, own, ALU.is_equal)
            dve.tensor_tensor(beats, other, own, ALU.is_gt)
            dve.drain()
            dve.tensor_tensor(ties, ties, tri, ALU.mult)
            dve.drain()
            dve.tensor_tensor(beats, beats, ties, ALU.add)
            dve.drain()
            dve.tensor_reduce(grank, tmp[:, 0:2048].rearrange("p (g h) -> p g h", h=G), AX.X, ALU.add)
            dve.drain()
            dve.tensor_scalar(grank, grank, TG - 0.5, None, ALU.is_lt)
            dve.drain()
            sce = scores.rearrange("p (g e) -> p g e", e=EG)
            dve.tensor_tensor(sce, sce, grank.unsqueeze(2).broadcast_to([P, TILES * G, EG]), ALU.mult)
            dve.drain()
            for t in range(TILES):
                dve.max(top8[:, t, :], sc3[:, t, :])
            dve.drain()
            for t in range(TILES):
                dve.max_index(idx8[:, t, :], top8[:, t, :], sc3[:, t, :])
            dve.tensor_reduce(wsum, top8[:, :, 0:K], AX.X, ALU.add)
            dve.drain()
            dve.tensor_copy(idxf, idx8[:, :, 0:K])
            dve.tensor_scalar(wsum, wsum, EPS_W, None, ALU.add)
            dve.drain()
            dve.reciprocal(wsum, wsum)
            dve.tensor_tensor(onehot, idxf_r.unsqueeze(2).broadcast_to([P, TILES * K, E]),
                              c["iota_e"].unsqueeze(1).broadcast_to([P, TILES * K, E]), ALU.is_equal)
            dve.drain()
            dve.tensor_tensor(wk[:, :, :], top8[:, :, 0:K], wsum.unsqueeze(2).broadcast_to([P, TILES, K]), ALU.mult)
            with nc.allow_low_precision("zeros and ones"):
                dve.tensor_reduce(picked.rearrange("p (t e) -> p t e", e=E),
                                  onehot.rearrange("p (t k) e -> p t e k", k=K), AX.X, ALU.add).then_inc(pick_ready, 1)
            dve.memset(base[:, 0, :], 0.0)
            dve.wait_ge(count_ps, 1)
            for t in range(TILES):
                dve.drain()
                dve.tensor_tensor(base[:, t + 1, :], base[:, t, :], bank[4 + t // 8][:, (t % 8) * E:(t % 8 + 1) * E], ALU.add)
            dve.drain().then_inc(base_ready, 1)
            dve.tensor_scalar(cnt_i, base[:, TILES, :], float(P - 1), None, ALU.add)
            dve.drain()
            dve.tensor_scalar(cnt_i, cnt_i, 7, None, ALU.logical_shift_right)
            dve.drain()
            dve.tensor_copy(scan[0], cnt_i)
            dve.tensor_copy(ntile, cnt_i)
            s = 0
            for d in (1, 2, 4, 8, 16, 32):
                dve.drain()
                dve.tensor_tensor(scan[1 - s][:, d:], scan[s][:, d:], scan[s][:, :E - d], ALU.add)
                dve.tensor_copy(scan[1 - s][:, :d], scan[s][:, :d])
                s = 1 - s
            dve.drain()
            incl = scan[s]
            tm = tmp[:, 0:2 * E].rearrange("p (a e) -> p a e", e=E)
            dve.tensor_tensor(tm, incl.unsqueeze(1).broadcast_to([P, 2, E]),
                              c["iota_j"].unsqueeze(2).broadcast_to([P, 2, E]), ALU.is_le)
            dve.tensor_tensor(ntile, incl, ntile, ALU.subtract)
            dve.drain()
            dve.tensor_reduce(te_f, tm, AX.X, ALU.add)
            dve.tensor_scalar(ntile, ntile, float(P), None, ALU.mult)
            dve.drain()
            dve.tensor_scalar(te_i, te_f, float(E - 1), None, ALU.min).then_inc(te_ready, 1)
            dve.tensor_tensor(base[:, 0:TILES, :], base[:, 0:TILES, :],
                              ntile.unsqueeze(1).broadcast_to([P, TILES, E]), ALU.add)
            dve.drain()
            dve.wait_ge(rank_ps, 1)
            for k in range(4):
                ins = dve.tensor_tensor(scores[:, k * 512:(k + 1) * 512], bank[4 + k][:, :],
                                        base[:, k * 8:(k + 1) * 8, :].rearrange("p t e -> p (t e)"), ALU.add)
            ins.then_inc(rank_read, 1)
            nt = 8
            for k in range(TILES // nt):
                dve.drain()
                dve.tensor_tensor(tmp[:, 0:nt * K * E].rearrange("p (t k e) -> p t k e", k=K, e=E),
                                  onehot[:, k * nt * K:(k + 1) * nt * K, :].rearrange("p (t k) e -> p t k e", k=K),
                                  sc3[:, k * nt:(k + 1) * nt, :].unsqueeze(2).broadcast_to([P, nt, K, E]), ALU.mult)
                dve.drain()
                dve.tensor_reduce(slot[:, k * nt * K:(k + 1) * nt * K],
                                  tmp[:, 0:nt * K * E].rearrange("p (q e) -> p q e", e=E), AX.X, ALU.add)
            dve.drain()
            dve.tensor_copy(slot_i, slot)
            dve.drain()
            dve.tensor_scalar(t1, slot_i, P - 1, 2, ALU.bitwise_and, ALU.logical_shift_left)
            dve.tensor_scalar(t2, slot_i, 7, CT - 1, ALU.logical_shift_right, ALU.bitwise_and)
            dve.tensor_scalar(addr[:, :], slot_i, 0x7fffffff ^ (HALF - 1), None, ALU.bitwise_and)
            dve.drain()
            dve.tensor_tensor(t1, t1, t2, ALU.bitwise_or)
            dve.drain()
            dve.tensor_tensor(addr[:, :], t1, addr[:, :], ALU.bitwise_or)
            dve.drain().then_inc(addr_ready, 1)

            def normalize(n, eps):
                moments(BT, lambda t: xo[:, t, :], eps)
                if n:
                    dve.wait_ge(back_ps, 2 * n)
                for t in range(BT):
                    dve.tensor_scalar(xh[:, t, :], xo[:, t, :], mv[:, t, 0:1], rstd[:, t:t + 1], ALU.subtract, ALU.mult)
                dve.drain().then_inc(xh_ready, 1)

            dve.wait_ge(te_out, 16)
            for b in range(B):
                for hf in range(2):
                    dve.wait_ge(res_ps, 2 * b + hf + 1)
                    t0 = b * BT + hf * CT
                    dve.tensor_tensor(xo[:, hf * CT:(hf + 1) * CT, :].rearrange("p t f -> p (t f)"), bank[5 + hf][:, :],
                                      xn_tm[:, t0:t0 + CT, :].rearrange("p t f -> p (t f)"), ALU.add).then_inc(res_read, 1)
                dve.drain()
                normalize(b, EPS_LN)

            def key_mean(n):
                r = n % 2
                dve.wait_ge(qk_done, 4 * n + 2)
                dve.tensor_tensor(km[:, :], kacc[:, r, 0:1], kacc[:, r, 1:2], ALU.add)
                dve.drain()
                dve.tensor_scalar(km[:, :], km[:, :], 1.0 / N, SHIFT, ALU.mult, ALU.add)
                dve.drain()
                dve.tensor_scalar(kb[:, r, :], c["hmask"], km[:, :], None, ALU.mult)
                dve.drain().then_inc(kb_ready, 1)

            def key_values(n):
                dve.wait_ge(kvden_ps, n + 1)
                dve.tensor_copy(ksum[:, :], bank[4][:, H:H + 2])
                dve.tensor_scalar(z, bank[4][:, 384:512], EPS_Z, None, ALU.add)
                dve.drain().then_inc(den_read, 1)
                dve.scalar_tensor_tensor(kva[:, :], bv_b[:, n // B, :], ksum[:, 0:1], bank[4][:, 0:H], ALU.mult, ALU.add)
                dve.drain()
                dve.tensor_tensor(kva[:, :], kva[:, :], c["bdmask"], ALU.mult).then_inc(kva_ready, 1)
                dve.reciprocal(z, z)
                dve.drain()

            def queries(n):
                r = n % 2
                dve.wait_ge(qk_done, 4 * n + 4)
                dve.tensor_scalar(qp[r], qp[r], SHIFT, None, ALU.add)
                dve.drain()
                dve.tensor_tensor(qc[r], qp[r], cos_fm, ALU.mult)
                dve.tensor_tensor(qs[r], qp[r], sin_fm, ALU.mult).then_inc(q_ready, 1)

            def keys(n):
                if n:
                    dve.wait_ge(kvden_ps, n)
                for hf in range(2):
                    dve.wait_ge(kt_ps, 2 * n + hf + 1)
                    s = slice(hf * HALF, (hf + 1) * HALF)
                    ev, od = slice(hf * HALF, (hf + 1) * HALF, 2), slice(hf * HALF + 1, (hf + 1) * HALF, 2)
                    dve.scalar_tensor_tensor(kr[:, s], bank[hf][:, :], SHIFT, cos_tm[:, s], ALU.add, ALU.mult)
                    dve.scalar_tensor_tensor(t2r[:, ev], bank[hf][:, 1::2], SHIFT, sin_tm[:, ev], ALU.add, ALU.mult)
                    dve.scalar_tensor_tensor(t2r[:, od], bank[hf][:, 0::2], SHIFT, sin_tm[:, od], ALU.add, ALU.mult)
                    dve.drain()
                    dve.tensor_tensor(kr[:, s], kr[:, s], t2r[:, s], ALU.add).then_inc(kr_ready, 1)

            def attended(n):
                for hf in range(2):
                    o = xo[:, hf * CT:(hf + 1) * CT, :].rearrange("p t (h d) -> p (t h) d", d=HD)
                    zz = z[:, hf * CT * HEADS:(hf + 1) * CT * HEADS].unsqueeze(2).broadcast_to([P, CT * HEADS, HD])
                    dve.wait_ge(out_ps, 2 * n + hf + 1)
                    dve.tensor_tensor(o, bank[5 + hf][:, :].rearrange("p (t d) -> p t d", d=HD), zz, ALU.mult).then_inc(out_read, 1)
                dve.drain()
                for hf in range(2):
                    o = xo[:, hf * CT:(hf + 1) * CT, :].rearrange("p t f -> p (t f)")
                    dve.wait_ge(res_ps, 2 * (B + n) + hf + 1)
                    dve.tensor_tensor(o, o, bank[2 + hf][:, :], ALU.add).then_inc(res_read, 1)
                dve.drain()
                normalize(B + n, EPS_LN)

            def attention(n0, n1):
                for n in range(n0, n1 + 1):
                    if n < n1:
                        key_mean(n)
                    if n > n0:
                        key_values(n - 1)
                    if n < n1:
                        if n == 0:
                            dve.wait_ge(tables_in, 16)
                        queries(n)
                        keys(n)
                    if n > n0:
                        attended(n - 1)

            def shared_gated(i, b):
                dve.wait_ge(shs_ready, i * 2 + (b + 1))
                if not is_first(i):
                    dve.wait_ge(shd_ps, i * 2 + (b - 1))
                dve.tensor_tensor(shh[b], shs[b], bank[2 + b][:, :], ALU.mult).then_inc(shh_ready, 1)

            def shared_sum(i, b):
                dve.wait_ge(shd_ps, i * 2 + (b + 1))
                dst = x_tm[:, bass.ds(i * 2 * CT + b * CT, CT), :].rearrange("p t f -> p (t f)")
                dve.tensor_tensor(dst, dst, bank[4 + b][:, :], ALU.add).then_inc(shd_read, 1)

            pipeline(dve, XCHUNKS, [(0, shared_gated), (-1, shared_sum)])
            phase_end(dve, 1)

            dve.wait_ge(attn_in, 32)
            attention(0, HALFWAY)
            phase_end(dve, 2)

            def gated(i, b):
                dve.wait_ge(silu_ready, i * 2 + (b + 1))
                if not is_first(i):
                    dve.wait_ge(gatedT_ps, i * 2 + (b - 1))
                g4 = bank[2 + b][:, :].rearrange("p (c v) -> p c v", v=2 * I)
                dve.tensor_tensor(hh[b], sg[b], g4[:, :, I:], ALU.mult).then_inc(gated_ready, 1)

            def gated_columns(i, b):
                dve.wait_ge(gatedT_ps, i * 2 + (b + 1))
                if not is_first(i):
                    dve.wait_ge(down_ps, i * 2 + (b - 1))
                hT4 = hT[b].rearrange("p (q a s) -> p q a s", a=2, s=P)
                for k in range(2):
                    ins = dve.tensor_copy(hT4[:, :, k, :],
                                          bank[4 + b][k * I:(k + 1) * I, 0:2 * P].rearrange("p (q s) -> p q s", s=P))
                ins.then_inc(gatedT_ready, 1)

            def expert_rows(i, b):
                dve.wait_ge(down_ps, i * 2 + (b + 1))
                if not is_first(i):
                    dve.wait_ge(rows_out[b], i * 16)
                dve.tensor_copy(yo[b].rearrange("p c f -> p (c f)"), bank[6 + b][:, :]).then_inc(rows_ready, 1)

            pipeline(dve, CHUNKS, [(0, gated), (-1, gated_columns), (-2, expert_rows)])
            phase_end(dve, 3)
            for b in range(2):
                dve.wait_ge(rows_out[b], 16 * CHUNKS // 2)

            attention(HALFWAY, STEPS)
            phase_end(dve, 4)

            def ffn_residual(i, b):
                dve.wait_ge(f2_ps, i * 2 + (b + 1))
                if not is_first(i):
                    dve.wait_ge(fy_ps, i * 2 + (b - 1))
                dve.scalar_tensor_tensor(fy[b], bank[2 + b][:, :], fb2_c, h_fm[:, bass.ds(i * 2 * HALF + b * HALF, HALF)],
                                         ALU.add, ALU.add).then_inc(fy_ready, 1)

            def ffn_norm(i, b):
                dve.wait_ge(fy_ps, i * 2 + (b + 1))
                tile = lambda t: bank[4 + b][:, t * H:(t + 1) * H]
                moments(CT, tile, EPS_LN)
                for t in range(CT):
                    ins = dve.scalar_tensor_tensor(ft[b][:, t, :], tile(t), mv[:, t, 0:1], ln2g_b[:, :], ALU.subtract, ALU.mult)
                ins.then_inc(fy_read, 1)
                dve.drain()
                for t in range(CT):
                    dst = x_tm[:, bass.ds(i * 2 * CT + b * CT + t, 1), :].rearrange("p t f -> p (t f)")
                    dve.scalar_tensor_tensor(dst, ft[b][:, t, :], rstd[:, t:t + 1], dst, ALU.mult, ALU.add)
                dve.drain()

            pipeline(dve, XCHUNKS, [(-1, ffn_residual), (-2, ffn_norm)])

            done = 0
            for part, (lo, hi) in enumerate(GPARTS):
                done += (hi - lo) * K
                dve.wait_ge(gathered, 16 * done)
                for k in range(K):
                    for t in range(lo, hi):
                        dve.scalar_tensor_tensor(x_tm[:, t, :], yg(t - lo, k), wk[:, t, k:k + 1], x_tm[:, t, :], ALU.mult, ALU.add)
                    if k < K - 1:
                        dve.drain()
                dve.drain().then_inc(part_done, 1)
                dve.nop().then_inc(sum_ready, 1)

        @block.scalar
        def _(act):
            def stage(i, b):
                c1 = i * 2 + (b + 1)
                act.wait_ge(xt_ps, c1)
                if not is_first(i):
                    act.wait_ge(logits_ps, i * 2 + (b - 1))
                    act.wait_ge(xf_kept, i * 2 + (b - 1))
                act.activation(xf_st[b], bank[b][:, :], ACT.Copy).then_inc(xf_ready, 1)
                act.wait_ge(logits_ps, c1)
                act.activation(scores[:, bass.ds((i * 2 + b) * (CT * E), CT * E)], bank[2 + b][:, 0:CT * E],
                               ACT.Sigmoid).then_inc(sig_ready, 1)

            for b in range(2):
                stage(0, b)
            with act.Fori(1, XCHUNKS // 2) as i:
                for b in range(2):
                    stage(i, b)

            def load_x4(b):
                r = b % 2
                act.wait_ge(xf_kept, 2 * (b + 1))
                for g in range(CG):
                    for s in range(4):
                        lo, hi = max(0, 2 - s), min(X4W, N + 2 - s)
                        act.dma_start(x4[CW * s:CW * (s + 1), r, g, lo:hi],
                                      xn_fm[CW * g:CW * (g + 1), b * N + lo + s - 2:b * N + hi + s - 2]).then_inc(x4_in[r], 16)

            act.wait_ge(fills, 5)
            load_x4(0)
            load_x4(1)
            act.wait_ge(param_in, 16 * NPARAM)
            act.wait_ge(fills, 7)
            for b in range(B):
                for g in range(CG):
                    for hf in range(2):
                        n = (b * CG + g) * 2 + hf
                        act.wait_ge(c1_ps, n + 1)
                        if b and g == 0 and hf == 0:
                            act.wait_ge(c2_ps, 2 * b)
                        act.activation(h1[:, g, 2 + hf * HALF:2 + (hf + 1) * HALF], bank[hf][:, :], ACT.Gelu,
                                       bias=cb1_c[:, g:g + 1]).then_inc(c1_done, 1)
                if b + 2 < B:
                    load_x4(b + 2)
                for hf in range(2):
                    act.wait_ge(c2_ps, 2 * b + hf + 1)
                    act.activation(h_fm[:, b * N + hf * HALF:b * N + (hf + 1) * HALF], bank[2 + hf][:, :], ACT.Identity,
                                   bias=cb2_c).then_inc(c2_done, 1)

            def feature_major(n, g, bias):
                for hf in range(2):
                    s = (n % B) * N + hf * HALF
                    act.wait_ge(back_ps, 2 * n + hf + 1)
                    act.activation(h_fm[:, s:s + HALF], bank[7][:, :], ACT.Identity, bias=bias, scale=g).then_inc(back_done, 1)
                act.drain().then_inc(h_ready, 1)

            for b in range(B):
                feature_major(b, ln0g_c, ln0b_c)

            def projected(n):
                l, r = n // B, n % 2
                if n:
                    act.wait_ge(kt_ps, 2 * n)
                if n >= 2:
                    act.wait_ge(kb_ready, n - 1)
                for hf in range(2):
                    act.wait_ge(qk_ps, 4 * n + hf + 1)
                    act.activation(kf[:, hf * HALF:(hf + 1) * HALF], bank[hf][:, :], ACT.Gelu, bias=bk_c[:, l:l + 1],
                                   accum_out=kacc[:, r, hf:hf + 1]).then_inc(qk_done, 1)
                if n >= 2:
                    act.wait_ge(out_ps, 2 * (n - 1))
                for hf in range(2):
                    act.wait_ge(qk_ps, 4 * n + 2 + hf + 1)
                    act.activation(qp[r][:, hf * HALF:(hf + 1) * HALF], bank[hf][:, :], ACT.Gelu,
                                   bias=bq_c[:, l:l + 1]).then_inc(qk_done, 1)
                for hf in range(2):
                    act.wait_ge(v_ps, 2 * n + hf + 1)
                    act.activation(vv[r][:, hf * CT:(hf + 1) * CT, 0:H],
                                   bank[2 + hf][:, :].rearrange("p (t f) -> p t f", f=H), ACT.Copy).then_inc(v_done, 1)

            def rotated(n):
                act.wait_ge(kvb_ps, n + 1)
                if n:
                    act.wait_ge(out_ps, 2 * n)
                act.activation(kvb[:, :], bank[4][:, 256:384], ACT.Copy).then_inc(kvb_ready, 1)

            def attention(n0, n1):
                for r in range(2):
                    act.activation(vv[r][:, :, H:H + 2], ident[:, 0:2 * BT].rearrange("p (t o) -> p t o", o=2),
                                   ACT.Identity, bias=1.0, scale=0.0)
                act.drain().then_inc(v_done, 1)
                for n in range(n0, n1 + 2):
                    if n < n1:
                        projected(n)
                    if n > n0 + 1:
                        m = n - 2
                        feature_major(B + m, gA_c[:, m // B:m // B + 1], bA_c[:, m // B:m // B + 1])
                    if n0 < n <= n1:
                        rotated(n - 1)

            def shared_silu(i, b):
                act.wait_ge(shg_ps, i * 2 + (b + 1))
                if not is_first(i):
                    act.wait_ge(shh_ready, i * 2 + (b - 1))
                act.activation(shs[b], bank[b][:, :], ACT.Silu).then_inc(shs_ready, 1)

            pipeline(act, XCHUNKS, [(0, shared_silu)])
            phase_end(act, 1)

            attention(0, HALFWAY)
            phase_end(act, 2)

            def columns(i, b):
                act.wait_ge(rowsT_ps, i * 2 + (b + 1))
                if not is_first(i):
                    act.wait_ge(gu_ps, i * 2 + (b - 1))
                act.activation(xT[b], bank[b][:, :], ACT.Copy).then_inc(rowsT_ready, 1)

            def silu(i, b):
                act.wait_ge(gu_ps, i * 2 + (b + 1))
                if not is_first(i):
                    act.wait_ge(gated_ready, i * 2 + (b - 1))
                g4 = bank[2 + b][:, :].rearrange("p (c v) -> p c v", v=2 * I)
                act.activation(sg[b], g4[:, :, 0:I], ACT.Silu).then_inc(silu_ready, 1)

            pipeline(act, CHUNKS, [(1, columns), (0, silu)])
            phase_end(act, 3)
            for b in range(2):
                act.wait_ge(rows_out[b], 16 * CHUNKS // 2)

            attention(HALFWAY, STEPS)
            phase_end(act, 4)

            def ffn_gelu(i, b):
                if not is_first(i):
                    act.wait_ge(f2_ps, i * 2 + (b - 1))
                for j in range(MUL):
                    act.wait_ge(f1_ps, i * (2 * MUL) + (b * MUL + j + 1))
                    act.activation(fh[:, b, j, :], bank[(0, 1, 6, 7)[j]][:, :], ACT.Gelu,
                                   bias=fb1_c[:, j:j + 1]).then_inc(fh_ready, 1)

            pipeline(act, XCHUNKS, [(0, ffn_gelu)])

        @block.tensor
        def _(pe):
            def stage(i, b):
                c1 = i * 2 + (b + 1)
                pe.wait_ge(xn_ready, c1)
                if not is_first(i):
                    pe.wait_ge(xf_ready, i * 2 + (b - 1))
                for t in range(CT):
                    ins = pe.transpose(bank[b][:, t * P:(t + 1) * P], xn_st[b][:, t, :], ident)
                ins.then_inc(xt_ps, 1)
                pe.wait_ge(xf_ready, c1)
                if not is_first(i):
                    pe.wait_ge(sig_ready, i * 2 + (b - 1))
                for t in range(CT):
                    ins = pe.matmul(bank[2 + b][:, t * E:(t + 1) * E], xf_st[b][:, t * P:(t + 1) * P], gate_sb,
                                    start=True, stop=True)
                ins.then_inc(logits_ps, 1)

            pe.wait_ge(const_in, 16 * NCONST)
            for b in range(2):
                stage(0, b)
            with pe.Fori(1, XCHUNKS // 2) as i:
                for b in range(2):
                    stage(i, b)

            def conv(b):
                r = b % 2
                pe.wait_ge(x4_in[r], 16 * NX4 * (b // 2 + 1))
                for g in range(CG):
                    for hf in range(2):
                        n = (b * CG + g) * 2 + hf
                        if n >= 2:
                            pe.wait_ge(c1_done, n - 1)
                        pe.matmul(bank[hf][:, :], w1a[:, g, :], x4[:, r, g, hf * HALF:(hf + 1) * HALF], start=True, stop=False)
                        pe.matmul(bank[hf][:, :], w1b[:, g, :], x4[:, r, g, hf * HALF + 1:(hf + 1) * HALF + 1],
                                  start=False, stop=True).then_inc(c1_ps, 1)
                pe.wait_ge(c1_done, 2 * CG * (b + 1))
                for hf in range(2):
                    if b:
                        pe.wait_ge(c2_done, 2 * b - 1 + hf)
                    for k in range(TAPS):
                        for g in range(CG):
                            ins = pe.matmul(bank[2 + hf][CW * g:CW * (g + 1), :], w2c[:, g * TAPS + k, :],
                                            h1[:, g, hf * HALF + k:(hf + 1) * HALF + k], start=(k == 0), stop=(k == TAPS - 1))
                    ins.then_inc(c2_ps, 1)

            pe.wait_ge(convw_ready, 1)
            pe.wait_ge(xf_ready, XCHUNKS)
            pe.wait_ge(sig_ready, XCHUNKS)
            for b in range(B - 1):
                conv(b)
            pe.wait_ge(pick_ready, 1)
            for k in range(4):
                ins = pe.matmul(bank[4 + k][:, :], ones_bf, picked[:, k * 512:(k + 1) * 512], start=True, stop=True)
            ins.then_inc(count_ps, 1)
            pe.wait_ge(base_ready, 1)
            for k in range(4):
                ins = pe.matmul(bank[4 + k][:, :], utri, picked[:, k * 512:(k + 1) * 512], start=True, stop=True)
            ins.then_inc(rank_ps, 1)
            conv(B - 1)

            def turn(dst, s, sm):
                for t in range(CT):
                    ins = pe.transpose(dst[:, t * P:(t + 1) * P], h_fm[:, s + t * P:s + (t + 1) * P], ident)
                ins.then_inc(sm, 1)

            def back(n, hf):
                if hf == 0:
                    pe.wait_ge(xh_ready, n + 1)
                if n or hf:
                    pe.wait_ge(back_done, 2 * n + hf)
                for t in range(CT):
                    ins = pe.transpose(bank[7][:, t * P:(t + 1) * P], xh[:, hf * CT + t, :], ident)
                ins.then_inc(back_ps, 1)

            pe.wait_ge(rank_read, 1)
            for b in range(B + 1):
                if b < B:
                    for hf in range(2):
                        pe.wait_ge(c2_done, 2 * b + hf + 1)
                        if b:
                            pe.wait_ge(res_read, 2 * b - 1 + hf)
                        turn(bank[5 + hf], b * N + hf * HALF, res_ps)
                if b:
                    back(b - 1, 0)
                    back(b - 1, 1)

            def project(n):
                l, b = n // B, n % B
                pe.wait_ge(h_ready, n + 1)
                for k, (m, first) in enumerate(((1, 0), (1, 1), (0, 0), (0, 1))):
                    hf = first
                    if k < 2:
                        if n:
                            pe.wait_ge(kr_ready, 2 * n - 1 + hf)
                    else:
                        pe.wait_ge(qk_done, 4 * n + hf + 1)
                    pe.matmul(bank[hf][:, :], wqkv[:, l, m, :], h_fm[:, b * N + hf * HALF:b * N + (hf + 1) * HALF],
                              start=True, stop=True).then_inc(qk_ps, 1)
                for hf in range(2):
                    pe.wait_ge(res_read, 2 * (B + n) - 3 + hf)
                    for t in range(CT):
                        s = b * N + hf * HALF + t * P
                        ins = pe.matmul(bank[2 + hf][:, t * P:(t + 1) * P], h_fm[:, s:s + P], wqkv[:, l, 2, :],
                                        start=True, stop=True)
                    ins.then_inc(v_ps, 1)

            def sums(n, ones):
                r = n % 2
                pe.wait_ge(kr_ready, 2 * n + 2)
                pe.wait_ge(v_done, 2 * n + 2 + ones)
                if n:
                    pe.wait_ge(kvb_ready, n)
                for t in range(BT):
                    pe.matmul(bank[4][:, 0:H + 2], kr[:, t * P:(t + 1) * P], vv[r][:, t, :], start=(t == 0), stop=(t == BT - 1))
                pe.wait_ge(kb_ready, n + 1)
                pe.wait_ge(q_ready, n + 1)
                for t in range(BT):
                    ins = pe.matmul(bank[4][:, 384 + t * HEADS:384 + (t + 1) * HEADS], qp[r][:, t * P:(t + 1) * P],
                                    kb[:, r, :], start=True, stop=True)
                ins.then_inc(kvden_ps, 1)

            def keys(n):
                for hf in range(2):
                    pe.wait_ge(qk_done, 4 * n + 3 + hf)
                    for t in range(CT):
                        s = hf * HALF + t * P
                        ins = pe.transpose(bank[hf][:, t * P:(t + 1) * P], kf[:, s:s + P], ident)
                    ins.then_inc(kt_ps, 1)

            def attend(n):
                b, r = n % B, n % 2
                pe.wait_ge(kva_ready, n + 1)
                pe.wait_ge(den_read, n + 1)
                pe.matmul(bank[4][:, 256:384], c["rot"], kva[:, :], start=True, stop=True).then_inc(kvb_ps, 1)
                for hf in range(2):
                    pe.wait_ge(v_done, v_needed(n) + hf)
                    turn(bank[2 + hf], b * N + hf * HALF, res_ps)
                pe.wait_ge(kvb_ready, n + 1)
                for hf in range(2):
                    if n:
                        pe.wait_ge(out_read, 2 * n - 1 + hf)
                    for t in range(CT):
                        s = hf * HALF + t * P
                        o = bank[5 + hf][:, t * P:(t + 1) * P]
                        pe.matmul(o, qc[r][:, s:s + P], kva[:, :], start=True, stop=False)
                        ins = pe.matmul(o, qs[r][:, s:s + P], kvb[:, :], start=False, stop=True)
                    ins.then_inc(out_ps, 1)

            def v_needed(n):
                n1 = HALFWAY if n < HALFWAY else STEPS
                ones = 1 if n < HALFWAY else 2
                last = min(n + 1, n1 - 1)
                return ones + 2 * last + 1

            def attention(n0, n1, ones):
                for n in range(n0, n1 + 2):
                    if n < n1:
                        project(n)
                    if n > n0 + 1:
                        back(B + n - 2, 0)
                    if n0 < n <= n1:
                        sums(n - 1, ones)
                    if n > n0 + 1:
                        back(B + n - 2, 1)
                    if n < n1:
                        keys(n)
                    if n0 < n <= n1:
                        attend(n - 1)

            def shared_up(i, b):
                if not is_first(i):
                    pe.wait_ge(shh_ready, i * 2 + (b - 1))
                h = xn_fm[:, bass.ds(i * 2 * HALF + b * HALF, HALF)]
                pe.matmul(bank[b][:, :], swg, h, start=True, stop=True)
                pe.matmul(bank[2 + b][:, :], swu, h, start=True, stop=True).then_inc(shg_ps, 1)

            def shared_down(i, b):
                pe.wait_ge(shh_ready, i * 2 + (b + 1))
                if not is_first(i):
                    pe.wait_ge(shd_read, i * 2 + (b - 1))
                for t in range(CT):
                    o = bank[4 + b][:, t * P:(t + 1) * P]
                    pe.matmul(o, shh[b][:, t * P:(t + 1) * P], swd, start=True, stop=False)
                    ins = pe.matmul(o, ones_r[:, :], ln2b_r[:, :], start=False, stop=True)
                ins.then_inc(shd_ps, 1)

            pe.wait_ge(shared_in, 48)
            pe.wait_ge(param_in, 16 * NPARAM)
            pipeline(pe, XCHUNKS, [(0, shared_up), (-1, shared_down)])
            phase_end(pe, 1)

            pe.wait_ge(attn_in, 32)
            attention(0, HALFWAY, 1)
            phase_end(pe, 2)

            regs = [pe.alloc_register(f"expert{t}") for t in range(CT)]

            def experts_of(i, b):
                pe.load(regs, te_row[0:1, bass.ds(i * 2 * CT + b * CT, CT)])
                return [pe.snap(r, min_val=0, max_val=E - 1) for r in regs]

            def rows_T(i, b):
                pe.wait_ge(rows_in[b], i * 16 + 16)
                if not is_first(i):
                    pe.wait_ge(rowsT_ready, i * 2 + (b - 1))
                for t in range(CT):
                    ins = pe.transpose(bank[b][:, t * P:(t + 1) * P], xg[b][:, t, :], ident)
                ins.then_inc(rowsT_ps, 1)

            def gate_up(i, b):
                ex = experts_of(i, b)
                pe.wait_ge(rowsT_ready, i * 2 + (b + 1))
                if not is_first(i):
                    pe.wait_ge(gated_ready, i * 2 + (b - 1))
                for t in range(CT):
                    ins = pe.matmul(bank[2 + b][:, t * P:(t + 1) * P], xT[b][:, t * P:(t + 1) * P],
                                    wgu_sb[:, bass.ds(ex[t], 1), :].rearrange("p a v -> p (a v)"), start=True, stop=True)
                ins.then_inc(gu_ps, 1)

            def gated_T(i, b):
                pe.wait_ge(gated_ready, i * 2 + (b + 1))
                if not is_first(i):
                    pe.wait_ge(gatedT_ready, i * 2 + (b - 1))
                for t in range(CT // 2):
                    ins = pe.transpose(bank[4 + b][:, t * P:(t + 1) * P],
                                       hh[b][:, 2 * t:2 * t + 2, :].rearrange("p c i -> p (c i)"), ident)
                ins.then_inc(gatedT_ps, 1)

            def down(i, b):
                ex = experts_of(i, b)
                pe.wait_ge(gatedT_ready, i * 2 + (b + 1))
                if not is_first(i):
                    pe.wait_ge(rows_ready, i * 2 + (b - 1))
                for t in range(CT):
                    ins = pe.matmul(bank[6 + b][:, t * P:(t + 1) * P], hT[b][:, t * P:(t + 1) * P],
                                    wed_sb[:, bass.ds(ex[t], 1), :].rearrange("p a v -> p (a v)"), start=True, stop=True)
                ins.then_inc(down_ps, 1)

            pe.wait_ge(experts_in, 32)
            pe.wait_ge(te_in, 16)
            pipeline(pe, CHUNKS, [(1, rows_T), (0, gate_up), (-1, gated_T), (-2, down)])
            phase_end(pe, 3)

            attention(HALFWAY, STEPS, 2)
            phase_end(pe, 4)

            def ffn_up(i, b):
                h = h_fm[:, bass.ds(i * 2 * HALF + b * HALF, HALF)]
                for j in range(MUL):
                    if not (is_first(i) and b == 0):
                        pe.wait_ge(fh_ready, i * (2 * MUL) + (b * MUL + j + 1 - MUL))
                    pe.matmul(bank[(0, 1, 6, 7)[j]][:, :], fw1[:, j * H:(j + 1) * H], h, start=True, stop=True).then_inc(f1_ps, 1)

            def ffn_down(i, b):
                pe.wait_ge(fh_ready, i * (2 * MUL) + (b * MUL + MUL))
                if not is_first(i):
                    pe.wait_ge(fy_ready, i * 2 + (b - 1))
                for j in range(MUL):
                    ins = pe.matmul(bank[2 + b][:, :], fw2[:, j * H:(j + 1) * H], fh[:, b, j, :], start=(j == 0), stop=(j == MUL - 1))
                ins.then_inc(f2_ps, 1)

            def ffn_T(i, b):
                pe.wait_ge(fy_ready, i * 2 + (b + 1))
                if not is_first(i):
                    pe.wait_ge(fy_read, i * 2 + (b - 1))
                for t in range(CT):
                    ins = pe.transpose(bank[4 + b][:, t * P:(t + 1) * P], fy[b][:, t * P:(t + 1) * P], ident)
                ins.then_inc(fy_ps, 1)

            pe.wait_ge(ffn_in, 32)
            pipeline(pe, XCHUNKS, [(0, ffn_up), (-1, ffn_down), (-2, ffn_T)])


def constants():
    at, n = const_table()
    table = np.zeros((P, n), np.float32)
    p = np.arange(P)
    values = {
        "ident": np.eye(P),
        "iota_e": np.broadcast_to(np.arange(E), (P, E)),
        "tri_g": np.broadcast_to(np.tril(np.ones((G, G)), -1).reshape(1, -1), (P, G * G)),
        "iota_j": 2 * p[:, None] + np.arange(2),
        "dmask": p[:, None] % CW == np.arange(CW),
        "dmask3": (p[:, None] % CW == np.arange(CW)) & (p[:, None] >= 3 * CW),
        "dmask2": p[:, None] // MUL == np.arange(CW),
        "bdmask": (p[:, None] // HD == p // HD) / N,
        "hmask": p[:, None] // HD == np.arange(HEADS),
        "utri": np.triu(np.ones((P, P)), 1),
        "rot": np.where((p[:, None] == p + 1) & (p % 2 == 0), 1.0, np.where((p[:, None] == p - 1) & (p % 2 == 1), -1.0, 0.0)),
    }
    for name, (lo, width) in at.items():
        table[:, lo:lo + width] = values[name]
    inv = 1.0 / 10000.0 ** (np.arange(0, H, 2, dtype=np.float32) / H)
    ang = np.repeat(np.arange(N, dtype=np.float32)[:, None] * inv.astype(np.float32)[None], 2, axis=-1).astype(np.float32)
    cos, sin = np.cos(ang), np.sin(ang)
    sign = np.where(np.arange(H) % 2 == 0, -1.0, 1.0).astype(np.float32)
    tm = lambda v: v.reshape(BT, P, H).transpose(1, 0, 2).reshape(P, N)
    rope = np.concatenate([tm(cos), tm(sin * sign), cos.T, sin.T], axis=1).astype(np.float32)
    return table, rope


def kernel(**inputs):
    import concourse.bacc as _bacc
    from concourse.bass_utils import run_bass_kernel_spmd as _run

    nc = _bacc.Bacc("TRN2", target_bir_lowering=False, num_devices=1)
    f = {k.replace("L0_attn_", "").replace("L0_", ""): np.asarray(v) for k, v in inputs.items()}
    table, rope = constants()
    w1 = f["conv1_w"].reshape(CG, CW, MUL, TAPS)
    w2 = f["conv2_w"].reshape(CG, CW, MUL, TAPS)
    w1_taps = w1.transpose(3, 1, 0, 2)[:4].reshape(P, CG * MUL)
    w1_last = np.tile(w1[..., 4].transpose(1, 0, 2).reshape(CW, CG * MUL), (4, 1))
    w2_rows = w2.transpose(1, 2, 0, 3).reshape(P, CG * TAPS)
    arrays = {
        "x": f["x"], "consts": table, "rope": rope, "gate_w": f["ffn_gate_w"].T, "gate_bias": f["ffn_gate_bias"],
        "conv_w": np.concatenate([w1_taps, w1_last, w2_rows], axis=1),
        "cols": np.concatenate([f["bq"].T, f["bk"].T, f["lnA_g"].T, f["lnA_b"].T, f["ln0_g"][:, None], f["ln0_b"][:, None],
                                f["conv2_b"][:, None], f["b2"][:, None], f["conv1_b"].reshape(CG, P).T,
                                f["b1"].reshape(MUL, P).T], axis=1),
        "wqkv": np.stack([f["Wq"], f["Wk"], f["Wv"]], axis=1).transpose(2, 0, 1, 3),
        "bv": f["bv"], "ln2_g": f["ln2_g"], "ln2_b": f["ln2_b"], "w1": f["W1"], "w2": f["W2"],
        "wgu": np.concatenate([f["ffn_eg_w"], f["ffn_eu_w"]], axis=1).transpose(2, 0, 1),
        "wed": f["ffn_ed_w"].transpose(2, 0, 1),
        "sg": f["ffn_sg_w"].T, "su": f["ffn_su_w"].T, "sd": f["ffn_sd_w"].T,
    }
    arrays = {f"in_{k}": np.ascontiguousarray(v) for k, v in arrays.items()}
    aps = {k[3:]: nc.dram_tensor(k, v.shape, mybir.dt.from_np(v.dtype), kind="ExternalInput").ap() for k, v in arrays.items()}
    out = nc.dram_tensor("out_0", (B, N, H), F32, kind="ExternalOutput").ap()
    block_kernel(nc, aps, out)
    r = _run(nc, [arrays], core_ids=[0])
    return r.results[0]["out_0"]
```

```python
from contextlib import ExitStack

import numpy as np
import concourse.bass as bass
from concourse import mybir

F32 = mybir.dt.float32
BF16 = mybir.dt.bfloat16
I32 = mybir.dt.int32
U32 = mybir.dt.uint32
ALU = mybir.AluOpType
ACT = mybir.ActivationFunctionType
AX = mybir.AxisListType

P = 128
B, N, H = 4, 1024, 128
T = B * N
TILES = T // P
BT = N // P
HALF = 512
CT = HALF // P
E, G, TG, K, I = 64, 8, 4, 6, 64
EG = E // G
SLOT_TILES = T * K // P + E
SLOTS = SLOT_TILES * P
CHUNKS = SLOT_TILES // CT
RB = 4
STORE_LAG = 3
XCHUNKS = T // HALF
LAYERS, HEADS = 4, 16
HD = H // HEADS
CG, CW, TAPS, MUL = 4, 32, 5, 4
X4W = N + 2
H1W = N + TAPS - 1
SHIFT = 0.21
EPS_X, EPS_LN, EPS_Z, EPS_W = 1e-5, 1e-12, 1e-6, 1e-8
STEPS = LAYERS * B
HALFWAY = STEPS // 2
GPARTS = ((0, 26), (26, 32))


def const_table():
    at, n = {}, 0
    for name, width in (("ident", P), ("iota_e", E), ("tri_g", G * G), ("iota_j", 2), ("dmask", CW), ("dmask3", CW),
                        ("dmask2", CW), ("bdmask", P), ("hmean", HEADS), ("hshift", HEADS), ("eps_z", 1), ("rot", P), ("utri", P)):
        at[name] = (n, width)
        n += width
    return at, n


def block_kernel(nc, a, out):
    consts_at, consts_n = const_table()
    with ExitStack() as ctx:
        def sb(name, shape, dt=F32):
            return ctx.enter_context(nc.sbuf_tensor(name, shape, dt))

        def sem(name):
            return ctx.enter_context(nc.semaphore(name))

        def carve(region, sizes):
            at, views = 0, []
            for size in sizes:
                views.append(region[:, at:at + size])
                at += size
            assert at <= region.shape[1], (at, region.shape)
            return views

        xs = nc.dram_tensor("rows_in", [SLOTS, H], F32).ap()
        ys = nc.dram_tensor("rows_out", [SLOTS, H], F32).ap()
        te_dram = nc.dram_tensor("tile_expert", [P, 2], I32).ap()

        x_tm = sb("x_tm", [P, TILES, H])
        xn_tm = sb("xn_tm", [P, TILES, H])
        xn_fm = sb("xn_fm", [P, T])
        h_fm = sb("h_fm", [P, T])
        cst = sb("cst", [P, consts_n])
        c = {name: cst[:, at:at + width] for name, (at, width) in consts_at.items()}
        ident = c["ident"]
        cols = sb("cols", [P, 4 * LAYERS + 2 + 1 + 1 + 2 * MUL])
        wk = sb("wk", [P, TILES, K])
        addr = sb("addr", [P, TILES * K], I32)
        te_row = sb("te_row", [1, 2 * P], I32)
        ln2g_b = sb("ln2g_b", [P, H])
        ln2b_r = sb("ln2b_r", [1, H])
        ones_r = sb("ones_r", [1, P])
        nw_a = sb("nw_a", [P, BT])
        nw_t = sb("nw_t", [P, BT])
        nmr = sb("nmr", [P, BT])
        rstd = sb("rstd", [P, BT])
        stats = sb("stats", [P, BT, 6])
        mv = sb("mv", [P, BT, 2])
        bq_c, bk_c, gA_c, bA_c = (cols[:, k * LAYERS:(k + 1) * LAYERS] for k in range(4))
        k0 = 4 * LAYERS
        ln0g_c, ln0b_c, cb2_c, fb2_c = (cols[:, k0 + k:k0 + k + 1] for k in range(4))
        cb1_c, fb1_c = cols[:, k0 + 4:k0 + 8], cols[:, k0 + 8:k0 + 12]

        arena = sb("arena", [P, 2 * E * H])
        u = sb("u", [P, 14144])
        w = sb("w", [P, CG * H1W])

        x4_r, w1a_r, w1b_r, w2c_r, tmp, zeros = carve(arena, [2 * CG * X4W, CG * P, CG * P, CG * TAPS * CW, 4096, 2048])
        onehot_r, scores, base_r, utri_r, ones_r_, picked_r, gate_sb, gbias, gs, grank, top8_r, idx8_r, idxf_r, slot, \
            slot_i, t1, t2, scan0, scan1, ntile, cnt_i, te_f, te_i, wsum = carve(u, [
                TILES * K * E // 2, TILES * E, (TILES + 1) * E, P // 2, P // 2, TILES * E // 2, E, E, TILES * G,
                TILES * G, TILES * 8, TILES * 8, TILES * K, TILES * K, TILES * K, TILES * K, TILES * K, E, E, E, E,
                2, 2, TILES])
        onehot = onehot_r.bitcast(BF16).rearrange("p (q e) -> p q e", e=E)
        picked = picked_r.bitcast(BF16)
        utri = utri_r.bitcast(BF16)
        ones_bf = ones_r_.bitcast(BF16)
        base = base_r.rearrange("p (t e) -> p t e", e=E)
        top8 = top8_r.rearrange("p (t k) -> p t k", k=8)
        idx8 = idx8_r.bitcast(U32).rearrange("p (t k) -> p t k", k=8)
        idxf = idxf_r.rearrange("p (t k) -> p t k", k=K)
        slot_i, t1, t2, cnt_i, te_i = (v.bitcast(I32) for v in (slot_i, t1, t2, cnt_i, te_i))
        scan = [scan0, scan1]
        st0, st1, xf0, xf1 = carve(w, [HALF] * 4)
        xn_st = [v.rearrange("p (t f) -> p t f", f=H) for v in (st0, st1)]
        xf_st = [xf0, xf1]
        x4 = x4_r.rearrange("p (r g m) -> p r g m", r=2, g=CG)
        w1a, w1b = (v.rearrange("p (g m) -> p g m", g=CG) for v in (w1a_r, w1b_r))
        w2c = w2c_r.rearrange("p (g m) -> p g m", m=CW)
        h1 = w[:, :].rearrange("p (g m) -> p g m", g=CG)
        cwv = sb("cwv", [P, 2 * CG * MUL + CG * TAPS])
        w1v, w1v4, w2v = carve(cwv, [CG * MUL, CG * MUL, CG * TAPS])
        cos_tm, sin_tm, cos_fm, sin_fm = carve(xn_fm, [N] * 4)
        wqkv_r, bv_r, kva, kvb, kvm, z, den, shift_m = carve(w, [LAYERS * 3 * H, LAYERS * H, P, P, P, BT * HEADS,
                                                            BT * HEADS, P])
        wqkv = wqkv_r.rearrange("p (l m f) -> p l m f", l=LAYERS, m=3)
        bv_b = bv_r.rearrange("p (l f) -> p l f", l=LAYERS)
        q0_, q1_, qc0, qc1, qs0, qs1, kf, kc, ks, v0, v1, xo_r, xh_r = carve(
            u, [N] * 9 + [BT * (H + 2)] * 2 + [N] * 2)
        qp, qc, qs = [q0_, q1_], [qc0, qc1], [qs0, qs1]
        vv = [v.rearrange("p (t f) -> p t f", f=H + 2) for v in (v0, v1)]
        xo = xo_r.rearrange("p (t f) -> p t f", f=H)
        xh = xh_r.rearrange("p (t f) -> p t f", f=H)
        kacc = sb("kacc", [P, 2, 2])
        kbt = sb("kbt", [P, HEADS])
        kb = sb("kb", [P, 2, HEADS])
        ksum = sb("ksum", [P, 2])
        wgu_sb = arena[:, 0:E * H].rearrange("p (e v) -> p e v", e=E)
        wed_sb = arena[0:I, E * H:2 * E * H].rearrange("p (e v) -> p e v", e=E)
        xg0, xg1, xg2, xg3, yo0, yo1, yo2, yo3, xT0, xT1, hT0, hT1, sg0, sg1, hh0, hh1 = carve(
            u, [HALF] * 12 + [CT * I] * 4)
        xg = [v.rearrange("p (t f) -> p t f", f=H) for v in (xg0, xg1, xg2, xg3)]
        xT = [xT0, xT1]
        sg = [v.rearrange("p (t f) -> p t f", f=I) for v in (sg0, sg1)]
        hh = [v.rearrange("p (t f) -> p t f", f=I) for v in (hh0, hh1)]
        hT = [hT0[0:I, :], hT1[0:I, :]]
        yo = [yo0, yo1, yo2, yo3]
        yg_a = arena[:, :].rearrange("p (q f) -> p q f", f=H)
        swg, swu, swd, shs0, shs1, shh0, shh1 = carve(u, [P, P, P] + [HALF] * 4)
        shs, shh = [shs0, shs1], [shh0, shh1]
        fw1, fw2, fh_r, fy0, fy1, ft0, ft1 = carve(u, [4 * H, 4 * H, 8 * HALF] + [HALF] * 4)
        fh = fh_r.rearrange("p (b j m) -> p b j m", b=2, j=MUL)
        fy, ft = [fy0, fy1], [v.rearrange("p (t f) -> p t f", f=H) for v in (ft0, ft1)]

        bank = [ctx.enter_context(nc.psum_tensor(f"bank{k}", [P, HALF], F32)) for k in range(8)]

        x_in = [sem(f"x_in{q}") for q in range(4)]
        const_in = sem("const_in")
        param_in = sem("param_in")
        attn_in = sem("attn_in")
        tables_in = sem("tables_in")
        experts_in = sem("experts_in")
        shared_in = sem("shared_in")
        ffn_in = sem("ffn_in")
        fills = sem("fills")
        rows_zero = sem("rows_zero")
        xn_ready = sem("xn_ready")
        xn_kept = sem("xn_kept")
        xt_ps = sem("xt_ps")
        xf_ready = sem("xf_ready")
        xf_kept = sem("xf_kept")
        logits_ps = sem("logits_ps")
        sig_ready = sem("sig_ready")
        pick_ready = sem("pick_ready")
        count_ps = sem("count_ps")
        base_ready = sem("base_ready")
        rank_ps = sem("rank_ps")
        rank_read = sem("rank_read")
        addr_ready = sem("addr_ready")
        te_ready = sem("te_ready")
        te_out = sem("te_out")
        te_in = sem("te_in")
        scattered = sem("scattered")
        convw_ready = sem("convw_ready")
        x4_in = [sem(f"x4_in{r}") for r in range(2)]
        c1_ps = sem("c1_ps")
        c1_done = sem("c1_done")
        c2_ps = sem("c2_ps")
        c2_done = sem("c2_done")
        res_ps = sem("res_ps")
        res_read = sem("res_read")
        stats_ready = sem("stats_ready")
        xh_ready = sem("xh_ready")
        back_ps = sem("back_ps")
        back_done = sem("back_done")
        h_ready = sem("h_ready")
        qk_ps = sem("qk_ps")
        qk_done = sem("qk_done")
        v_ps = sem("v_ps")
        v_done = sem("v_done")
        kb_ready = sem("kb_ready")
        shift_ready = sem("shift_ready")
        q_ready = sem("q_ready")
        kt_ps = sem("kt_ps")
        kr_ready = sem("kr_ready")
        kvden_ps = sem("kvden_ps")
        kva_ready = sem("kva_ready")
        den_ready = sem("den_ready")
        kvb_ps = sem("kvb_ps")
        kvb_ready = sem("kvb_ready")
        out_ps = sem("out_ps")
        out_read = sem("out_read")
        phase = sem("phase")
        shg_ps = sem("shg_ps")
        shs_ready = sem("shs_ready")
        shh_ready = sem("shh_ready")
        shd_ps = sem("shd_ps")
        shd_read = sem("shd_read")
        rows_in = [sem(f"rows_in{r}") for r in range(RB)]
        rowsT_ps = sem("rowsT_ps")
        rowsT_ready = sem("rowsT_ready")
        gu_ps = sem("gu_ps")
        silu_ready = sem("silu_ready")
        gated_ready = sem("gated_ready")
        gatedT_ps = sem("gatedT_ps")
        evenT_ready = sem("evenT_ready")
        oddT_ready = sem("oddT_ready")
        down_ps = sem("down_ps")
        rows_ready = sem("rows_ready")
        rows_out = [sem(f"rows_out{r}") for r in range(RB)]
        gathered = sem("gathered")
        part_done = sem("part_done")
        f1_ps = sem("f1_ps")
        fh_ready = sem("fh_ready")
        f2_ps = sem("f2_ps")
        fy_ready = sem("fy_ready")
        fy_ps = sem("fy_ps")
        fy_read = sem("fy_read")
        sum_ready = sem("sum_ready")
        out_sent = sem("out_sent")

        NFILL = SLOTS // (P * 16)
        NX4 = CG * 4
        NCONST = 4
        NPARAM = 3

        x_v = a["x"].rearrange("b (t p) f -> p (b t) f", p=P)
        out_v = out.rearrange("b (t p) f -> p (b t) f", p=P)
        xs_v = xs.rearrange("(c p r) f -> c p (r f)", p=P, r=CT)
        ys_v = ys.rearrange("(c p r) f -> c p (r f)", p=P, r=CT)
        fill_v = xs.rearrange("(z p r) f -> z p (r f)", p=P, r=16)

        def yg(t, k):
            q = t * K + k
            n = 2 * E
            return yg_a[:, q, :] if q < n else xn_tm[:, q - n, :]

        def is_first(i, s=0):
            return isinstance(i, int) and i == 0 and s < 2

        def pipeline(eng, count, stages, unit=2):
            def step(i, r):
                for off, stage in stages:
                    o = r + off
                    if isinstance(i, int) and not 0 <= unit * i + o < count:
                        continue
                    stage(i + o // unit, o % unit)

            first, last = -(-4 // unit), count // unit - 1
            for s in range(-1, first * unit):
                step(s // unit, s % unit)
            with eng.Fori(first, last) as i:
                for r in range(unit):
                    step(i, r)
            for s in range(last * unit, count + 2):
                step(s // unit, s % unit)

        def phase_end(eng, k):
            eng.drain().then_inc(phase, 1)
            eng.wait_ge(phase, 3 * k)

        block = ctx.enter_context(nc.Block())

        @block.sync
        def _(sp):
            n = TILES // 4
            for q in range(4):
                sp.dma_start(x_tm[:, q * n:(q + 1) * n, :], x_v[:, q * n:(q + 1) * n, :]).then_inc(x_in[q], 16)
                if q == 0:
                    sp.dma_start(cst[:, :], a["consts"]).then_inc(const_in, 16)
                    sp.dma_start(gate_sb, a["gate_w"]).then_inc(const_in, 16)
                    sp.dma_start(gbias, a["gate_bias"].rearrange("(a e) -> a e", a=1).broadcast_to([P, E])).then_inc(const_in, 16)
                    sp.dma_start(cwv[:, :], a["conv_w"]).then_inc(const_in, 16)
            sp.dma_start(cols[:, :], a["cols"]).then_inc(param_in, 16)
            sp.dma_start(ln2g_b[:, :], a["ln2_g"].rearrange("(a f) -> a f", a=1).broadcast_to([P, H])).then_inc(param_in, 16)
            sp.dma_start(ln2b_r[:, :], a["ln2_b"].rearrange("(a f) -> a f", a=1)).then_inc(param_in, 16)
            sp.wait_ge(fills, 1)
            for k in range(NFILL):
                sp.dma_start(fill_v[k], zeros).then_inc(rows_zero, 16)
            sp.wait_ge(te_ready, 1)
            sp.dma_start(te_dram[:, :], te_i).then_inc(te_out, 16)
            sp.wait_ge(te_out, 16)
            sp.dma_start(te_row[:, :], te_dram.rearrange("(o p) a -> o (p a)", o=1)).then_inc(te_in, 16)
            sp.wait_ge(c2_ps, 2 * B)
            sp.dma_start(wqkv, a["wqkv"]).then_inc(attn_in, 16)
            sp.dma_start(bv_r, a["bv"].rearrange("(a l) f -> a (l f)", a=1).broadcast_to([P, LAYERS * H])).then_inc(attn_in, 16)
            sp.wait_ge(addr_ready, 1)
            sp.dma_start(swg, a["sg"]).then_inc(shared_in, 16)
            sp.dma_start(swu, a["su"]).then_inc(shared_in, 16)
            sp.dma_start(swd, a["sd"]).then_inc(shared_in, 16)
            sp.wait_ge(rows_zero, 16 * NFILL)
            sp.dma_start(wgu_sb, a["wgu"]).then_inc(experts_in, 16)
            sp.dma_start(wed_sb, a["wed"]).then_inc(experts_in, 16)
            sp.wait_ge(phase, 3)
            sp.dma_start(xn_fm[:, :], a["rope"]).then_inc(tables_in, 16)

            def load_rows(i, r):
                if not (isinstance(i, int) and i == 0):
                    sp.wait_ge(rowsT_ps, i * RB + (r + 1 - RB))
                sp.dma_start(xg[r].rearrange("p r f -> p (r f)"), xs_v[bass.ds(i * RB + r, 1)]).then_inc(rows_in[r], 16)

            def store_rows(i, r):
                sp.wait_ge(rows_ready, i * RB + (r + 1))
                sp.dma_start(ys_v[bass.ds(i * RB + r, 1)], yo[r]).then_inc(rows_out[r], 16)

            sp.wait_ge(scattered, 16 * TILES * K)
            sp.wait_ge(phase, 6)
            for r in range(RB + STORE_LAG):
                load_rows(r // RB, r % RB)
            with sp.Fori(0, CHUNKS // RB - 2) as i:
                for r in range(RB):
                    load_rows(i + 1 + (r + STORE_LAG) // RB, (r + STORE_LAG) % RB)
                    store_rows(i, r)
            for j in range(CHUNKS - 2 * RB, CHUNKS):
                if j + RB + STORE_LAG < CHUNKS:
                    load_rows((j + RB + STORE_LAG) // RB, (j + STORE_LAG) % RB)
                store_rows(j // RB, j % RB)
            sp.wait_ge(phase, 12)
            sp.dma_start(fw1, a["w1"]).then_inc(ffn_in, 16)
            sp.dma_start(fw2.rearrange("p (j f) -> p j f", f=H), a["w2"].rearrange("(j p) f -> p j f", p=P)).then_inc(ffn_in, 16)
            for k, (lo, hi) in enumerate(GPARTS):
                sp.wait_ge(sum_ready, k + 1)
                sp.dma_start(out_v[:, lo:hi, :], x_tm[:, lo:hi, :]).then_inc(out_sent, 16)
            sp.wait_ge(out_sent, 16 * len(GPARTS))

        @block.gpsimd
        def _(pool):
            pool.memset(zeros, 0.0).then_inc(fills, 1)
            pool.memset(ones_bf, 1.0).then_inc(fills, 1)
            pool.memset(ones_r[:, :], 1.0).then_inc(fills, 1)
            x4_all = x4_r.rearrange("p (q m) -> p q m", m=X4W)
            pool.memset(x4_all[:, :, 0:2], 0.0).then_inc(fills, 1)
            pool.memset(x4_all[:, :, N - 2:X4W], 0.0).then_inc(fills, 1)

            def keep(i, b):
                c1 = i * 2 + (b + 1)
                pool.wait_ge(xn_ready, c1)
                pool.tensor_copy(xn_tm[:, bass.ds(i * 8 + b * CT, CT), :], xn_st[b]).then_inc(xn_kept, 1)
                pool.wait_ge(xf_ready, c1)
                pool.tensor_copy(xn_fm[:, bass.ds((i * 2 + b) * HALF, HALF)], xf_st[b]).then_inc(xf_kept, 1)

            for b in range(2):
                keep(0, b)
            with pool.Fori(1, XCHUNKS // 2) as i:
                for b in range(2):
                    keep(i, b)
            pool.wait_ge(xf_kept, XCHUNKS)
            pool.wait_ge(xn_kept, XCHUNKS)
            pool.wait_ge(logits_ps, XCHUNKS)
            pool.memset(h1[:, :, 0:2], 0.0).then_inc(fills, 1)
            pool.memset(h1[:, :, N + 2:], 0.0).then_inc(fills, 1)

            pool.wait_ge(addr_ready, 1)
            pool.wait_ge(rows_zero, 16 * NFILL)
            for t in range(TILES):
                for k in range(K):
                    q = t * K + k
                    pool.indirect_dma_start(xs[:, :], bass.IndirectOffsetOnAxis(addr[:, q:q + 1].bitcast(U32), 0),
                                            xn_tm[:, t, :], None).then_inc(scattered, 16)
            for r in range(RB):
                pool.wait_ge(rows_out[r], 16 * CHUNKS // RB)
            pool.wait_ge(phase, 9)
            for part, (lo, hi) in enumerate(GPARTS):
                if part:
                    pool.wait_ge(part_done, part)
                for t in range(lo, hi):
                    for k in range(K):
                        q = t * K + k
                        pool.indirect_dma_start(yg(t - lo, k), None, ys[:, :],
                                                bass.IndirectOffsetOnAxis(addr[:, q:q + 1].bitcast(U32), 0)).then_inc(gathered, 16)

        @block.vector
        def _(dve):
            def inv_sqrt(n, eps):
                y, var, s, t = rstd[:, 0:n], mv[:, 0:n, 1], nw_a[:, 0:n], nw_t[:, 0:n]
                dve.tensor_scalar(s, var, eps, None, ALU.add)
                dve.drain()
                dve.tensor_scalar(t.bitcast(I32), s.bitcast(I32), 1, None, ALU.logical_shift_right)
                dve.drain()
                dve.tensor_scalar(y.bitcast(I32), t.bitcast(I32), -1.0, float(0x5f3759df), ALU.mult, ALU.add)
                for _ in range(3):
                    dve.drain()
                    dve.scalar_tensor_tensor(t, y, -0.5, y, ALU.mult, ALU.mult)
                    dve.drain()
                    dve.tensor_tensor(t, t, s, ALU.mult)
                    dve.drain()
                    dve.scalar_tensor_tensor(y, t, 1.5, y, ALU.add, ALU.mult)

            def moments(n, tile, eps):
                for t in range(n):
                    dve.bn_stats(stats[:, t, :], tile(t))
                dve.drain()
                for t in range(n):
                    dve.bn_aggr(mv[:, t, :], stats[:, t, :])
                dve.drain()
                inv_sqrt(n, eps)
                dve.drain()

            def norm(i, b):
                def tile(t):
                    return x_tm[:, bass.ds(i * (2 * CT) + (b * CT + t), 1), :].rearrange("p a f -> p (a f)")

                moments(CT, tile, EPS_X)
                if not is_first(i):
                    dve.wait_ge(xt_ps, i * 2 + (b - 1))
                    dve.wait_ge(xn_kept, i * 2 + (b - 1))
                for t in range(CT):
                    ins = dve.tensor_scalar(xn_st[b][:, t, :], tile(t), mv[:, t, 0:1], rstd[:, t:t + 1],
                                            ALU.subtract, ALU.mult)
                ins.then_inc(xn_ready, 1)
                dve.drain()

            dve.wait_ge(x_in[0], 16)
            for b in range(2):
                norm(0, b)
            for q in range(1, 4):
                dve.wait_ge(x_in[q], 16)
            with dve.Fori(1, XCHUNKS // 2) as i:
                for b in range(2):
                    norm(i, b)

            dve.wait_ge(const_in, 16 * NCONST)
            for dst, mask, val in ((w1a, c["dmask"], w1v), (w1b, c["dmask3"], w1v4)):
                dve.tensor_tensor(dst.rearrange("p g (c j) -> p g c j", j=MUL),
                                  mask.unsqueeze(1).unsqueeze(3).broadcast_to([P, CG, CW, MUL]),
                                  val.rearrange("p (g j) -> p g j", j=MUL).unsqueeze(2).broadcast_to([P, CG, CW, MUL]), ALU.mult)
            dve.tensor_tensor(w2c, c["dmask2"].unsqueeze(1).broadcast_to([P, CG * TAPS, CW]),
                              w2v.unsqueeze(2).broadcast_to([P, CG * TAPS, CW]), ALU.mult)
            dve.tensor_copy(utri, c["utri"])
            dve.drain().then_inc(convw_ready, 1)

            dve.wait_ge(sig_ready, XCHUNKS)
            sc3 = scores.rearrange("p (t e) -> p t e", e=E)
            dve.tensor_tensor(sc3, sc3, gbias.unsqueeze(1).broadcast_to([P, TILES, E]), ALU.add)
            dve.drain()
            dve.tensor_reduce(gs, scores.rearrange("p (g e) -> p g e", e=EG), AX.X, ALU.max)
            dve.drain()
            g3 = gs.rearrange("p (t g) -> p t g", g=G)
            other = g3.unsqueeze(2).broadcast_to([P, TILES, G, G])
            own = g3.unsqueeze(3).broadcast_to([P, TILES, G, G])
            beats, ties = (v.rearrange("p (t g h) -> p t g h", g=G, h=G) for v in (tmp[:, 0:2048], tmp[:, 2048:4096]))
            tri = c["tri_g"].rearrange("p (g h) -> p g h", g=G).unsqueeze(1).broadcast_to([P, TILES, G, G])
            dve.tensor_tensor(ties, other, own, ALU.is_equal)
            dve.tensor_tensor(beats, other, own, ALU.is_gt)
            dve.drain()
            dve.tensor_tensor(ties, ties, tri, ALU.mult)
            dve.drain()
            dve.tensor_tensor(beats, beats, ties, ALU.add)
            dve.drain()
            dve.tensor_reduce(grank, tmp[:, 0:2048].rearrange("p (g h) -> p g h", h=G), AX.X, ALU.add)
            dve.drain()
            dve.tensor_scalar(grank, grank, TG - 0.5, None, ALU.is_lt)
            dve.drain()
            sce = scores.rearrange("p (g e) -> p g e", e=EG)
            dve.tensor_tensor(sce, sce, grank.unsqueeze(2).broadcast_to([P, TILES * G, EG]), ALU.mult)
            dve.drain()
            for t in range(TILES):
                dve.max(top8[:, t, :], sc3[:, t, :])
            dve.drain()
            for t in range(TILES):
                dve.max_index(idx8[:, t, :], top8[:, t, :], sc3[:, t, :])
            dve.tensor_reduce(wsum, top8[:, :, 0:K], AX.X, ALU.add)
            dve.drain()
            dve.tensor_copy(idxf, idx8[:, :, 0:K])
            dve.tensor_scalar(wsum, wsum, EPS_W, None, ALU.add)
            dve.drain()
            dve.reciprocal(wsum, wsum)
            dve.tensor_tensor(onehot, idxf_r.unsqueeze(2).broadcast_to([P, TILES * K, E]),
                              c["iota_e"].unsqueeze(1).broadcast_to([P, TILES * K, E]), ALU.is_equal)
            dve.drain()
            dve.tensor_tensor(wk[:, :, :], top8[:, :, 0:K], wsum.unsqueeze(2).broadcast_to([P, TILES, K]), ALU.mult)
            with nc.allow_low_precision("zeros and ones"):
                dve.tensor_reduce(picked.rearrange("p (t e) -> p t e", e=E),
                                  onehot.rearrange("p (t k) e -> p t e k", k=K), AX.X, ALU.add).then_inc(pick_ready, 1)
            dve.memset(base[:, 0, :], 0.0)
            dve.wait_ge(count_ps, 1)
            for t in range(TILES):
                dve.drain()
                dve.tensor_tensor(base[:, t + 1, :], base[:, t, :], bank[4 + t // 8][:, (t % 8) * E:(t % 8 + 1) * E], ALU.add)
            dve.drain().then_inc(base_ready, 1)
            dve.tensor_scalar(cnt_i, base[:, TILES, :], float(P - 1), None, ALU.add)
            dve.drain()
            dve.tensor_scalar(cnt_i, cnt_i, 7, None, ALU.logical_shift_right)
            dve.drain()
            dve.tensor_copy(scan[0], cnt_i)
            dve.tensor_copy(ntile, cnt_i)
            s = 0
            for d in (1, 2, 4, 8, 16, 32):
                dve.drain()
                dve.tensor_tensor(scan[1 - s][:, d:], scan[s][:, d:], scan[s][:, :E - d], ALU.add)
                dve.tensor_copy(scan[1 - s][:, :d], scan[s][:, :d])
                s = 1 - s
            dve.drain()
            incl = scan[s]
            tm = tmp[:, 0:2 * E].rearrange("p (a e) -> p a e", e=E)
            dve.tensor_tensor(tm, incl.unsqueeze(1).broadcast_to([P, 2, E]),
                              c["iota_j"].unsqueeze(2).broadcast_to([P, 2, E]), ALU.is_le)
            dve.tensor_tensor(ntile, incl, ntile, ALU.subtract)
            dve.drain()
            dve.tensor_reduce(te_f, tm, AX.X, ALU.add)
            dve.tensor_scalar(ntile, ntile, float(P), None, ALU.mult)
            dve.drain()
            dve.tensor_scalar(te_i, te_f, float(E - 1), None, ALU.min).then_inc(te_ready, 1)
            dve.tensor_tensor(base[:, 0:TILES, :], base[:, 0:TILES, :],
                              ntile.unsqueeze(1).broadcast_to([P, TILES, E]), ALU.add)
            dve.drain()
            dve.wait_ge(rank_ps, 1)
            for k in range(4):
                ins = dve.tensor_tensor(scores[:, k * 512:(k + 1) * 512], bank[4 + k][:, :],
                                        base[:, k * 8:(k + 1) * 8, :].rearrange("p t e -> p (t e)"), ALU.add)
            ins.then_inc(rank_read, 1)
            nt = 8
            for k in range(TILES // nt):
                dve.drain()
                dve.tensor_tensor(tmp[:, 0:nt * K * E].rearrange("p (t k e) -> p t k e", k=K, e=E),
                                  onehot[:, k * nt * K:(k + 1) * nt * K, :].rearrange("p (t k) e -> p t k e", k=K),
                                  sc3[:, k * nt:(k + 1) * nt, :].unsqueeze(2).broadcast_to([P, nt, K, E]), ALU.mult)
                dve.drain()
                dve.tensor_reduce(slot[:, k * nt * K:(k + 1) * nt * K],
                                  tmp[:, 0:nt * K * E].rearrange("p (q e) -> p q e", e=E), AX.X, ALU.add)
            dve.drain()
            dve.tensor_copy(slot_i, slot)
            dve.drain()
            dve.tensor_scalar(t1, slot_i, P - 1, 2, ALU.bitwise_and, ALU.logical_shift_left)
            dve.tensor_scalar(t2, slot_i, 7, CT - 1, ALU.logical_shift_right, ALU.bitwise_and)
            dve.tensor_scalar(addr[:, :], slot_i, 0x7fffffff ^ (HALF - 1), None, ALU.bitwise_and)
            dve.drain()
            dve.tensor_tensor(t1, t1, t2, ALU.bitwise_or)
            dve.drain()
            dve.tensor_tensor(addr[:, :], t1, addr[:, :], ALU.bitwise_or)
            dve.drain().then_inc(addr_ready, 1)

            def normalize(eps):
                moments(BT, lambda t: xo[:, t, :], eps)
                dve.scalar_tensor_tensor(nmr[:, :], mv[:, :, 0], -1.0, rstd[:, :], ALU.mult, ALU.mult)
                dve.drain().then_inc(stats_ready, 1)

            dve.wait_ge(te_out, 16)
            for b in range(B):
                if b:
                    dve.wait_ge(xh_ready, b)
                for hf in range(2):
                    dve.wait_ge(res_ps, 2 * b + hf + 1)
                    t0 = b * BT + hf * CT
                    dve.tensor_tensor(xo[:, hf * CT:(hf + 1) * CT, :].rearrange("p t f -> p (t f)"), bank[5 + hf][:, :],
                                      xn_tm[:, t0:t0 + CT, :].rearrange("p t f -> p (t f)"), ALU.add).then_inc(res_read, 1)
                dve.drain()
                normalize(EPS_LN)

            def key_mean(n):
                r = n % 2
                dve.wait_ge(qk_done, 4 * n + 2)
                dve.scalar_tensor_tensor(kbt[:, :], c["hmean"], kacc[:, r, 0:1], c["hshift"], ALU.mult, ALU.add)
                dve.drain()
                dve.scalar_tensor_tensor(kb[:, r, :], c["hmean"], kacc[:, r, 1:2], kbt[:, :], ALU.mult, ALU.add)
                dve.drain().then_inc(kb_ready, 1)

            def key_values(n):
                dve.wait_ge(kvden_ps, n + 1)
                dve.tensor_copy(ksum[:, :], bank[4][:, H:H + 2])
                dve.drain()
                dve.scalar_tensor_tensor(kvm, bv_b[:, n // B, :], ksum[:, 0:1], bank[4][:, 0:H], ALU.mult, ALU.add)
                dve.drain()
                dve.tensor_tensor(kva[:, :], kvm, c["bdmask"], ALU.mult).then_inc(kva_ready, 1)

            def queries(n):
                r = n % 2
                dve.wait_ge(qk_done, 4 * n + 4)
                dve.scalar_tensor_tensor(qc[r], qp[r], SHIFT, cos_fm, ALU.add, ALU.mult)
                dve.scalar_tensor_tensor(qs[r], qp[r], SHIFT, sin_fm, ALU.add, ALU.mult).then_inc(q_ready, 1)

            def keys(n):
                if n:
                    dve.wait_ge(kvden_ps, n)
                for hf in range(2):
                    dve.wait_ge(kt_ps, 2 * n + hf + 1)
                    s = slice(hf * HALF, (hf + 1) * HALF)
                    ev, od = slice(hf * HALF, (hf + 1) * HALF, 2), slice(hf * HALF + 1, (hf + 1) * HALF, 2)
                    dve.scalar_tensor_tensor(kc[:, s], bank[hf][:, :], SHIFT, cos_tm[:, s], ALU.add, ALU.mult)
                    dve.scalar_tensor_tensor(ks[:, ev], bank[hf][:, 1::2], SHIFT, sin_tm[:, ev], ALU.add, ALU.mult)
                    dve.scalar_tensor_tensor(ks[:, od], bank[hf][:, 0::2], SHIFT, sin_tm[:, od], ALU.add,
                                             ALU.mult).then_inc(kr_ready, 1)

            def attended(n):
                dve.wait_ge(den_ready, n + 1)
                dve.reciprocal(z, den)
                dve.drain()
                dve.wait_ge(xh_ready, B + n)
                for hf in range(2):
                    o = xo[:, hf * CT:(hf + 1) * CT, :].rearrange("p t (h d) -> p (t h) d", d=HD)
                    zz = z[:, hf * CT * HEADS:(hf + 1) * CT * HEADS].unsqueeze(2).broadcast_to([P, CT * HEADS, HD])
                    dve.wait_ge(out_ps, 2 * n + hf + 1)
                    dve.tensor_tensor(o, bank[5 + hf][:, :].rearrange("p (t d) -> p t d", d=HD), zz, ALU.mult).then_inc(out_read, 1)
                dve.drain()
                for hf in range(2):
                    o = xo[:, hf * CT:(hf + 1) * CT, :].rearrange("p t f -> p (t f)")
                    dve.wait_ge(res_ps, 2 * (B + n) + hf + 1)
                    dve.tensor_tensor(o, o, bank[2 + hf][:, :], ALU.add).then_inc(res_read, 1)
                dve.drain()
                normalize(EPS_LN)

            def attention(n0, n1):
                dve.memset(shift_m, SHIFT)
                dve.drain().then_inc(shift_ready, 1)
                for n in range(n0, n1 + 1):
                    if n > n0:
                        key_values(n - 1)
                    if n < n1:
                        key_mean(n)
                        if n == 0:
                            dve.wait_ge(tables_in, 16)
                        queries(n)
                        keys(n)
                    if n > n0:
                        attended(n - 1)

            def shared_gated(i, b):
                dve.wait_ge(shs_ready, i * 2 + (b + 1))
                if not is_first(i):
                    dve.wait_ge(shd_ps, i * 2 + (b - 1))
                dve.tensor_tensor(shh[b], shs[b], bank[2 + b][:, :], ALU.mult).then_inc(shh_ready, 1)

            def shared_sum(i, b):
                dve.wait_ge(shd_ps, i * 2 + (b + 1))
                dst = x_tm[:, bass.ds(i * 2 * CT + b * CT, CT), :].rearrange("p t f -> p (t f)")
                dve.tensor_tensor(dst, dst, bank[4 + b][:, :], ALU.add).then_inc(shd_read, 1)

            pipeline(dve, XCHUNKS, [(0, shared_gated), (-1, shared_sum)])
            phase_end(dve, 1)

            dve.wait_ge(attn_in, 32)
            attention(0, HALFWAY)
            phase_end(dve, 2)

            def gated(i, r):
                b = r % 2
                dve.wait_ge(silu_ready, i * RB + (r + 1))
                if not is_first(i, r):
                    dve.wait_ge(gatedT_ps, i * RB + (r - 1))
                g4 = bank[2 + b][:, :].rearrange("p (c v) -> p c v", v=2 * I)
                dve.tensor_tensor(hh[b], sg[b], g4[:, :, I:], ALU.mult).then_inc(gated_ready, 1)

            def even_columns(i, r):
                b = r % 2
                dve.wait_ge(gatedT_ps, i * RB + (r + 1))
                if not is_first(i, r):
                    dve.wait_ge(down_ps, i * RB + (r - 1))
                dve.tensor_copy(hT[b].rearrange("p (q a s) -> p q a s", a=2, s=P)[:, :, 0, :],
                                bank[4 + b][0:I, 0:2 * P].rearrange("p (q s) -> p q s", s=P)).then_inc(evenT_ready, 1)

            def expert_rows(i, r):
                b = r % 2
                dve.wait_ge(down_ps, i * RB + (r + 1))
                if not (isinstance(i, int) and i == 0):
                    dve.wait_ge(rows_out[r], i * 16)
                dve.tensor_copy(yo[r], bank[6 + b][:, :]).then_inc(rows_ready, 1)

            pipeline(dve, CHUNKS, [(0, gated), (-1, even_columns), (-2, expert_rows)], RB)
            phase_end(dve, 3)
            for r in range(RB):
                dve.wait_ge(rows_out[r], 16 * CHUNKS // RB)

            attention(HALFWAY, STEPS)
            phase_end(dve, 4)

            def ffn_residual(i, b):
                dve.wait_ge(f2_ps, i * 2 + (b + 1))
                if not is_first(i):
                    dve.wait_ge(fy_ps, i * 2 + (b - 1))
                dve.scalar_tensor_tensor(fy[b], bank[2 + b][:, :], fb2_c, h_fm[:, bass.ds(i * 2 * HALF + b * HALF, HALF)],
                                         ALU.add, ALU.add).then_inc(fy_ready, 1)

            def ffn_norm(i, b):
                dve.wait_ge(fy_ps, i * 2 + (b + 1))
                tile = lambda t: bank[4 + b][:, t * H:(t + 1) * H]
                moments(CT, tile, EPS_LN)
                for t in range(CT):
                    ins = dve.scalar_tensor_tensor(ft[b][:, t, :], tile(t), mv[:, t, 0:1], ln2g_b[:, :], ALU.subtract, ALU.mult)
                ins.then_inc(fy_read, 1)
                dve.drain()
                for t in range(CT):
                    dst = x_tm[:, bass.ds(i * 2 * CT + b * CT + t, 1), :].rearrange("p t f -> p (t f)")
                    dve.scalar_tensor_tensor(dst, ft[b][:, t, :], rstd[:, t:t + 1], dst, ALU.mult, ALU.add)
                dve.drain()

            pipeline(dve, XCHUNKS, [(-1, ffn_residual), (-2, ffn_norm)])

            done = 0
            for part, (lo, hi) in enumerate(GPARTS):
                done += (hi - lo) * K
                dve.wait_ge(gathered, 16 * done)
                for k in range(K):
                    for t in range(lo, hi):
                        dve.scalar_tensor_tensor(x_tm[:, t, :], yg(t - lo, k), wk[:, t, k:k + 1], x_tm[:, t, :], ALU.mult, ALU.add)
                    if k < K - 1:
                        dve.drain()
                dve.drain().then_inc(part_done, 1)
                dve.nop().then_inc(sum_ready, 1)

        @block.scalar
        def _(act):
            def stage(i, b):
                c1 = i * 2 + (b + 1)
                act.wait_ge(xt_ps, c1)
                if not is_first(i):
                    act.wait_ge(logits_ps, i * 2 + (b - 1))
                    act.wait_ge(xf_kept, i * 2 + (b - 1))
                act.activation(xf_st[b], bank[b][:, :], ACT.Copy).then_inc(xf_ready, 1)
                act.wait_ge(logits_ps, c1)
                act.activation(scores[:, bass.ds((i * 2 + b) * (CT * E), CT * E)], bank[2 + b][:, 0:CT * E],
                               ACT.Sigmoid).then_inc(sig_ready, 1)

            for b in range(2):
                stage(0, b)
            with act.Fori(1, XCHUNKS // 2) as i:
                for b in range(2):
                    stage(i, b)

            def load_x4(b):
                r = b % 2
                act.wait_ge(xf_kept, 2 * (b + 1))
                for g in range(CG):
                    for s in range(4):
                        lo, hi = max(0, 2 - s), min(X4W, N + 2 - s)
                        act.dma_start(x4[CW * s:CW * (s + 1), r, g, lo:hi],
                                      xn_fm[CW * g:CW * (g + 1), b * N + lo + s - 2:b * N + hi + s - 2]).then_inc(x4_in[r], 16)

            act.wait_ge(fills, 5)
            load_x4(0)
            load_x4(1)
            act.wait_ge(param_in, 16 * NPARAM)
            act.wait_ge(fills, 7)
            for b in range(B):
                for g in range(CG):
                    for hf in range(2):
                        n = (b * CG + g) * 2 + hf
                        act.wait_ge(c1_ps, n + 1)
                        if b and g == 0 and hf == 0:
                            act.wait_ge(c2_ps, 2 * b)
                        act.activation(h1[:, g, 2 + hf * HALF:2 + (hf + 1) * HALF], bank[hf][:, :], ACT.Gelu,
                                       bias=cb1_c[:, g:g + 1]).then_inc(c1_done, 1)
                if b + 2 < B:
                    load_x4(b + 2)
                for hf in range(2):
                    act.wait_ge(c2_ps, 2 * b + hf + 1)
                    act.activation(h_fm[:, b * N + hf * HALF:b * N + (hf + 1) * HALF], bank[2 + hf][:, :], ACT.Identity,
                                   bias=cb2_c).then_inc(c2_done, 1)

            def normalized(n):
                act.wait_ge(stats_ready, n + 1)
                if n:
                    act.wait_ge(back_ps, 2 * n)
                for t in range(BT):
                    ins = act.activation(xh[:, t, :], xo[:, t, :], ACT.Identity, bias=nmr[:, t:t + 1], scale=rstd[:, t:t + 1])
                ins.then_inc(xh_ready, 1)

            def feature_major(n, g, bias):
                for hf in range(2):
                    s = (n % B) * N + hf * HALF
                    act.wait_ge(back_ps, 2 * n + hf + 1)
                    act.activation(h_fm[:, s:s + HALF], bank[7][:, :], ACT.Identity, bias=bias, scale=g).then_inc(back_done, 1)
                act.drain().then_inc(h_ready, 1)

            for b in range(B):
                normalized(b)
                feature_major(b, ln0g_c, ln0b_c)

            def projected(n):
                l, r = n // B, n % 2
                if n:
                    act.wait_ge(kt_ps, 2 * n)
                if n >= 2:
                    act.wait_ge(kb_ready, n - 1)
                for hf in range(2):
                    act.wait_ge(qk_ps, 4 * n + hf + 1)
                    act.activation(kf[:, hf * HALF:(hf + 1) * HALF], bank[hf][:, :], ACT.Gelu, bias=bk_c[:, l:l + 1],
                                   accum_out=kacc[:, r, hf:hf + 1]).then_inc(qk_done, 1)
                if n >= 2:
                    act.wait_ge(out_ps, 2 * (n - 1))
                for hf in range(2):
                    act.wait_ge(qk_ps, 4 * n + 2 + hf + 1)
                    act.activation(qp[r][:, hf * HALF:(hf + 1) * HALF], bank[hf][:, :], ACT.Gelu,
                                   bias=bq_c[:, l:l + 1]).then_inc(qk_done, 1)
                for hf in range(2):
                    act.wait_ge(v_ps, 2 * n + hf + 1)
                    act.activation(vv[r][:, hf * CT:(hf + 1) * CT, 0:H],
                                   bank[2 + hf][:, :].rearrange("p (t f) -> p t f", f=H), ACT.Copy).then_inc(v_done, 1)

            def denominators(n):
                act.wait_ge(kva_ready, n + 1)
                if n:
                    act.wait_ge(out_read, 2 * n)
                act.activation(den, bank[4][:, 384:512], ACT.Identity, bias=c["eps_z"]).then_inc(den_ready, 1)

            def rotated(n):
                act.wait_ge(kvb_ps, n + 1)
                if n:
                    act.wait_ge(out_ps, 2 * n)
                act.activation(kvb[:, :], bank[4][:, 256:384], ACT.Copy).then_inc(kvb_ready, 1)

            def attention(n0, n1):
                for r in range(2):
                    act.activation(vv[r][:, :, H:H + 2], ident[:, 0:2 * BT].rearrange("p (t o) -> p t o", o=2),
                                   ACT.Identity, bias=1.0, scale=0.0)
                act.drain().then_inc(v_done, 1)
                for n in range(n0, n1 + 2):
                    if n < n1:
                        projected(n)
                    if n0 < n <= n1:
                        denominators(n - 1)
                        rotated(n - 1)
                    if n > n0 + 1:
                        m = n - 2
                        normalized(B + m)
                        feature_major(B + m, gA_c[:, m // B:m // B + 1], bA_c[:, m // B:m // B + 1])

            def shared_silu(i, b):
                act.wait_ge(shg_ps, i * 2 + (b + 1))
                if not is_first(i):
                    act.wait_ge(shh_ready, i * 2 + (b - 1))
                act.activation(shs[b], bank[b][:, :], ACT.Silu).then_inc(shs_ready, 1)

            pipeline(act, XCHUNKS, [(0, shared_silu)])
            phase_end(act, 1)

            attention(0, HALFWAY)
            phase_end(act, 2)

            def columns(i, r):
                b = r % 2
                act.wait_ge(rowsT_ps, i * RB + (r + 1))
                if not is_first(i, r):
                    act.wait_ge(gu_ps, i * RB + (r - 1))
                act.activation(xT[b], bank[b][:, :], ACT.Copy).then_inc(rowsT_ready, 1)

            def silu(i, r):
                b = r % 2
                act.wait_ge(gu_ps, i * RB + (r + 1))
                if not is_first(i, r):
                    act.wait_ge(gated_ready, i * RB + (r - 1))
                g4 = bank[2 + b][:, :].rearrange("p (c v) -> p c v", v=2 * I)
                act.activation(sg[b], g4[:, :, 0:I], ACT.Silu).then_inc(silu_ready, 1)

            def odd_columns(i, r):
                b = r % 2
                act.wait_ge(gatedT_ps, i * RB + (r + 1))
                if not is_first(i, r):
                    act.wait_ge(down_ps, i * RB + (r - 1))
                act.activation(hT[b].rearrange("p (q a s) -> p q a s", a=2, s=P)[:, :, 1, :],
                               bank[4 + b][I:P, 0:2 * P].rearrange("p (q s) -> p q s", s=P), ACT.Copy).then_inc(oddT_ready, 1)

            pipeline(act, CHUNKS, [(1, columns), (0, silu), (-1, odd_columns)], RB)
            phase_end(act, 3)
            for r in range(RB):
                act.wait_ge(rows_out[r], 16 * CHUNKS // RB)

            attention(HALFWAY, STEPS)
            phase_end(act, 4)

            def ffn_gelu(i, b):
                if not is_first(i):
                    act.wait_ge(f2_ps, i * 2 + (b - 1))
                for j in range(MUL):
                    act.wait_ge(f1_ps, i * (2 * MUL) + (b * MUL + j + 1))
                    act.activation(fh[:, b, j, :], bank[(0, 1, 6, 7)[j]][:, :], ACT.Gelu,
                                   bias=fb1_c[:, j:j + 1]).then_inc(fh_ready, 1)

            pipeline(act, XCHUNKS, [(0, ffn_gelu)])

        @block.tensor
        def _(pe):
            def stage(i, b):
                c1 = i * 2 + (b + 1)
                pe.wait_ge(xn_ready, c1)
                if not is_first(i):
                    pe.wait_ge(xf_ready, i * 2 + (b - 1))
                for t in range(CT):
                    ins = pe.transpose(bank[b][:, t * P:(t + 1) * P], xn_st[b][:, t, :], ident)
                ins.then_inc(xt_ps, 1)
                pe.wait_ge(xf_ready, c1)
                if not is_first(i):
                    pe.wait_ge(sig_ready, i * 2 + (b - 1))
                for t in range(CT):
                    ins = pe.matmul(bank[2 + b][:, t * E:(t + 1) * E], xf_st[b][:, t * P:(t + 1) * P], gate_sb,
                                    start=True, stop=True)
                ins.then_inc(logits_ps, 1)

            pe.wait_ge(const_in, 16 * NCONST)
            for b in range(2):
                stage(0, b)
            with pe.Fori(1, XCHUNKS // 2) as i:
                for b in range(2):
                    stage(i, b)

            def conv(b):
                r = b % 2
                pe.wait_ge(x4_in[r], 16 * NX4 * (b // 2 + 1))
                for g in range(CG):
                    for hf in range(2):
                        n = (b * CG + g) * 2 + hf
                        if n >= 2:
                            pe.wait_ge(c1_done, n - 1)
                        pe.matmul(bank[hf][:, :], w1a[:, g, :], x4[:, r, g, hf * HALF:(hf + 1) * HALF], start=True, stop=False)
                        pe.matmul(bank[hf][:, :], w1b[:, g, :], x4[:, r, g, hf * HALF + 1:(hf + 1) * HALF + 1],
                                  start=False, stop=True).then_inc(c1_ps, 1)
                pe.wait_ge(c1_done, 2 * CG * (b + 1))
                for hf in range(2):
                    if b:
                        pe.wait_ge(c2_done, 2 * b - 1 + hf)
                    for k in range(TAPS):
                        for g in range(CG):
                            ins = pe.matmul(bank[2 + hf][CW * g:CW * (g + 1), :], w2c[:, g * TAPS + k, :],
                                            h1[:, g, hf * HALF + k:(hf + 1) * HALF + k], start=(k == 0), stop=(k == TAPS - 1))
                    ins.then_inc(c2_ps, 1)

            pe.wait_ge(convw_ready, 1)
            pe.wait_ge(xf_ready, XCHUNKS)
            pe.wait_ge(sig_ready, XCHUNKS)
            for b in range(B - 1):
                conv(b)
            pe.wait_ge(pick_ready, 1)
            for k in range(4):
                ins = pe.matmul(bank[4 + k][:, :], ones_bf, picked[:, k * 512:(k + 1) * 512], start=True, stop=True)
            ins.then_inc(count_ps, 1)
            pe.wait_ge(base_ready, 1)
            for k in range(4):
                ins = pe.matmul(bank[4 + k][:, :], utri, picked[:, k * 512:(k + 1) * 512], start=True, stop=True)
            ins.then_inc(rank_ps, 1)
            conv(B - 1)

            def turn(dst, s, sm):
                for t in range(CT):
                    ins = pe.transpose(dst[:, t * P:(t + 1) * P], h_fm[:, s + t * P:s + (t + 1) * P], ident)
                ins.then_inc(sm, 1)

            def back(n, hf):
                if hf == 0:
                    pe.wait_ge(xh_ready, n + 1)
                if n or hf:
                    pe.wait_ge(back_done, 2 * n + hf)
                for t in range(CT):
                    ins = pe.transpose(bank[7][:, t * P:(t + 1) * P], xh[:, hf * CT + t, :], ident)
                ins.then_inc(back_ps, 1)

            pe.wait_ge(rank_read, 1)
            for b in range(B + 1):
                if b < B:
                    for hf in range(2):
                        pe.wait_ge(c2_done, 2 * b + hf + 1)
                        if b:
                            pe.wait_ge(res_read, 2 * b - 1 + hf)
                        turn(bank[5 + hf], b * N + hf * HALF, res_ps)
                if b:
                    back(b - 1, 0)
                    back(b - 1, 1)

            def project(n):
                l, b = n // B, n % B
                pe.wait_ge(h_ready, n + 1)
                for k, (m, first) in enumerate(((1, 0), (1, 1), (0, 0), (0, 1))):
                    hf = first
                    if k < 2:
                        if n:
                            pe.wait_ge(kr_ready, 2 * n - 1 + hf)
                    else:
                        pe.wait_ge(qk_done, 4 * n + hf + 1)
                    pe.matmul(bank[hf][:, :], wqkv[:, l, m, :], h_fm[:, b * N + hf * HALF:b * N + (hf + 1) * HALF],
                              start=True, stop=True).then_inc(qk_ps, 1)
                for hf in range(2):
                    pe.wait_ge(res_read, 2 * (B + n) - 3 + hf)
                    for t in range(CT):
                        s = b * N + hf * HALF + t * P
                        ins = pe.matmul(bank[2 + hf][:, t * P:(t + 1) * P], h_fm[:, s:s + P], wqkv[:, l, 2, :],
                                        start=True, stop=True)
                    ins.then_inc(v_ps, 1)

            def sums(n, ones):
                r = n % 2
                pe.wait_ge(kr_ready, 2 * n + 2)
                pe.wait_ge(v_done, 2 * n + 2 + ones)
                if n:
                    pe.wait_ge(kvb_ready, n)
                    pe.wait_ge(kva_ready, n)
                    pe.wait_ge(den_ready, n)
                for t in range(BT):
                    for k, part in enumerate((kc, ks)):
                        pe.matmul(bank[4][:, 0:H + 2], part[:, t * P:(t + 1) * P], vv[r][:, t, :],
                                  start=(t == 0 and k == 0), stop=(t == BT - 1 and k == 1))
                pe.wait_ge(kb_ready, n + 1)
                pe.wait_ge(q_ready, n + 1)
                pe.matmul(bank[4][:, 384:512].rearrange("p (t h) -> p t h", h=HEADS), shift_m,
                          kb[:, r, :].unsqueeze(1).broadcast_to([P, BT, HEADS]), start=True, stop=False)
                for t in range(BT):
                    ins = pe.matmul(bank[4][:, 384 + t * HEADS:384 + (t + 1) * HEADS], qp[r][:, t * P:(t + 1) * P],
                                    kb[:, r, :], start=False, stop=(t == BT - 1))
                ins.then_inc(kvden_ps, 1)

            def keys(n):
                for hf in range(2):
                    pe.wait_ge(qk_done, 4 * n + 3 + hf)
                    for t in range(CT):
                        s = hf * HALF + t * P
                        ins = pe.transpose(bank[hf][:, t * P:(t + 1) * P], kf[:, s:s + P], ident)
                    ins.then_inc(kt_ps, 1)

            def attend(n):
                b, r = n % B, n % 2
                pe.wait_ge(kva_ready, n + 1)
                pe.wait_ge(den_ready, n + 1)
                pe.matmul(bank[4][:, 256:384], c["rot"], kva[:, :], start=True, stop=True).then_inc(kvb_ps, 1)
                for hf in range(2):
                    pe.wait_ge(v_done, v_needed(n) + hf)
                    turn(bank[2 + hf], b * N + hf * HALF, res_ps)
                pe.wait_ge(kvb_ready, n + 1)
                for hf in range(2):
                    if n:
                        pe.wait_ge(out_read, 2 * n - 1 + hf)
                    for t in range(CT):
                        s = hf * HALF + t * P
                        o = bank[5 + hf][:, t * P:(t + 1) * P]
                        pe.matmul(o, qc[r][:, s:s + P], kva[:, :], start=True, stop=False)
                        ins = pe.matmul(o, qs[r][:, s:s + P], kvb[:, :], start=False, stop=True)
                    ins.then_inc(out_ps, 1)

            def v_needed(n):
                n1 = HALFWAY if n < HALFWAY else STEPS
                ones = 1 if n < HALFWAY else 2
                last = min(n + 1, n1 - 1)
                return ones + 2 * last + 1

            def attention(n0, n1, ones):
                pe.wait_ge(shift_ready, ones)
                for n in range(n0, n1 + 2):
                    if n0 < n <= n1:
                        sums(n - 1, ones)
                    if n < n1:
                        project(n)
                    if n < n1:
                        keys(n)
                    if n0 < n <= n1:
                        attend(n - 1)
                    if n > n0 + 1:
                        back(B + n - 2, 0)
                        back(B + n - 2, 1)

            def shared_up(i, b):
                if not is_first(i):
                    pe.wait_ge(shh_ready, i * 2 + (b - 1))
                h = xn_fm[:, bass.ds(i * 2 * HALF + b * HALF, HALF)]
                pe.matmul(bank[b][:, :], swg, h, start=True, stop=True)
                pe.matmul(bank[2 + b][:, :], swu, h, start=True, stop=True).then_inc(shg_ps, 1)

            def shared_down(i, b):
                pe.wait_ge(shh_ready, i * 2 + (b + 1))
                if not is_first(i):
                    pe.wait_ge(shd_read, i * 2 + (b - 1))
                for t in range(CT):
                    o = bank[4 + b][:, t * P:(t + 1) * P]
                    pe.matmul(o, shh[b][:, t * P:(t + 1) * P], swd, start=True, stop=False)
                    ins = pe.matmul(o, ones_r[:, :], ln2b_r[:, :], start=False, stop=True)
                ins.then_inc(shd_ps, 1)

            pe.wait_ge(shared_in, 48)
            pe.wait_ge(param_in, 16 * NPARAM)
            pipeline(pe, XCHUNKS, [(0, shared_up), (-1, shared_down)])
            phase_end(pe, 1)

            pe.wait_ge(attn_in, 32)
            attention(0, HALFWAY, 1)
            phase_end(pe, 2)

            regs = [pe.alloc_register(f"expert{t}") for t in range(CT)]

            def experts_of(i, r):
                pe.load(regs, te_row[0:1, bass.ds(i * RB * CT + r * CT, CT)])
                return [pe.snap(reg, min_val=0, max_val=E - 1) for reg in regs]

            def rows_T(i, r):
                b = r % 2
                pe.wait_ge(rows_in[r], i * 16 + 16)
                if not is_first(i, r):
                    pe.wait_ge(rowsT_ready, i * RB + (r - 1))
                for t in range(CT):
                    ins = pe.transpose(bank[b][:, t * P:(t + 1) * P], xg[r][:, t, :], ident)
                ins.then_inc(rowsT_ps, 1)

            def gate_up(i, r):
                b = r % 2
                ex = experts_of(i, r)
                pe.wait_ge(rowsT_ready, i * RB + (r + 1))
                if not is_first(i, r):
                    pe.wait_ge(gated_ready, i * RB + (r - 1))
                for t in range(CT):
                    ins = pe.matmul(bank[2 + b][:, t * P:(t + 1) * P], xT[b][:, t * P:(t + 1) * P],
                                    wgu_sb[:, bass.ds(ex[t], 1), :].rearrange("p a v -> p (a v)"), start=True, stop=True)
                ins.then_inc(gu_ps, 1)

            def gated_T(i, r):
                b = r % 2
                pe.wait_ge(gated_ready, i * RB + (r + 1))
                if not is_first(i, r):
                    pe.wait_ge(evenT_ready, i * RB + (r - 1))
                    pe.wait_ge(oddT_ready, i * RB + (r - 1))
                for t in range(CT // 2):
                    ins = pe.transpose(bank[4 + b][:, t * P:(t + 1) * P],
                                       hh[b][:, 2 * t:2 * t + 2, :].rearrange("p c i -> p (c i)"), ident)
                ins.then_inc(gatedT_ps, 1)

            def down(i, r):
                b = r % 2
                ex = experts_of(i, r)
                pe.wait_ge(evenT_ready, i * RB + (r + 1))
                pe.wait_ge(oddT_ready, i * RB + (r + 1))
                if not is_first(i, r):
                    pe.wait_ge(rows_ready, i * RB + (r - 1))
                for t in range(CT):
                    ins = pe.matmul(bank[6 + b][:, t * P:(t + 1) * P], hT[b][:, t * P:(t + 1) * P],
                                    wed_sb[:, bass.ds(ex[t], 1), :].rearrange("p a v -> p (a v)"), start=True, stop=True)
                ins.then_inc(down_ps, 1)

            pe.wait_ge(experts_in, 32)
            pe.wait_ge(te_in, 16)
            pipeline(pe, CHUNKS, [(1, rows_T), (0, gate_up), (-1, gated_T), (-2, down)], RB)
            phase_end(pe, 3)

            attention(HALFWAY, STEPS, 2)
            phase_end(pe, 4)

            def ffn_up(i, b):
                h = h_fm[:, bass.ds(i * 2 * HALF + b * HALF, HALF)]
                for j in range(MUL):
                    if not (is_first(i) and b == 0):
                        pe.wait_ge(fh_ready, i * (2 * MUL) + (b * MUL + j + 1 - MUL))
                    pe.matmul(bank[(0, 1, 6, 7)[j]][:, :], fw1[:, j * H:(j + 1) * H], h, start=True, stop=True).then_inc(f1_ps, 1)

            def ffn_down(i, b):
                pe.wait_ge(fh_ready, i * (2 * MUL) + (b * MUL + MUL))
                if not is_first(i):
                    pe.wait_ge(fy_ready, i * 2 + (b - 1))
                for j in range(MUL):
                    ins = pe.matmul(bank[2 + b][:, :], fw2[:, j * H:(j + 1) * H], fh[:, b, j, :], start=(j == 0), stop=(j == MUL - 1))
                ins.then_inc(f2_ps, 1)

            def ffn_T(i, b):
                pe.wait_ge(fy_ready, i * 2 + (b + 1))
                if not is_first(i):
                    pe.wait_ge(fy_read, i * 2 + (b - 1))
                for t in range(CT):
                    ins = pe.transpose(bank[4 + b][:, t * P:(t + 1) * P], fy[b][:, t * P:(t + 1) * P], ident)
                ins.then_inc(fy_ps, 1)

            pe.wait_ge(ffn_in, 32)
            pipeline(pe, XCHUNKS, [(0, ffn_up), (-1, ffn_down), (-2, ffn_T)])


def constants():
    at, n = const_table()
    table = np.zeros((P, n), np.float32)
    p = np.arange(P)
    values = {
        "ident": np.eye(P),
        "iota_e": np.broadcast_to(np.arange(E), (P, E)),
        "tri_g": np.broadcast_to(np.tril(np.ones((G, G)), -1).reshape(1, -1), (P, G * G)),
        "iota_j": 2 * p[:, None] + np.arange(2),
        "dmask": p[:, None] % CW == np.arange(CW),
        "dmask3": (p[:, None] % CW == np.arange(CW)) & (p[:, None] >= 3 * CW),
        "dmask2": p[:, None] // MUL == np.arange(CW),
        "bdmask": (p[:, None] // HD == p // HD) / N,
        "hmean": (p[:, None] // HD == np.arange(HEADS)) / N,
        "hshift": (p[:, None] // HD == np.arange(HEADS)) * SHIFT,
        "eps_z": np.full((P, 1), EPS_Z),
        "utri": np.triu(np.ones((P, P)), 1),
        "rot": np.where((p[:, None] == p + 1) & (p % 2 == 0), 1.0, np.where((p[:, None] == p - 1) & (p % 2 == 1), -1.0, 0.0)),
    }
    for name, (lo, width) in at.items():
        table[:, lo:lo + width] = values[name]
    inv = 1.0 / 10000.0 ** (np.arange(0, H, 2, dtype=np.float32) / H)
    ang = np.repeat(np.arange(N, dtype=np.float32)[:, None] * inv.astype(np.float32)[None], 2, axis=-1).astype(np.float32)
    cos, sin = np.cos(ang), np.sin(ang)
    sign = np.where(np.arange(H) % 2 == 0, -1.0, 1.0).astype(np.float32)
    tm = lambda v: v.reshape(BT, P, H).transpose(1, 0, 2).reshape(P, N)
    rope = np.concatenate([tm(cos), tm(sin * sign), cos.T, sin.T], axis=1).astype(np.float32)
    return table, rope


def kernel(**inputs):
    import concourse.bacc as _bacc
    from concourse.bass_utils import run_bass_kernel_spmd as _run

    nc = _bacc.Bacc("TRN2", target_bir_lowering=False, num_devices=1)
    f = {k.replace("L0_attn_", "").replace("L0_", ""): np.asarray(v) for k, v in inputs.items()}
    table, rope = constants()
    w1 = f["conv1_w"].reshape(CG, CW, MUL, TAPS)
    w2 = f["conv2_w"].reshape(CG, CW, MUL, TAPS)
    w1_taps = w1.transpose(3, 1, 0, 2)[:4].reshape(P, CG * MUL)
    w1_last = np.tile(w1[..., 4].transpose(1, 0, 2).reshape(CW, CG * MUL), (4, 1))
    w2_rows = w2.transpose(1, 2, 0, 3).reshape(P, CG * TAPS)
    arrays = {
        "x": f["x"], "consts": table, "rope": rope, "gate_w": f["ffn_gate_w"].T, "gate_bias": f["ffn_gate_bias"],
        "conv_w": np.concatenate([w1_taps, w1_last, w2_rows], axis=1),
        "cols": np.concatenate([f["bq"].T, f["bk"].T, f["lnA_g"].T, f["lnA_b"].T, f["ln0_g"][:, None], f["ln0_b"][:, None],
                                f["conv2_b"][:, None], f["b2"][:, None], f["conv1_b"].reshape(CG, P).T,
                                f["b1"].reshape(MUL, P).T], axis=1),
        "wqkv": np.stack([f["Wq"], f["Wk"], f["Wv"]], axis=1).transpose(2, 0, 1, 3),
        "bv": f["bv"], "ln2_g": f["ln2_g"], "ln2_b": f["ln2_b"], "w1": f["W1"], "w2": f["W2"],
        "wgu": np.concatenate([f["ffn_eg_w"], f["ffn_eu_w"]], axis=1).transpose(2, 0, 1),
        "wed": f["ffn_ed_w"].transpose(2, 0, 1),
        "sg": f["ffn_sg_w"].T, "su": f["ffn_su_w"].T, "sd": f["ffn_sd_w"].T,
    }
    arrays = {f"in_{k}": np.ascontiguousarray(v) for k, v in arrays.items()}
    aps = {k[3:]: nc.dram_tensor(k, v.shape, mybir.dt.from_np(v.dtype), kind="ExternalInput").ap() for k, v in arrays.items()}
    out = nc.dram_tensor("out_0", (B, N, H), F32, kind="ExternalOutput").ap()
    block_kernel(nc, aps, out)
    r = _run(nc, [arrays], core_ids=[0])
    return r.results[0]["out_0"]
```

```python
from contextlib import ExitStack

import numpy as np
import concourse.bass as bass
from concourse import mybir

F32 = mybir.dt.float32
BF16 = mybir.dt.bfloat16
I32 = mybir.dt.int32
U32 = mybir.dt.uint32
ALU = mybir.AluOpType
ACT = mybir.ActivationFunctionType
AX = mybir.AxisListType

P = 128
B, N, H = 4, 1024, 128
T = B * N
TILES = T // P
BT = N // P
HALF = 512
CT = HALF // P
E, G, TG, K, I = 64, 8, 4, 6, 64
EG = E // G
SLOT_TILES = T * K // P + E
SLOTS = SLOT_TILES * P
CHUNKS = SLOT_TILES // CT
RB = 4
STORE_LAG = 3
XCHUNKS = T // HALF
LAYERS, HEADS = 4, 16
HD = H // HEADS
CG, CW, TAPS, MUL = 8, 16, 5, 4
NP = N // 2
SHIFTS = TAPS + 1
K6 = SHIFTS * CW
PT = 3
H1W = NP + PT - 1
SHIFT = 0.21
EPS_X, EPS_LN, EPS_Z, EPS_W = 1e-5, 1e-12, 1e-6, 1e-8
STEPS = LAYERS * B
HALFWAY = 8
NORM_AT = 2
FFN_BEFORE = 4
COUNT_AT = 2
CONV_AT, CONV_EARLY = 3, 1
RW = H + 1
BIG = 3e38


def const_table():
    at, n = {}, 0
    for name, width in (("ident", P), ("iota_e", E), ("iota_j", 2), ("dmask", CW), ("dmask2", CW), ("same", 2 * CW),
                        ("bdmask", P), ("hmean", HEADS), ("hshift", HEADS), ("eps_z", 1), ("rot", P), ("rest", P)):
        at[name] = (n, width)
        n += width
    return at, n


def block_kernel(nc, a, out):
    consts_at, consts_n = const_table()
    with ExitStack() as ctx:
        def sb(name, shape, dt=F32):
            return ctx.enter_context(nc.sbuf_tensor(name, shape, dt))

        def sem(name):
            return ctx.enter_context(nc.semaphore(name))

        def carve(region, sizes):
            at, views = 0, []
            for size in sizes:
                views.append(region[:, at:at + size])
                at += size
            assert at <= region.shape[1], (at, region.shape)
            return views

        xs = nc.dram_tensor("rows_in", [SLOTS, RW], F32).ap()
        ys = nc.dram_tensor("rows_out", [SLOTS, H], F32).ap()
        xd = nc.dram_tensor("x_pairs", [B, H, 2, NP], F32).ap()
        te_dram = nc.dram_tensor("tile_expert", [P, 2], I32).ap()

        x_tm = sb("x_tm", [P, TILES, H])
        xn_r = sb("xn_r", [P, TILES * RW])
        xn_w = xn_r[:, :].rearrange("p (t f) -> p t f", f=RW)
        xn_tm = xn_w[:, :, 0:H]
        xn_fm = sb("xn_fm", [P, T])
        h_fm = sb("h_fm", [P, T])
        cst = sb("cst", [P, consts_n])
        c = {name: cst[:, at:at + width] for name, (at, width) in consts_at.items()}
        ident = c["ident"]
        cols = sb("cols", [P, 4 * LAYERS + 2 + 2 + 1 + CG + MUL])
        wk = sb("wk", [P, TILES, K])
        addr = sb("addr", [P, TILES * K], I32)
        te_row = sb("te_row", [1, 2 * P], I32)
        ln2g_b = sb("ln2g_b", [P, H])
        ln2b_b = sb("ln2b_b", [P, H])
        nw_a = sb("nw_a", [P, BT])
        nw_t = sb("nw_t", [P, BT])
        nmr = sb("nmr", [P, 2, BT])
        rstd_r = sb("rstd_r", [P, 2, BT])
        stats = sb("stats", [P, BT, 6])
        mv = sb("mv", [P, BT, 2])
        bq_c, bk_c, gA_c, bA_c = (cols[:, k * LAYERS:(k + 1) * LAYERS] for k in range(4))
        k0 = 4 * LAYERS
        ln0g_c, ln0b_c, fb2_c = (cols[:, k0 + k:k0 + k + 1] for k in range(3))
        cb2_c, cb1_c, fb1_c = cols[:, k0 + 3:k0 + 5], cols[:, k0 + 5:k0 + 5 + CG], cols[:, k0 + 5 + CG:k0 + 5 + CG + MUL]

        arena = sb("arena", [P, 2 * E * H])
        u = sb("u", [P, 14144])
        w = sb("w", [P, CG * H1W])

        x6_r, w1_r, w2c_r, tmp, zeros = carve(arena, [2 * CG * NP, CG * P, CG * PT * 2 * CW, 4096, 16 * RW])
        SW = E + 2
        scores_r, left_r, incl, picked_r, rest_r, ones_r_, gate_sb, gbias, gs_r, gleft_r, gtop_r, gmask_r, top8_r, \
            idx8_r, slot8_r, idxf_r, rank_r, slot_i, t1, t2, ntile, one_e, first, ends, cnt_i, te_f, te_i, wsum, tm_r, \
            restart, pair_r = carve(u, [
                TILES * SW, TILES * SW, TILES * E, TILES * E // 2, P // 2, P // 2, E, E, TILES * (G + TG),
                TILES * (G + TG), TILES * 8, TILES * G, TILES * 8, TILES * 8, TILES * 8, TILES * K, TILES * K, TILES * K,
                TILES * K, TILES * K, E, E, E, E, E, 2, 2, TILES, 2 * E, HALF, TILES * K * K])
        scores, left = (v.rearrange("p (t e) -> p t e", e=SW) for v in (scores_r, left_r))
        gs, gleft = (v.rearrange("p (t g) -> p t g", g=G + TG) for v in (gs_r, gleft_r))
        gmask = gmask_r.rearrange("p (t g) -> p t g", g=G)
        picked = picked_r.bitcast(BF16)
        rest, ones_bf = rest_r.bitcast(BF16), ones_r_.bitcast(BF16)
        gtop, top8, slot8 = (v.rearrange("p (t k) -> p t k", k=8) for v in (gtop_r, top8_r, slot8_r))
        idx8 = idx8_r.bitcast(U32).rearrange("p (t k) -> p t k", k=8)
        idxf, rank = (v.rearrange("p (t k) -> p t k", k=K) for v in (idxf_r, rank_r))
        pair = pair_r.rearrange("p (t j i) -> p t j i", j=K, i=K)
        slot_i, t1, t2, cnt_i, te_i = (v.bitcast(I32) for v in (slot_i, t1, t2, cnt_i, te_i))
        place, slot_em = tmp[:, 0:TILES * E], tmp[:, TILES * E:2 * TILES * E]
        x6 = x6_r.rearrange("p (r g m) -> p r g m", r=2, g=CG)
        w1c = w1_r.rearrange("p (g m) -> p g m", g=CG)
        w2c = w2c_r.rearrange("p (g m) -> p g m", m=2 * CW)
        x_de = tmp[:, 0:T].rearrange("p (b a i) -> p b a i", b=B, a=2)
        h1 = w[:, :].rearrange("p (g m) -> p g m", g=CG)
        cwv = sb("cwv", [P, CG * 2 * MUL + CG * PT * 2])
        w1v, w2v = carve(cwv, [CG * 2 * MUL, CG * PT * 2])
        cos_tm, sin_tm, cos_fm, sin_fm = carve(xn_fm, [N] * 4)
        wqkv_r, bv_r, kva, kvb, kvm, z, den, shift_m, fw1, fw2 = carve(w, [
            LAYERS * 3 * H, LAYERS * H, P, P, P, BT * HEADS, BT * HEADS, P, MUL * H, MUL * H])
        wqkv = wqkv_r.rearrange("p (l m f) -> p l m f", l=LAYERS, m=3)
        bv_b = bv_r.rearrange("p (l f) -> p l f", l=LAYERS)
        q0_, q1_, qc0, qc1, qs0, qs1, kf, kc, ks, v0, v1, xo_r, xh_r = carve(
            u, [N] * 9 + [BT * (H + 2)] * 2 + [N] * 2)
        qp, qc, qs = [q0_, q1_], [qc0, qc1], [qs0, qs1]
        vv = [v.rearrange("p (t f) -> p t f", f=H + 2) for v in (v0, v1)]
        xo = xo_r.rearrange("p (t f) -> p t f", f=H)
        xh = xh_r.rearrange("p (t f) -> p t f", f=H)
        xo2 = [xo, u[:, 4 * N:5 * N].rearrange("p (t f) -> p t f", f=H)]
        kacc = sb("kacc", [P, 2, 2])
        kbt = sb("kbt", [P, HEADS])
        kb = sb("kb", [P, 2, HEADS])
        ksum = sb("ksum", [P, 2])
        wgu_sb = arena[:, 0:E * H].rearrange("p (e v) -> p e v", e=E)
        wed_sb = arena[0:I, E * H:2 * E * H].rearrange("p (e v) -> p e v", e=E)
        xg0, xg1, xg2, xg3, yo0, yo1, yo2, yo3 = carve(xn_r, [CT * RW] * 4 + [HALF] * 4)
        xT0, xT1, hT0, hT1, sg0, sg1, hh0, hh1 = carve(u, [HALF] * 4 + [CT * I] * 4)
        xg = [v.rearrange("p (t f) -> p t f", f=RW) for v in (xg0, xg1, xg2, xg3)]
        xT = [xT0, xT1]
        sg = [v.rearrange("p (t f) -> p t f", f=I) for v in (sg0, sg1)]
        hh = [v.rearrange("p (t f) -> p t f", f=I) for v in (hh0, hh1)]
        hT = [hT0[0:I, :], hT1[0:I, :]]
        yo = [yo0, yo1, yo2, yo3]
        row_w = sb("row_w", [P, RB, CT])
        swg, swu, swd, shs0, shs1, shh0, shh1 = carve(u, [P, P, P] + [HALF] * 4)
        shs, shh = [shs0, shs1], [shh0, shh1]
        routed_r, fh_r, hb0, hb1, ft0, ft1 = carve(arena, [T, 2 * MUL * HALF] + [HALF] * 4)
        routed = routed_r.rearrange("p (t f) -> p t f", f=H)
        fh = fh_r.rearrange("p (b j m) -> p b j m", b=2, j=MUL)
        hb, ft = [hb0, hb1], [v.rearrange("p (t f) -> p t f", f=H) for v in (ft0, ft1)]

        bank = [ctx.enter_context(nc.psum_tensor(f"bank{k}", [P, HALF], F32)) for k in range(8)]

        x_in = [sem(f"x_in{q}") for q in range(4)]
        const_in = sem("const_in")
        param_in = sem("param_in")
        attn_in = sem("attn_in")
        tables_in = sem("tables_in")
        experts_in = sem("experts_in")
        shared_in = sem("shared_in")
        ffn_in = sem("ffn_in")
        fills = sem("fills")
        pads_zero = sem("pads_zero")
        rows_zero = sem("rows_zero")
        xn_ready = sem("xn_ready")
        xt_ps = sem("xt_ps")
        xf_ready = sem("xf_ready")
        logits_ps = sem("logits_ps")
        sig_ready = sem("sig_ready")
        pick_ready = sem("pick_ready")
        count_ps = sem("count_ps")
        base_ready = sem("base_ready")
        rank_ps = sem("rank_ps")
        rank_read = sem("rank_read")
        addr_ready = sem("addr_ready")
        te_ready = sem("te_ready")
        te_out = sem("te_out")
        te_in = sem("te_in")
        scattered = [sem(f"scattered{h}") for h in range(2)]
        convw_ready = sem("convw_ready")
        de_ready = sem("de_ready")
        de_out = sem("de_out")
        x6_in = [sem(f"x6_in{r}") for r in range(2)]
        bias_added = sem("bias_added")
        c1_ps = sem("c1_ps")
        c1_done = sem("c1_done")
        c2_ps = sem("c2_ps")
        c2_done = sem("c2_done")
        res_ps = sem("res_ps")
        res_read = sem("res_read")
        stats_ready = sem("stats_ready")
        xh_ready = sem("xh_ready")
        back_ps = sem("back_ps")
        back_done = sem("back_done")
        h_ready = sem("h_ready")
        qk_ps = sem("qk_ps")
        qk_done = sem("qk_done")
        v_ps = sem("v_ps")
        v_done = sem("v_done")
        kb_ready = sem("kb_ready")
        shift_ready = sem("shift_ready")
        q_ready = sem("q_ready")
        kt_ps = sem("kt_ps")
        kr_ready = sem("kr_ready")
        kvden_ps = sem("kvden_ps")
        kva_ready = sem("kva_ready")
        den_ready = sem("den_ready")
        kvb_ps = sem("kvb_ps")
        kvb_ready = sem("kvb_ready")
        out_ps = sem("out_ps")
        out_read = sem("out_read")
        shg_ps = sem("shg_ps")
        shs_ready = sem("shs_ready")
        shh_ready = sem("shh_ready")
        shd_ps = sem("shd_ps")
        shd_read = sem("shd_read")
        rows_in = [sem(f"rows_in{r}") for r in range(RB)]
        rowsT_ps = sem("rowsT_ps")
        rowsT_ready = sem("rowsT_ready")
        gu_ps = sem("gu_ps")
        silu_ready = sem("silu_ready")
        gated_ready = sem("gated_ready")
        gatedT_ps = sem("gatedT_ps")
        evenT_ready = sem("evenT_ready")
        oddT_ready = sem("oddT_ready")
        down_ps = sem("down_ps")
        rows_ready = sem("rows_ready")
        rows_out = [sem(f"rows_out{r}") for r in range(RB)]
        gathered = [sem(f"gathered{h}") for h in range(2)]
        weights_put = sem("weights_put")
        row_w_kept = sem("row_w_kept")
        f1_ps = sem("f1_ps")
        fh_ready = sem("fh_ready")
        f2_ps = sem("f2_ps")
        hb_ready = sem("hb_ready")
        f2_read = sem("f2_read")
        sum_ready = sem("sum_ready")
        out_sent = sem("out_sent")

        NFILL = SLOTS // (P * 16)
        NX6 = SHIFTS
        NFILLS = 4
        NCONST = 4
        NPARAM = 3

        x_v = a["x"].rearrange("b (t p) f -> p (b t) f", p=P)
        out_v = out.rearrange("b (t p) f -> p (b t) f", p=P)
        xs_v = xs.rearrange("(c p r) f -> c p (r f)", p=P, r=CT)
        ys_v = ys.rearrange("(c p r) f -> c p (r f)", p=P, r=CT)
        fill_v = xs.rearrange("(z p r) f -> z p (r f)", p=P, r=16)

        def is_first(i, s=0):
            return isinstance(i, int) and i == 0 and s < 2

        def pipeline(eng, count, stages, unit=2):
            def step(i, r):
                for off, stage in stages:
                    o = r + off
                    if isinstance(i, int) and not 0 <= unit * i + o < count:
                        continue
                    stage(i + o // unit, o % unit)

            first, last = -(-4 // unit), count // unit - 1
            for s in range(-1, first * unit):
                step(s // unit, s % unit)
            with eng.Fori(first, last) as i:
                for r in range(unit):
                    step(i, r)
            for s in range(last * unit, count + 2):
                step(s // unit, s % unit)

        block = ctx.enter_context(nc.Block())

        @block.sync
        def _(sp):
            n = TILES // 4
            for q in range(4):
                sp.dma_start(x_tm[:, q * n:(q + 1) * n, :], x_v[:, q * n:(q + 1) * n, :]).then_inc(x_in[q], 16)
                if q == 0:
                    sp.dma_start(cst[:, :], a["consts"]).then_inc(const_in, 16)
                    sp.dma_start(gate_sb, a["gate_w"]).then_inc(const_in, 16)
                    sp.dma_start(gbias, a["gate_bias"].rearrange("(a e) -> a e", a=1).broadcast_to([P, E])).then_inc(const_in, 16)
                    sp.dma_start(cwv[:, :], a["conv_w"]).then_inc(const_in, 16)
            sp.dma_start(cols[:, :], a["cols"]).then_inc(param_in, 16)
            sp.dma_start(ln2g_b[:, :], a["ln2_g"].rearrange("(a f) -> a f", a=1).broadcast_to([P, H])).then_inc(param_in, 16)
            sp.dma_start(ln2b_b[:, :], a["ln2_b"].rearrange("(a f) -> a f", a=1).broadcast_to([P, H])).then_inc(param_in, 16)

            def store_pairs(b):
                sp.wait_ge(de_ready, 2 * (b + 1))
                sp.dma_start(xd[b].rearrange("f a i -> f (a i)"), x_de[:, b].rearrange("p a i -> p (a i)")).then_inc(de_out, 16)

            def load_x6(b):
                r = b % 2
                if b < 2:
                    sp.wait_ge(de_out, 16 * (b + 1))
                else:
                    sp.wait_ge(de_out, 16 * B)
                    sp.wait_ge(c2_ps, 2 * (b - 1))
                src = xd[b].rearrange("(g c) a i -> a c g i", c=CW)
                for s in range(SHIFTS):
                    d = s // 2 - 1
                    lo, hi = max(0, -d), min(NP, NP - d)
                    sp.dma_start(x6[CW * s:CW * (s + 1), r, :, lo:hi], src[s % 2][:, :, lo + d:hi + d]).then_inc(x6_in[r], 16)

            for b in range(B):
                store_pairs(b)
                if b < 2:
                    load_x6(b)
            for b in range(2, B):
                for k in range((b - 2) * NFILL // 2, (b - 1) * NFILL // 2):
                    if k == 0:
                        sp.wait_ge(fills, 1)
                    sp.dma_start(fill_v[k], zeros).then_inc(rows_zero, 16)
                load_x6(b)
            sp.wait_ge(te_ready, 1)
            sp.dma_start(te_dram[:, :], te_i).then_inc(te_out, 16)
            sp.wait_ge(te_out, 16)
            sp.dma_start(te_row[:, :], te_dram.rearrange("(o p) a -> o (p a)", o=1)).then_inc(te_in, 16)
            sp.wait_ge(addr_ready, 1)
            sp.dma_start(swg, a["sg"]).then_inc(shared_in, 16)
            sp.dma_start(swu, a["su"]).then_inc(shared_in, 16)
            sp.dma_start(swd, a["sd"]).then_inc(shared_in, 16)
            sp.wait_ge(c2_ps, 2 * B)
            sp.dma_start(wqkv, a["wqkv"]).then_inc(attn_in, 16)
            sp.dma_start(bv_r, a["bv"].rearrange("(a l) f -> a (l f)", a=1).broadcast_to([P, LAYERS * H])).then_inc(attn_in, 16)
            sp.dma_start(fw1, a["w1"]).then_inc(ffn_in, 16)
            sp.dma_start(fw2.rearrange("p (j f) -> p j f", f=H), a["w2"].rearrange("(j p) f -> p j f", p=P)).then_inc(ffn_in, 16)
            sp.wait_ge(shg_ps, XCHUNKS)
            sp.dma_start(xn_fm[:, :], a["rope"]).then_inc(tables_in, 16)
            sp.wait_ge(rows_zero, 16 * NFILL)
            sp.dma_start(wgu_sb, a["wgu"]).then_inc(experts_in, 16)
            sp.dma_start(wed_sb, a["wed"]).then_inc(experts_in, 16)

            def load_rows(i, r):
                if not (isinstance(i, int) and i == 0):
                    sp.wait_ge(rowsT_ps, i * RB + (r + 1 - RB))
                    sp.wait_ge(row_w_kept, i * RB + (r + 1 - RB))
                sp.dma_start(xg[r].rearrange("p r f -> p (r f)"), xs_v[bass.ds(i * RB + r, 1)]).then_inc(rows_in[r], 16)

            def store_rows(i, r):
                sp.wait_ge(rows_ready, i * RB + (r + 1))
                sp.dma_start(ys_v[bass.ds(i * RB + r, 1)], yo[r]).then_inc(rows_out[r], 16)

            for h in range(2):
                sp.wait_ge(scattered[h], 16 * TILES // 2 * K)
            sp.wait_ge(xh_ready, B)
            for r in range(RB + STORE_LAG):
                load_rows(r // RB, r % RB)
            with sp.Fori(0, CHUNKS // RB - 2) as i:
                for r in range(RB):
                    load_rows(i + 1 + (r + STORE_LAG) // RB, (r + STORE_LAG) % RB)
                    store_rows(i, r)
            for j in range(CHUNKS - 2 * RB, CHUNKS):
                if j + RB + STORE_LAG < CHUNKS:
                    load_rows((j + RB + STORE_LAG) // RB, (j + STORE_LAG) % RB)
                store_rows(j // RB, j % RB)
            for k in range(XCHUNKS):
                sp.wait_ge(sum_ready, k + 1)
                sp.dma_start(out_v[:, k * CT:(k + 1) * CT, :], x_tm[:, k * CT:(k + 1) * CT, :]).then_inc(out_sent, 16)
            sp.wait_ge(out_sent, 16 * XCHUNKS)

        @block.gpsimd
        def _(pool):
            pool.memset(zeros, 0.0).then_inc(fills, 1)
            pool.memset(ones_bf, 1.0).then_inc(fills, 1)
            pool.memset(h1[:, :, 0:1], 0.0).then_inc(fills, 1)
            pool.memset(h1[:, :, NP + 1:], 0.0).then_inc(fills, 1)
            pool.wait_ge(param_in, 16 * NPARAM)
            pool.wait_ge(xn_ready, XCHUNKS)
            pool.tensor_tensor(x_tm[:, :, :], x_tm[:, :, :], ln2b_b[:, :].unsqueeze(1).broadcast_to([P, TILES, H]),
                               ALU.add).then_inc(bias_added, 1)

            pool.wait_ge(addr_ready, 1)
            pool.wait_ge(rows_zero, 16 * NFILL)
            for k in range(K):
                for h in range(2):
                    tiles = range(h * TILES // 2, (h + 1) * TILES // 2)
                    if k:
                        pool.wait_ge(scattered[h], 16 * len(tiles) * k)
                    pool.tensor_copy(xn_w[:, tiles.start:tiles.stop, H], wk[:, tiles.start:tiles.stop, k]).then_inc(weights_put, 1)
                    pool.wait_ge(weights_put, 2 * k + h + 1)
                    for t in tiles:
                        q = t * K + k
                        pool.indirect_dma_start(xs[:, :], bass.IndirectOffsetOnAxis(addr[:, q:q + 1].bitcast(U32), 0),
                                                xn_w[:, t, :], None).then_inc(scattered[h], 16)
            for r in range(RB):
                pool.wait_ge(rows_out[r], 16 * CHUNKS // RB)
            for k in range(K):
                for h in range(2):
                    tiles = range(h * TILES // 2, (h + 1) * TILES // 2)
                    if k:
                        pool.wait_ge(gathered[h], 16 * len(tiles) * k)
                    for t in tiles:
                        q = t * K + k
                        pool.indirect_dma_start(routed[:, t, :], None, ys[:, :],
                                                bass.IndirectOffsetOnAxis(addr[:, q:q + 1].bitcast(U32), 0),
                                                compute_op=ALU.add if k else ALU.bypass).then_inc(gathered[h], 16)

        @block.vector
        def _(dve):
            dve.memset(x6[0:2 * CW, :, :, 0:1], 0.0).then_inc(pads_zero, 1)
            dve.memset(x6[4 * CW:6 * CW, :, :, NP - 1:NP], 0.0).then_inc(pads_zero, 1)

            def inv_sqrt(n, eps, rstd):
                y, var, s, t = rstd[:, 0:n], mv[:, 0:n, 1], nw_a[:, 0:n], nw_t[:, 0:n]
                dve.tensor_scalar(s, var, eps, None, ALU.add)
                dve.drain()
                dve.tensor_scalar(t.bitcast(I32), s.bitcast(I32), 1, None, ALU.logical_shift_right)
                dve.drain()
                dve.tensor_scalar(y.bitcast(I32), t.bitcast(I32), -1.0, float(0x5f3759df), ALU.mult, ALU.add)
                for _ in range(3):
                    dve.drain()
                    dve.scalar_tensor_tensor(t, y, -0.5, y, ALU.mult, ALU.mult)
                    dve.drain()
                    dve.tensor_tensor(t, t, s, ALU.mult)
                    dve.drain()
                    dve.scalar_tensor_tensor(y, t, 1.5, y, ALU.add, ALU.mult)

            def moments(n, tile, eps, rstd):
                for t in range(n):
                    dve.bn_stats(stats[:, t, :], tile(t))
                dve.drain()
                for t in range(n):
                    dve.bn_aggr(mv[:, t, :], stats[:, t, :])
                dve.drain()
                inv_sqrt(n, eps, rstd)
                dve.drain()

            def conv_weights():
                dve.wait_ge(const_in, 16 * NCONST)
                v1 = w1v.rearrange("p (g a j) -> p g a j", g=CG, a=2)
                v2 = w2v.rearrange("p (g a) -> p g a", a=2)
                for a2 in range(2):
                    dve.tensor_tensor(w1c[:, :, a2 * P // 2:(a2 + 1) * P // 2].rearrange("p g (c j) -> p g c j", j=MUL),
                                      c["dmask"].unsqueeze(1).unsqueeze(3).broadcast_to([P, CG, CW, MUL]),
                                      v1[:, :, a2, :].unsqueeze(2).broadcast_to([P, CG, CW, MUL]), ALU.mult)
                    dve.tensor_tensor(w2c[:, :, a2 * CW:(a2 + 1) * CW],
                                      c["dmask2"].unsqueeze(1).broadcast_to([P, CG * PT, CW]),
                                      v2[:, :, a2].unsqueeze(2).broadcast_to([P, CG * PT, CW]), ALU.mult)
                dve.tensor_copy(rest, c["rest"])
                dve.drain().then_inc(convw_ready, 1)

            for q in range(4):
                if q == 1:
                    conv_weights()
                dve.wait_ge(x_in[q], 16)
                rstd = rstd_r[:, 0, :]
                moments(BT, lambda t: x_tm[:, q * BT + t, :], EPS_X, rstd)
                for t in range(BT):
                    ins = dve.tensor_scalar(xn_tm[:, q * BT + t, :], x_tm[:, q * BT + t, :], mv[:, t, 0:1],
                                            rstd[:, t:t + 1], ALU.subtract, ALU.mult)
                    if t % CT == CT - 1:
                        ins.then_inc(xn_ready, 1)
                dve.drain()

            dve.memset(scores[:, :, E:], BIG)
            dve.memset(gs[:, :, G:], BIG)
            dve.memset(restart, 1.0)
            dve.memset(one_e, 1.0)
            dve.drain()
            dve.memset(restart.rearrange("p (e t) -> p e t", t=TILES)[:, :, 0:1], 0.0)
            dve.wait_ge(sig_ready, XCHUNKS // 2)
            sc = scores[:, :, 0:E]
            dve.tensor_tensor(sc, sc, gbias.unsqueeze(1).broadcast_to([P, TILES, E]), ALU.add)
            dve.drain()
            dve.tensor_reduce(gs[:, :, 0:G], sc.rearrange("p t (g e) -> p t g e", e=EG), AX.X, ALU.max)
            dve.drain()
            for t in range(TILES):
                dve.max(gtop[:, t, :], gs[:, t, 0:G])
            dve.drain()
            dve.memset(gtop[:, :, TG:], BIG)
            dve.drain()
            for t in range(TILES):
                dve.match_replace(gleft[:, t, :], gtop[:, t, :], gs[:, t, :], -BIG)
            dve.drain()
            dve.tensor_scalar(gmask, gleft[:, :, 0:G], -BIG, None, ALU.is_equal)
            dve.drain()
            sce = sc.rearrange("p t (g e) -> p t g e", e=EG)
            dve.tensor_tensor(sce, sce, gmask.unsqueeze(3).broadcast_to([P, TILES, G, EG]), ALU.mult)
            dve.drain()
            for t in range(TILES):
                dve.max(top8[:, t, :], scores[:, t, 0:E])
            dve.drain()
            dve.memset(top8[:, :, K:], BIG)
            dve.drain()
            for t in range(TILES):
                dve.match_replace(left[:, t, :], top8[:, t, :], scores[:, t, :], -BIG)
            dve.drain()
            dve.tensor_scalar(picked.rearrange("p (e t) -> p t e", t=TILES), left[:, :, 0:E], -BIG, None,
                              ALU.is_equal).then_inc(pick_ready, 1)
            for t in range(TILES):
                dve.max_index(idx8[:, t, :], top8[:, t, :], scores[:, t, :])
            dve.tensor_reduce(wsum, top8[:, :, 0:K], AX.X, ALU.add)
            dve.drain()
            dve.tensor_copy(idxf, idx8[:, :, 0:K])
            dve.tensor_scalar(wsum, wsum, EPS_W, None, ALU.add)
            dve.drain()
            dve.tensor_tensor(pair, idxf.unsqueeze(2).broadcast_to([P, TILES, K, K]),
                              idxf.unsqueeze(3).broadcast_to([P, TILES, K, K]), ALU.is_gt)
            dve.reciprocal(wsum, wsum)
            dve.drain()
            dve.tensor_reduce(rank, pair, AX.X, ALU.add)
            dve.drain()
            dve.tensor_tensor(pair, rank.unsqueeze(2).broadcast_to([P, TILES, K, K]),
                              c["iota_e"][:, 0:K].unsqueeze(1).unsqueeze(3).broadcast_to([P, TILES, K, K]), ALU.is_equal)
            dve.drain()
            dve.tensor_tensor(pair, pair, top8[:, :, 0:K].unsqueeze(2).broadcast_to([P, TILES, K, K]), ALU.mult)
            dve.drain()
            dve.tensor_reduce(wk[:, :, :], pair, AX.X, ALU.add)
            dve.drain()
            dve.tensor_tensor(wk[:, :, :], wk[:, :, :], wsum.unsqueeze(2).broadcast_to([P, TILES, K]), ALU.mult)
            dve.wait_ge(count_ps, 1)
            for k in range(4):
                ins = dve.tensor_tensor_scan(incl[:, k * HALF:(k + 1) * HALF], restart, bank[4 + k][:, :], 0.0,
                                             ALU.mult, ALU.add)
            ins.then_inc(base_ready, 1)
            dve.drain()
            dve.tensor_scalar(cnt_i, incl.rearrange("p (e t) -> p e t", t=TILES)[:, :, TILES - 1], float(P - 1), None, ALU.add)
            dve.drain()
            dve.tensor_scalar(cnt_i, cnt_i, 7, None, ALU.logical_shift_right)
            dve.drain()
            dve.tensor_copy(ntile, cnt_i)
            dve.drain()
            dve.tensor_tensor_scan(ends, one_e, ntile, 0.0, ALU.mult, ALU.add)
            dve.drain()
            dve.tensor_tensor(ntile, ends, ntile, ALU.subtract)
            tm = tm_r.rearrange("p (a e) -> p a e", e=E)
            dve.tensor_tensor(tm, ends.unsqueeze(1).broadcast_to([P, 2, E]),
                              c["iota_j"].unsqueeze(2).broadcast_to([P, 2, E]), ALU.is_le)
            dve.drain()
            dve.tensor_scalar(first, ntile, float(P), 1.0, ALU.mult, ALU.add)
            dve.tensor_reduce(te_f, tm, AX.X, ALU.add)
            dve.drain()
            dve.wait_ge(de_out, 16 * B)
            dve.tensor_tensor(place.rearrange("p (e t) -> p e t", t=TILES), incl.rearrange("p (e t) -> p e t", t=TILES),
                              first.unsqueeze(2).broadcast_to([P, E, TILES]), ALU.add)
            dve.tensor_scalar(te_i, te_f, float(E - 1), None, ALU.min).then_inc(te_ready, 1)
            dve.wait_ge(rank_ps, 1)
            dve.drain()
            for k in range(4):
                ins = dve.tensor_tensor(place[:, k * HALF:(k + 1) * HALF], bank[4 + k][:, :],
                                        place[:, k * HALF:(k + 1) * HALF], ALU.add)
            ins.then_inc(rank_read, 1)
            dve.drain()
            dve.tensor_tensor(slot_em.rearrange("p (t e) -> p e t", e=E), place.rearrange("p (e t) -> p e t", t=TILES),
                              picked.rearrange("p (e t) -> p e t", t=TILES), ALU.mult)
            dve.drain()
            for t in range(TILES):
                dve.max(slot8[:, t, :], slot_em[:, t * E:(t + 1) * E])
            dve.drain()
            dve.tensor_scalar(slot_i.rearrange("p (t k) -> p t k", k=K), slot8[:, :, 0:K], -1.0, None, ALU.add)
            dve.drain()
            dve.tensor_scalar(t1, slot_i, P - 1, 2, ALU.bitwise_and, ALU.logical_shift_left)
            dve.tensor_scalar(t2, slot_i, 7, CT - 1, ALU.logical_shift_right, ALU.bitwise_and)
            dve.tensor_scalar(addr[:, :], slot_i, 0x7fffffff ^ (HALF - 1), None, ALU.bitwise_and)
            dve.drain()
            dve.tensor_tensor(t1, t1, t2, ALU.bitwise_or)
            dve.drain()
            dve.tensor_tensor(addr[:, :], t1, addr[:, :], ALU.bitwise_or)
            dve.drain().then_inc(addr_ready, 1)

            def normalize(n, xo, eps):
                r = n % 2
                moments(BT, lambda t: xo[:, t, :], eps, rstd_r[:, r, :])
                dve.scalar_tensor_tensor(nmr[:, r, :], mv[:, :, 0], -1.0, rstd_r[:, r, :], ALU.mult, ALU.mult)
                dve.drain().then_inc(stats_ready, 1)

            dve.wait_ge(te_out, 16)
            def conv_norm(b):
                o = xo2[b % 2]
                if b >= 2:
                    dve.wait_ge(xh_ready, b - 1)
                for hf in range(2):
                    dve.wait_ge(res_ps, 2 * b + hf + 1)
                    for q in range(2):
                        ins = dve.tensor_copy(
                            o[:, 4 * hf + 2 * q:4 * hf + 2 * q + 2, :].rearrange("p a (g c) -> p a g c", c=CW),
                            bank[5 + hf][:, q * 2 * H:(q + 1) * 2 * H].rearrange("p (g a c) -> p a g c", a=2, c=CW))
                    ins.then_inc(res_read, 1)
                dve.drain()
                normalize(b, o, EPS_LN)

            def key_mean(n):
                r = n % 2
                dve.wait_ge(qk_done, 4 * n + 2)
                dve.scalar_tensor_tensor(kbt[:, :], c["hmean"], kacc[:, r, 0:1], c["hshift"], ALU.mult, ALU.add)
                dve.drain()
                dve.scalar_tensor_tensor(kb[:, r, :], c["hmean"], kacc[:, r, 1:2], kbt[:, :], ALU.mult, ALU.add)
                dve.drain().then_inc(kb_ready, 1)

            def key_values(n):
                dve.wait_ge(kvden_ps, n + 1)
                dve.tensor_copy(ksum[:, :], bank[4][:, H:H + 2])
                dve.drain()
                dve.scalar_tensor_tensor(kvm, bv_b[:, n // B, :], ksum[:, 0:1], bank[4][:, 0:H], ALU.mult, ALU.add)
                dve.drain()
                dve.tensor_tensor(kva[:, :], kvm, c["bdmask"], ALU.mult).then_inc(kva_ready, 1)

            def queries(n):
                r = n % 2
                dve.wait_ge(qk_done, 4 * n + 4)
                dve.scalar_tensor_tensor(qc[r], qp[r], SHIFT, cos_fm, ALU.add, ALU.mult)
                dve.scalar_tensor_tensor(qs[r], qp[r], SHIFT, sin_fm, ALU.add, ALU.mult).then_inc(q_ready, 1)

            def keys(n):
                if n:
                    dve.wait_ge(kvden_ps, n)
                for hf in range(2):
                    dve.wait_ge(kt_ps, 2 * n + hf + 1)
                    s = slice(hf * HALF, (hf + 1) * HALF)
                    ev, od = slice(hf * HALF, (hf + 1) * HALF, 2), slice(hf * HALF + 1, (hf + 1) * HALF, 2)
                    dve.scalar_tensor_tensor(kc[:, s], bank[hf][:, :], SHIFT, cos_tm[:, s], ALU.add, ALU.mult)
                    dve.scalar_tensor_tensor(ks[:, ev], bank[hf][:, 1::2], SHIFT, sin_tm[:, ev], ALU.add, ALU.mult)
                    dve.scalar_tensor_tensor(ks[:, od], bank[hf][:, 0::2], SHIFT, sin_tm[:, od], ALU.add,
                                             ALU.mult).then_inc(kr_ready, 1)

            def attended(n):
                dve.wait_ge(den_ready, n + 1)
                dve.reciprocal(z, den)
                dve.drain()
                dve.wait_ge(xh_ready, B + n)
                for hf in range(2):
                    o = xo[:, hf * CT:(hf + 1) * CT, :].rearrange("p t (h d) -> p (t h) d", d=HD)
                    zz = z[:, hf * CT * HEADS:(hf + 1) * CT * HEADS].unsqueeze(2).broadcast_to([P, CT * HEADS, HD])
                    dve.wait_ge(out_ps, 2 * n + hf + 1)
                    dve.tensor_tensor(o, bank[5 + hf][:, :].rearrange("p (t d) -> p t d", d=HD), zz, ALU.mult).then_inc(out_read, 1)
                dve.drain()
                for hf in range(2):
                    o = xo[:, hf * CT:(hf + 1) * CT, :].rearrange("p t f -> p (t f)")
                    dve.wait_ge(res_ps, 2 * (B + n) + hf + 1)
                    dve.tensor_tensor(o, o, bank[2 + hf][:, :], ALU.add).then_inc(res_read, 1)
                dve.drain()
                normalize(B + n, xo, EPS_LN)

            def attention(n0, n1):
                for n in range(n0, n1 + 1):
                    if n > n0:
                        key_values(n - 1)
                    if n < n1:
                        key_mean(n)
                        if n == 0:
                            dve.wait_ge(tables_in, 16)
                        queries(n)
                        keys(n)
                    if n > n0:
                        attended(n - 1)

            def shared_gated(j):
                dve.wait_ge(shs_ready, j + 1)
                if j >= 2:
                    dve.wait_ge(shd_ps, j - 1)
                dve.tensor_tensor(shh[j % 2], shs[j % 2], bank[2 + j % 2][:, :], ALU.mult).then_inc(shh_ready, 1)

            def shared_sum(j):
                dve.wait_ge(shd_ps, j + 1)
                dst = x_tm[:, j * CT:(j + 1) * CT, :].rearrange("p t f -> p (t f)")
                dve.tensor_tensor(dst, dst, bank[4][:, :], ALU.add).then_inc(shd_read, 1)

            conv_norm(0)
            for b in range(B):
                if b < B - 1:
                    conv_norm(b + 1)
                if b:
                    shared_sum(2 * b - 1)
                shared_gated(2 * b)
                shared_gated(2 * b + 1)
                if b == 0:
                    dve.wait_ge(bias_added, 1)
                shared_sum(2 * b)
            shared_sum(XCHUNKS - 1)
            dve.wait_ge(attn_in, 32)
            dve.memset(shift_m, SHIFT)
            dve.drain().then_inc(shift_ready, 1)
            attention(0, HALFWAY)

            def gated(i, r):
                b = r % 2
                dve.wait_ge(silu_ready, i * RB + (r + 1))
                if not is_first(i, r):
                    dve.wait_ge(gatedT_ps, i * RB + (r - 1))
                g4 = bank[2 + b][:, :].rearrange("p (c v) -> p c v", v=2 * I)
                dve.tensor_tensor(hh[b], sg[b], g4[:, :, I:], ALU.mult).then_inc(gated_ready, 1)

            def even_columns(i, r):
                b = r % 2
                dve.wait_ge(gatedT_ps, i * RB + (r + 1))
                if not is_first(i, r):
                    dve.wait_ge(down_ps, i * RB + (r - 1))
                dve.tensor_copy(hT[b].rearrange("p (q a s) -> p q a s", a=2, s=P)[:, :, 0, :],
                                bank[4 + b][0:I, 0:2 * P].rearrange("p (q s) -> p q s", s=P)).then_inc(evenT_ready, 1)

            def keep_weights(i, r):
                dve.wait_ge(rows_in[r], i * 16 + 16)
                if not (isinstance(i, int) and i == 0):
                    dve.wait_ge(rows_ready, i * RB + (r + 1 - RB))
                dve.tensor_copy(row_w[:, r, :], xg[r][:, :, H]).then_inc(row_w_kept, 1)

            def expert_rows(i, r):
                b = r % 2
                dve.wait_ge(row_w_kept, i * RB + (r + 1))
                dve.wait_ge(down_ps, i * RB + (r + 1))
                if not (isinstance(i, int) and i == 0):
                    dve.wait_ge(rows_out[r], i * 16)
                dve.tensor_tensor(yo[r].rearrange("p (t f) -> p t f", f=H), bank[6 + b][:, :].rearrange("p (t f) -> p t f", f=H),
                                  row_w[:, r, :].unsqueeze(2).broadcast_to([P, CT, H]), ALU.mult).then_inc(rows_ready, 1)

            pipeline(dve, CHUNKS, [(1, keep_weights), (0, gated), (-1, even_columns), (-2, expert_rows)], RB)

            attention(HALFWAY, STEPS)
            def add_routed(j):
                dve.wait_ge(gathered[j * 2 // XCHUNKS], 16 * TILES // 2 * K)
                dst = x_tm[:, j * CT:(j + 1) * CT, :]
                dve.tensor_tensor(dst, dst, routed[:, j * CT:(j + 1) * CT, :], ALU.add).then_inc(sum_ready, 1)

            dve.wait_ge(xh_ready, B + STEPS)
            for j in range(XCHUNKS):
                dve.wait_ge(f2_ps, j + 1)
                tile = lambda t: bank[2 + j % 2][:, t * H:(t + 1) * H]
                rstd = rstd_r[:, 0, :]
                moments(CT, tile, EPS_LN, rstd)
                for t in range(CT):
                    ins = dve.scalar_tensor_tensor(ft[j % 2][:, t, :], tile(t), mv[:, t, 0:1], ln2g_b[:, :],
                                                   ALU.subtract, ALU.mult)
                ins.then_inc(f2_read, 1)
                dve.drain()
                for t in range(CT):
                    dst = x_tm[:, j * CT + t, :]
                    dve.scalar_tensor_tensor(dst, ft[j % 2][:, t, :], rstd[:, t:t + 1], dst, ALU.mult, ALU.add)
                dve.drain()
                if j >= XCHUNKS // 2:
                    add_routed(2 * j - XCHUNKS)
                    add_routed(2 * j - XCHUNKS + 1)

        @block.scalar
        def _(act):
            def normalized(n):
                act.wait_ge(stats_ready, n + 1)
                if n:
                    act.wait_ge(back_ps, 2 * n)
                src, r = xo2[n % 2] if n < B else xo, n % 2
                for t in range(BT):
                    ins = act.activation(xh[:, t, :], src[:, t, :], ACT.Identity, bias=nmr[:, r, t:t + 1],
                                         scale=rstd_r[:, r, t:t + 1])
                ins.then_inc(xh_ready, 1)

            def feature_major(n, g, bias):
                for hf in range(2):
                    s = (n % B) * N + hf * HALF
                    act.wait_ge(back_ps, 2 * n + hf + 1)
                    dst, src = h_fm[:, s:s + HALF], bank[7][:, :]
                    if n < B:
                        dst = dst.rearrange("p (q i a) -> p q a i", q=2, a=2)
                        src = src.rearrange("p (q a i) -> p q a i", q=2, a=2)
                    act.activation(dst, src, ACT.Identity, bias=bias, scale=g).then_inc(back_done, 1)
                act.drain().then_inc(h_ready, 1)

            def conv_gelu(b, g):
                act.wait_ge(c1_ps, b * CG + g + 1)
                if b and g == 0:
                    act.wait_ge(c2_ps, 2 * b)
                act.activation(h1[:, g, 1:NP + 1], bank[g % 2][:, :], ACT.Gelu, bias=cb1_c[:, g:g + 1]).then_inc(c1_done, 1)

            for j in range(XCHUNKS):
                act.wait_ge(xt_ps, j + 1)
                act.activation(xn_fm[:, j * HALF:(j + 1) * HALF], bank[2 + j % 2][:, :], ACT.Copy).then_inc(xf_ready, 1)
                act.activation(x_de[:, j // 2, :, j % 2 * NP // 2:(j % 2 + 1) * NP // 2].rearrange("p a i -> p i a"),
                               bank[2 + j % 2][:, :].rearrange("p (i a) -> p i a", a=2), ACT.Copy).then_inc(de_ready, 1)
                if j == CONV_AT:
                    act.wait_ge(param_in, 16 * NPARAM)
                    act.wait_ge(fills, NFILLS)
                    for g in range(CONV_EARLY):
                        conv_gelu(0, g)
            act.wait_ge(logits_ps, XCHUNKS)
            for k in range(XCHUNKS // 2):
                act.activation(scores[:, k * 2 * CT:(k + 1) * 2 * CT, 0:E],
                               bank[4 + k][:, :].rearrange("p (t e) -> p t e", e=E), ACT.Sigmoid).then_inc(sig_ready, 1)
            for b in range(B):
                for g in range(0 if b else CONV_EARLY, CG):
                    conv_gelu(b, g)
                for hf in range(2):
                    act.wait_ge(c2_ps, 2 * b + hf + 1)
                    act.activation(h_fm[:, b * N + hf * HALF:b * N + (hf + 1) * HALF], bank[2 + hf][:, :], ACT.Identity,
                                   bias=cb2_c[:, hf:hf + 1]).then_inc(c2_done, 1)

            def projected(n):
                l, r = n // B, n % 2
                if n:
                    act.wait_ge(kt_ps, 2 * n)
                if n >= 2:
                    act.wait_ge(kb_ready, n - 1)
                for hf in range(2):
                    act.wait_ge(qk_ps, 4 * n + hf + 1)
                    act.activation(kf[:, hf * HALF:(hf + 1) * HALF], bank[hf][:, :], ACT.Gelu, bias=bk_c[:, l:l + 1],
                                   accum_out=kacc[:, r, hf:hf + 1]).then_inc(qk_done, 1)
                if n >= 2:
                    act.wait_ge(out_ps, 2 * (n - 1))
                for hf in range(2):
                    act.wait_ge(qk_ps, 4 * n + 2 + hf + 1)
                    act.activation(qp[r][:, hf * HALF:(hf + 1) * HALF], bank[hf][:, :], ACT.Gelu,
                                   bias=bq_c[:, l:l + 1]).then_inc(qk_done, 1)
                for hf in range(2):
                    act.wait_ge(v_ps, 2 * n + hf + 1)
                    act.activation(vv[r][:, hf * CT:(hf + 1) * CT, 0:H],
                                   bank[2 + hf][:, :].rearrange("p (t f) -> p t f", f=H), ACT.Copy).then_inc(v_done, 1)

            def denominators(n):
                act.wait_ge(kva_ready, n + 1)
                if n:
                    act.wait_ge(out_read, 2 * n)
                act.activation(den, bank[4][:, 384:512], ACT.Identity, bias=c["eps_z"]).then_inc(den_ready, 1)

            def rotated(n):
                act.wait_ge(kvb_ps, n + 1)
                if n:
                    act.wait_ge(out_ps, 2 * n)
                act.activation(kvb[:, :], bank[4][:, 256:384], ACT.Copy).then_inc(kvb_ready, 1)

            def ffn_gelu(j):
                if j >= 2:
                    act.wait_ge(f2_ps, j - 1)
                for m in range(MUL):
                    act.wait_ge(f1_ps, j * MUL + m + 1)
                    act.activation(fh[:, j % 2, m, :], bank[m % 2][:, :], ACT.Gelu, bias=fb1_c[:, m:m + 1]).then_inc(fh_ready, 1)
                act.activation(hb[j % 2], h_fm[:, j * HALF:(j + 1) * HALF], ACT.Identity, bias=fb2_c).then_inc(hb_ready, 1)

            def attention(n0, n1):
                for n in range(n0, n1 + (2 if n1 == STEPS else 1)):
                    if n == STEPS + 1:
                        for j in range(FFN_BEFORE):
                            if j == NORM_AT:
                                normalized(B + STEPS - 1)
                            ffn_gelu(j)
                    if n < n1:
                        projected(n)
                    if n0 < n <= n1:
                        denominators(n - 1)
                        rotated(n - 1)
                    if n >= 2 and n > (n0 and HALFWAY):
                        m = n - 2
                        if m < STEPS - 1:
                            normalized(B + m)
                        feature_major(B + m, gA_c[:, m // B:m // B + 1], bA_c[:, m // B:m // B + 1])

            def shared_silu(j):
                act.wait_ge(shg_ps, j + 1)
                if j >= 2:
                    act.wait_ge(shh_ready, j - 1)
                act.activation(shs[j % 2], bank[j % 2][:, :], ACT.Silu).then_inc(shs_ready, 1)

            shared_silu(0)
            shared_silu(1)
            for b in range(B):
                normalized(b)
                if b < B - 1:
                    shared_silu(2 * b + 2)
                    shared_silu(2 * b + 3)
                feature_major(b, ln0g_c, ln0b_c)

            for r in range(2):
                act.activation(vv[r][:, :, H:H + 2], ident[:, 0:2 * BT].rearrange("p (t o) -> p t o", o=2),
                               ACT.Identity, bias=1.0, scale=0.0)
            act.drain().then_inc(v_done, 1)
            attention(0, HALFWAY)

            def columns(i, r):
                b = r % 2
                act.wait_ge(rowsT_ps, i * RB + (r + 1))
                if not is_first(i, r):
                    act.wait_ge(gu_ps, i * RB + (r - 1))
                act.activation(xT[b], bank[b][:, :], ACT.Copy).then_inc(rowsT_ready, 1)

            def silu(i, r):
                b = r % 2
                act.wait_ge(gu_ps, i * RB + (r + 1))
                if not is_first(i, r):
                    act.wait_ge(gated_ready, i * RB + (r - 1))
                g4 = bank[2 + b][:, :].rearrange("p (c v) -> p c v", v=2 * I)
                act.activation(sg[b], g4[:, :, 0:I], ACT.Silu).then_inc(silu_ready, 1)

            def odd_columns(i, r):
                b = r % 2
                act.wait_ge(gatedT_ps, i * RB + (r + 1))
                if not is_first(i, r):
                    act.wait_ge(down_ps, i * RB + (r - 1))
                act.activation(hT[b].rearrange("p (q a s) -> p q a s", a=2, s=P)[:, :, 1, :],
                               bank[4 + b][I:P, 0:2 * P].rearrange("p (q s) -> p q s", s=P), ACT.Copy).then_inc(oddT_ready, 1)

            pipeline(act, CHUNKS, [(1, columns), (0, silu), (-1, odd_columns)], RB)

            attention(HALFWAY, STEPS)
            for j in range(FFN_BEFORE, XCHUNKS):
                ffn_gelu(j)

        @block.tensor
        def _(pe):
            def logits(j):
                pe.wait_ge(xf_ready, j + 1)
                for t in range(CT):
                    s = (j * CT + t) * P
                    o = bank[4 + j // 2][:, (j % 2 * CT + t) * E:(j % 2 * CT + t + 1) * E]
                    ins = pe.matmul(o, xn_fm[:, s:s + P], gate_sb, start=True, stop=True)
                ins.then_inc(logits_ps, 1)

            def conv1(b, g):
                n = b * CG + g
                if n >= 2:
                    pe.wait_ge(c1_done, n - 1)
                pe.matmul(bank[g % 2][:, :], w1c[0:K6, g, :], x6[0:K6, b % 2, g, :], start=True, stop=True).then_inc(c1_ps, 1)

            pe.wait_ge(const_in, 16 * NCONST)
            for j in range(XCHUNKS):
                pe.wait_ge(xn_ready, j + 1)
                if j >= 2:
                    pe.wait_ge(de_ready, j - 1)
                for t in range(CT):
                    ins = pe.transpose(bank[2 + j % 2][:, t * P:(t + 1) * P], xn_tm[:, j * CT + t, :], ident)
                ins.then_inc(xt_ps, 1)
                if j:
                    logits(j - 1)
                if j == CONV_AT:
                    pe.wait_ge(convw_ready, 1)
                    pe.wait_ge(x6_in[0], 16 * NX6)
                    pe.wait_ge(fills, NFILLS)
                    pe.wait_ge(pads_zero, 2)
                    for g in range(CONV_EARLY):
                        conv1(0, g)
            logits(XCHUNKS - 1)

            def turn(dst, s, sm):
                for t in range(CT):
                    ins = pe.transpose(dst[:, t * P:(t + 1) * P], h_fm[:, s + t * P:s + (t + 1) * P], ident)
                ins.then_inc(sm, 1)

            def back(n, halves=(0, 1)):
                pe.wait_ge(xh_ready, n + 1)
                for hf in halves:
                    if n or hf:
                        pe.wait_ge(back_done, 2 * n + hf)
                    for t in range(CT):
                        ins = pe.transpose(bank[7][:, t * P:(t + 1) * P], xh[:, hf * CT + t, :], ident)
                    ins.then_inc(back_ps, 1)

            def conv_turn(b):
                pe.wait_ge(c2_done, 2 * b + 2)
                for hf in range(2):
                    if b:
                        pe.wait_ge(res_read, 2 * b - 1 + hf)
                    for q in range(2):
                        for k in range(2):
                            s = b * N + k * NP + (2 * hf + q) * P
                            ins = pe.transpose(bank[5 + hf][:, (2 * q + k) * P:(2 * q + k + 1) * P], h_fm[:, s:s + P], ident)
                    ins.then_inc(res_ps, 1)

            def conv2(b):
                pe.wait_ge(c1_done, CG * (b + 1))
                for hf in range(2):
                    if b:
                        pe.wait_ge(c2_done, 2 * b - 1 + hf)
                    for k in range(PT + 1):
                        for g4 in range(4):
                            g = 4 * hf + g4
                            o = bank[2 + hf][2 * CW * g4:2 * CW * (g4 + 1), :]
                            if k < PT:
                                ins = pe.matmul(o, w2c[:, g * PT + k, :], h1[:, g, k:k + NP], start=(k == 0), stop=False)
                            else:
                                ins = pe.matmul(o, c["same"][0:K6, :], x6[0:K6, b % 2, g, :], start=False, stop=True)
                    ins.then_inc(c2_ps, 1)

            pe.wait_ge(de_ready, XCHUNKS)
            for b in range(B):
                if b:
                    pe.wait_ge(x6_in[b % 2], 16 * NX6 * (b // 2 + 1))
                if b == COUNT_AT:
                    pe.wait_ge(pick_ready, 1)
                    for k in range(4):
                        ins = pe.matmul(bank[4 + k][:, :], ones_bf, picked[:, k * HALF:(k + 1) * HALF], start=True, stop=True)
                    ins.then_inc(count_ps, 1)
                for g in range(0 if b else CONV_EARLY, CG):
                    if b == COUNT_AT and g == CG - 2:
                        pe.wait_ge(base_ready, 1)
                        for k in range(4):
                            ins = pe.matmul(bank[4 + k][:, :], rest, picked[:, k * HALF:(k + 1) * HALF], start=True, stop=True)
                        ins.then_inc(rank_ps, 1)
                    conv1(b, g)
                if b == B - 1:
                    conv_turn(1)
                conv2(b)
                if b == COUNT_AT:
                    pe.wait_ge(rank_read, 1)
                    conv_turn(0)

            def project(n):
                l, b = n // B, n % B
                pe.wait_ge(h_ready, n + 1)
                for k, (m, first) in enumerate(((1, 0), (1, 1), (0, 0), (0, 1))):
                    hf = first
                    if k < 2:
                        if n:
                            pe.wait_ge(kr_ready, 2 * n - 1 + hf)
                    else:
                        pe.wait_ge(qk_done, 4 * n + hf + 1)
                    pe.matmul(bank[hf][:, :], wqkv[:, l, m, :], h_fm[:, b * N + hf * HALF:b * N + (hf + 1) * HALF],
                              start=True, stop=True).then_inc(qk_ps, 1)
                for hf in range(2):
                    pe.wait_ge(res_read, 2 * (B + n) - 3 + hf)
                    for t in range(CT):
                        s = b * N + hf * HALF + t * P
                        ins = pe.matmul(bank[2 + hf][:, t * P:(t + 1) * P], h_fm[:, s:s + P], wqkv[:, l, 2, :],
                                        start=True, stop=True)
                    ins.then_inc(v_ps, 1)

            def key_value_sums(n):
                r = n % 2
                pe.wait_ge(kr_ready, 2 * n + 2)
                pe.wait_ge(v_done, 2 * n + 2 + 1)
                if n == 0:
                    pe.wait_ge(shd_read, XCHUNKS)
                else:
                    pe.wait_ge(kvb_ready, n)
                    pe.wait_ge(kva_ready, n)
                    pe.wait_ge(den_ready, n)
                for t in range(BT):
                    for k, part in enumerate((kc, ks)):
                        pe.matmul(bank[4][:, 0:H + 2], part[:, t * P:(t + 1) * P], vv[r][:, t, :],
                                  start=(t == 0 and k == 0), stop=(t == BT - 1 and k == 1))

            def denominator_sums(n):
                r = n % 2
                pe.wait_ge(kb_ready, n + 1)
                pe.wait_ge(q_ready, n + 1)
                pe.matmul(bank[4][:, 384:512].rearrange("p (t h) -> p t h", h=HEADS), shift_m,
                          kb[:, r, :].unsqueeze(1).broadcast_to([P, BT, HEADS]), start=True, stop=False)
                for t in range(BT):
                    ins = pe.matmul(bank[4][:, 384 + t * HEADS:384 + (t + 1) * HEADS], qp[r][:, t * P:(t + 1) * P],
                                    kb[:, r, :], start=False, stop=(t == BT - 1))
                ins.then_inc(kvden_ps, 1)

            def keys(n):
                for hf in range(2):
                    pe.wait_ge(qk_done, 4 * n + 3 + hf)
                    for t in range(CT):
                        s = hf * HALF + t * P
                        ins = pe.transpose(bank[hf][:, t * P:(t + 1) * P], kf[:, s:s + P], ident)
                    ins.then_inc(kt_ps, 1)

            def attend(n):
                b, r = n % B, n % 2
                pe.wait_ge(kva_ready, n + 1)
                pe.wait_ge(den_ready, n + 1)
                pe.matmul(bank[4][:, 256:384], c["rot"], kva[:, :], start=True, stop=True).then_inc(kvb_ps, 1)
                for hf in range(2):
                    pe.wait_ge(v_done, v_needed(n) + hf)
                    turn(bank[2 + hf], b * N + hf * HALF, res_ps)
                pe.wait_ge(kvb_ready, n + 1)
                for hf in range(2):
                    if n:
                        pe.wait_ge(out_read, 2 * n - 1 + hf)
                    for t in range(CT):
                        s = hf * HALF + t * P
                        o = bank[5 + hf][:, t * P:(t + 1) * P]
                        pe.matmul(o, qc[r][:, s:s + P], kva[:, :], start=True, stop=False)
                        ins = pe.matmul(o, qs[r][:, s:s + P], kvb[:, :], start=False, stop=True)
                    ins.then_inc(out_ps, 1)

            def v_needed(n):
                n1 = HALFWAY if n < HALFWAY else STEPS
                last = min(n + 1, n1 - 1)
                return 1 + 2 * last + 1

            def ffn_up(j):
                pe.wait_ge(h_ready, B + STEPS - B + j * CT // BT + 1)
                h = h_fm[:, j * HALF:(j + 1) * HALF]
                for m in range(MUL):
                    if j or m >= 2:
                        pe.wait_ge(fh_ready, j * MUL + m - 1)
                    pe.matmul(bank[m % 2][:, :], fw1[:, m * H:(m + 1) * H], h, start=True, stop=True).then_inc(f1_ps, 1)

            def ffn_down(j):
                b = j % 2
                pe.wait_ge(fh_ready, (j + 1) * MUL)
                pe.wait_ge(hb_ready, j + 1)
                if j < 2:
                    pe.wait_ge(res_read, 2 * (B + STEPS))
                else:
                    pe.wait_ge(f2_read, j - 1)
                for t in range(CT):
                    o, tok = bank[2 + b][:, t * P:(t + 1) * P], slice(t * P, (t + 1) * P)
                    for m in range(MUL):
                        pe.matmul(o, fh[:, b, m, tok], fw2[:, m * H:(m + 1) * H], start=(m == 0), stop=False)
                    ins = pe.matmul(o, hb[b][:, tok], ident, start=False, stop=True)
                ins.then_inc(f2_ps, 1)

            def attention(n0, n1):
                for n in range(n0, n1 + (2 if n1 == STEPS else 1)):
                    if n0 < n <= n1:
                        key_value_sums(n - 1)
                    if n >= 3 and n > (n0 and HALFWAY + 1):
                        back(B + n - 3, (1,))
                    if n0 < n <= n1:
                        denominator_sums(n - 1)
                    if n == STEPS + 1:
                        pe.wait_ge(ffn_in, 32)
                        ffn_up(0)
                        ffn_up(1)
                        for j in range(FFN_BEFORE - 2):
                            ffn_down(j)
                            ffn_up(j + 2)
                    if n < n1:
                        project(n)
                    if n < n1:
                        keys(n)
                    if n0 < n <= n1:
                        attend(n - 1)
                    if n >= 2 and n > (n0 and HALFWAY):
                        back(B + n - 2, (0,))
                back(B + n - 2, (1,))

            def shared_up(j):
                if j >= 2:
                    pe.wait_ge(shh_ready, j - 1)
                h = xn_fm[:, j * HALF:(j + 1) * HALF]
                pe.matmul(bank[j % 2][:, :], swg, h, start=True, stop=True)
                pe.matmul(bank[2 + j % 2][:, :], swu, h, start=True, stop=True).then_inc(shg_ps, 1)

            def shared_down(j):
                pe.wait_ge(shh_ready, j + 1)
                if j:
                    pe.wait_ge(shd_read, j)
                for t in range(CT):
                    ins = pe.matmul(bank[4][:, t * P:(t + 1) * P], shh[j % 2][:, t * P:(t + 1) * P], swd, start=True, stop=True)
                ins.then_inc(shd_ps, 1)

            pe.wait_ge(shared_in, 48)
            pe.wait_ge(c1_done, CG * B)
            pe.wait_ge(c2_done, 2 * B)
            shared_up(0)
            shared_up(1)
            for b in range(B):
                if b < B - 2:
                    conv_turn(b + 2)
                for j in (2 * b, 2 * b + 1):
                    shared_down(j)
                    if j + 2 < XCHUNKS:
                        shared_up(j + 2)
                back(b)

            pe.wait_ge(attn_in, 32)
            pe.wait_ge(shift_ready, 1)
            attention(0, HALFWAY)

            regs = [[pe.alloc_register(f"expert{r}_{t}") for t in range(CT)] for r in range(RB)]

            def expert(r, t):
                return pe.snap(regs[r][t], min_val=0, max_val=E - 1)

            def rows_T(i, r):
                b = r % 2
                pe.wait_ge(rows_in[r], i * 16 + 16)
                for t in range(CT):
                    ins = pe.transpose(bank[b][:, t * P:(t + 1) * P], xg[r][:, t, 0:H], ident)
                ins.then_inc(rowsT_ps, 1)

            def gate_up(i, r):
                b = r % 2
                pe.load(regs[r], te_row[0:1, bass.ds(i * RB * CT + r * CT, CT)])
                pe.wait_ge(rowsT_ready, i * RB + (r + 1))
                for t in range(CT):
                    ins = pe.matmul(bank[2 + b][:, t * P:(t + 1) * P], xT[b][:, t * P:(t + 1) * P],
                                    wgu_sb[:, bass.ds(expert(r, t), 1), :].rearrange("p a v -> p (a v)"), start=True, stop=True)
                ins.then_inc(gu_ps, 1)

            def gated_T(i, r):
                b = r % 2
                pe.wait_ge(gated_ready, i * RB + (r + 1))
                for t in range(CT // 2):
                    ins = pe.transpose(bank[4 + b][:, t * P:(t + 1) * P],
                                       hh[b][:, 2 * t:2 * t + 2, :].rearrange("p c i -> p (c i)"), ident)
                ins.then_inc(gatedT_ps, 1)

            def down(i, r):
                b = r % 2
                pe.wait_ge(evenT_ready, i * RB + (r + 1))
                pe.wait_ge(oddT_ready, i * RB + (r + 1))
                if not is_first(i, r):
                    pe.wait_ge(rows_ready, i * RB + (r - 1))
                for t in range(CT):
                    ins = pe.matmul(bank[6 + b][:, t * P:(t + 1) * P], hT[b][:, t * P:(t + 1) * P],
                                    wed_sb[:, bass.ds(expert(r, t), 1), :].rearrange("p a v -> p (a v)"), start=True, stop=True)
                ins.then_inc(down_ps, 1)

            pe.wait_ge(experts_in, 32)
            pe.wait_ge(te_in, 16)
            pe.wait_ge(back_done, 2 * (B + HALFWAY - 1))
            pe.wait_ge(out_read, 2 * HALFWAY)
            pe.wait_ge(res_read, 2 * (B + HALFWAY))
            pipeline(pe, CHUNKS, [(1, rows_T), (0, gate_up), (-1, gated_T), (-2, down)], RB)

            attention(HALFWAY, STEPS)
            for j in range(FFN_BEFORE - 2, XCHUNKS):
                ffn_down(j)
                if j + 2 < XCHUNKS:
                    ffn_up(j + 2)


def constants():
    at, n = const_table()
    table = np.zeros((P, n), np.float32)
    p = np.arange(P)
    values = {
        "ident": np.eye(P),
        "iota_e": np.broadcast_to(np.arange(E), (P, E)),
        "iota_j": 2 * p[:, None] + np.arange(2),
        "dmask": p[:, None] % CW == np.arange(CW),
        "dmask2": p[:, None] // MUL % CW == np.arange(CW),
        "same": (p[:, None] // CW == 2 + np.arange(2 * CW) // CW) & (p[:, None] % CW == np.arange(2 * CW) % CW),
        "bdmask": (p[:, None] // HD == p // HD) / N,
        "hmean": (p[:, None] // HD == np.arange(HEADS)) / N,
        "hshift": (p[:, None] // HD == np.arange(HEADS)) * SHIFT,
        "eps_z": np.full((P, 1), EPS_Z),
        "rest": -np.tril(np.ones((P, P))),
        "rot": np.where((p[:, None] == p + 1) & (p % 2 == 0), 1.0, np.where((p[:, None] == p - 1) & (p % 2 == 1), -1.0, 0.0)),
    }
    for name, (lo, width) in at.items():
        table[:, lo:lo + width] = values[name]
    inv = 1.0 / 10000.0 ** (np.arange(0, H, 2, dtype=np.float32) / H)
    ang = np.repeat(np.arange(N, dtype=np.float32)[:, None] * inv.astype(np.float32)[None], 2, axis=-1).astype(np.float32)
    cos, sin = np.cos(ang), np.sin(ang)
    sign = np.where(np.arange(H) % 2 == 0, -1.0, 1.0).astype(np.float32)
    tm = lambda v: v.reshape(BT, P, H).transpose(1, 0, 2).reshape(P, N)
    rope = np.concatenate([tm(cos), tm(sin * sign), cos.T, sin.T], axis=1).astype(np.float32)
    return table, rope


def kernel(**inputs):
    import concourse.bacc as _bacc
    from concourse.bass_utils import run_bass_kernel_spmd as _run

    nc = _bacc.Bacc("TRN2", target_bir_lowering=False, num_devices=1)
    f = {k.replace("L0_attn_", "").replace("L0_", ""): np.asarray(v) for k, v in inputs.items()}
    table, rope = constants()
    def pairs(v):
        return np.stack([v, v], axis=2).reshape(len(v), P).T

    w1 = f["conv1_w"].reshape(CG, CW, MUL, TAPS)
    w2 = f["conv2_w"].reshape(CG, CW, MUL, TAPS)
    w1_rows = np.zeros((SHIFTS, CW, CG, 2, MUL), np.float32)
    w2_rows = np.zeros((2, CW, MUL, CG, PT, 2), np.float32)
    for out_par in range(2):
        for tap in range(TAPS):
            w1_rows[tap + out_par, :, :, out_par] = w1[..., tap].transpose(1, 0, 2)
            pair, in_par = divmod(out_par + tap, 2)
            w2_rows[in_par, :, :, :, pair, out_par] = w2[..., tap].transpose(1, 2, 0)
    w1_rows = np.concatenate([w1_rows.reshape(K6, -1), np.zeros((P - K6, CG * 2 * MUL), np.float32)])
    arrays = {
        "x": f["x"], "consts": table, "rope": rope, "gate_w": f["ffn_gate_w"].T, "gate_bias": f["ffn_gate_bias"],
        "conv_w": np.concatenate([w1_rows, w2_rows.reshape(P, -1)], axis=1),
        "cols": np.concatenate([f["bq"].T, f["bk"].T, f["lnA_g"].T, f["lnA_b"].T, f["ln0_g"][:, None], f["ln0_b"][:, None],
                                f["b2"][:, None], pairs(f["conv2_b"].reshape(2, CG // 2, CW)),
                                pairs(f["conv1_b"].reshape(CG, 1, CW * MUL)),
                                f["b1"].reshape(MUL, P).T], axis=1),
        "wqkv": np.stack([f["Wq"], f["Wk"], f["Wv"]], axis=1).transpose(2, 0, 1, 3),
        "bv": f["bv"], "ln2_g": f["ln2_g"], "ln2_b": f["ln2_b"], "w1": f["W1"], "w2": f["W2"],
        "wgu": np.concatenate([f["ffn_eg_w"], f["ffn_eu_w"]], axis=1).transpose(2, 0, 1),
        "wed": f["ffn_ed_w"].transpose(2, 0, 1),
        "sg": f["ffn_sg_w"].T, "su": f["ffn_su_w"].T, "sd": f["ffn_sd_w"].T,
    }
    arrays = {f"in_{k}": np.ascontiguousarray(v) for k, v in arrays.items()}
    aps = {k[3:]: nc.dram_tensor(k, v.shape, mybir.dt.from_np(v.dtype), kind="ExternalInput").ap() for k, v in arrays.items()}
    out = nc.dram_tensor("out_0", (B, N, H), F32, kind="ExternalOutput").ap()
    block_kernel(nc, aps, out)
    r = _run(nc, [arrays], core_ids=[0])
    return r.results[0]["out_0"]
```
